# Optimizing a Trainium2 kernel written in Bass

```python
import numpy as np
import jax
import jax.numpy as jnp

def _softmax(x, axis=-1):
    return jax.nn.softmax(x, axis=axis)

def _gelu(x):
    return jax.nn.gelu(x, approximate=True)

def _silu(x):
    return jax.nn.silu(x)

def _sigmoid(x):
    return jax.nn.sigmoid(x)

def _layernorm(x, axis=-1, eps=1e-05):
    m = jnp.mean(x, axis=axis, keepdims=True)
    v = jnp.var(x, axis=axis, keepdims=True)
    return (x - m) / jnp.sqrt(v + eps)

def _scatter_add(tgt, idx, src, axis=0):
    return tgt.at[idx].add(src)

def _segment_sum(src, seg, n):
    return jax.ops.segment_sum(src, seg, n)
kernel_name = 'mk_decoder_preln_d1_seqx_r4_6eade0'

def setup_inputs(seed: int=0):
    np.random.seed(seed)
    _w = jnp.asarray

    def _rec_inputs():
        import jax
        import jax.numpy as jnp
        _rk = jax.random.key(seed)
        x = -0.0003929 + 0.9999 * jax.random.normal(jax.random.fold_in(_rk, 1), (8, 256, 256), jnp.float32)
        _lenS = 256 - jax.random.randint(jax.random.fold_in(_rk, 7), (8,), 0, max(1, 256 // 4) + 1, jnp.int32)
        _lenS2 = 77 - jax.random.randint(jax.random.fold_in(_rk, 8), (8,), 0, max(1, 77 // 4) + 1, jnp.int32)
        _ctx_768P = jax.random.normal(jax.random.fold_in(_rk, 11), (8, 16, 192), jnp.float32)
        _ctx_768c = jax.random.dirichlet(jax.random.fold_in(_rk, 511), 0.3 * jnp.ones((16,), jnp.float32), (8, 77))
        _ctx_768t = jnp.einsum('bsk,bkd->bsd', _ctx_768c, _ctx_768P)
        _ctx_768t = _ctx_768t * jax.lax.rsqrt(jnp.mean(jnp.square(_ctx_768t)) + 1e-12) * 0.953939
        ctx_768 = -0.00055796 + 0.999787 * (_ctx_768t + 0.3 * jax.random.normal(jax.random.fold_in(_rk, 611), (8, 77, 192), jnp.float32))
        return (x, ctx_768)
    x, ctx_768 = _rec_inputs()

    def _L0_attn_setup():
        import jax, jax.numpy as jnp
        import numpy as np
        DIM = 256
        NUM_HEADS = 16
        HEAD_DIM = DIM // NUM_HEADS
        EPS = 1e-06

        def layer_norm(x, gamma, beta):
            mu = jnp.mean(x, axis=-1, keepdims=True)
            var = jnp.mean(jnp.square(x - mu), axis=-1, keepdims=True)
            return (x - mu) / jnp.sqrt(var + EPS) * gamma + beta

        def apply_rope(q, k):
            seq_len, head_dim = (q.shape[1], q.shape[3])
            half = head_dim // 2
            freq_range = jnp.arange(half, dtype=jnp.float32) / half
            inv_freq = 1.0 / 10000.0 ** freq_range
            t = jnp.arange(seq_len, dtype=jnp.float32)
            freqs = jnp.outer(t, inv_freq)
            emb = jnp.concatenate([freqs, freqs], axis=-1)
            cos = jnp.cos(emb)[None, :, None, :]
            sin = jnp.sin(emb)[None, :, None, :]

            def rotate_half(x):
                x1, x2 = (x[..., :half], x[..., half:])
                return jnp.concatenate([-x2, x1], axis=-1)
            return (q * cos + rotate_half(q) * sin, k * cos + rotate_half(k) * sin)
        key = jax.random.key(seed)
        ks = jax.random.split(key, 4)
        B, S = (2, 512)
        x = jax.random.normal(ks[0], (B, S, DIM), dtype=jnp.float32)
        lim_qkv = float(np.sqrt(6.0 / (DIM + 3 * DIM)))
        w_qkv = jax.random.uniform(ks[1], (3 * DIM, DIM), dtype=jnp.float32, minval=-lim_qkv, maxval=lim_qkv)
        lim_p = float(np.sqrt(6.0 / (DIM + DIM)))
        w_proj = jax.random.uniform(ks[2], (DIM, DIM), dtype=jnp.float32, minval=-lim_p, maxval=lim_p)
        b_proj = jnp.zeros((DIM,), dtype=jnp.float32)
        q_gamma = jnp.ones((HEAD_DIM,), dtype=jnp.float32)
        q_beta = jnp.zeros((HEAD_DIM,), dtype=jnp.float32)
        k_gamma = jnp.ones((HEAD_DIM,), dtype=jnp.float32)
        k_beta = jnp.zeros((HEAD_DIM,), dtype=jnp.float32)
        return {'x': x, 'w_qkv': w_qkv, 'w_proj': w_proj, 'b_proj': b_proj, 'q_gamma': q_gamma, 'q_beta': q_beta, 'k_gamma': k_gamma, 'k_beta': k_beta}
    _L0_attn_all = _L0_attn_setup()
    _L0_attn_in = {k: v for k, v in _L0_attn_all.items() if k in ('w_qkv', 'w_proj', 'b_proj', 'q_gamma', 'q_beta', 'k_gamma', 'k_beta')}
    del _L0_attn_all

    def _L0_xattn_setup():
        import jax, jax.numpy as jnp
        import numpy as np
        IMAGE_DIM = 256
        TEXT_DIM = 192
        NUM_HEADS = 16
        HEAD_DIM = IMAGE_DIM // NUM_HEADS
        key = jax.random.key(seed)
        ks = jax.random.split(key, 14)
        B, N, M = (4, 1024, 128)
        s_img = 1.0 / np.sqrt(IMAGE_DIM)
        s_txt = 1.0 / np.sqrt(TEXT_DIM)
        s_ff = 1.0 / np.sqrt(2 * IMAGE_DIM)
        return {'x': jax.random.normal(ks[0], (B, N, IMAGE_DIM), jnp.float32), 'y': jax.random.normal(ks[1], (B, M, TEXT_DIM), jnp.float32), 'Wq': jax.random.normal(ks[2], (IMAGE_DIM, IMAGE_DIM), jnp.float32) * s_img, 'bq': jax.random.normal(ks[3], (IMAGE_DIM,), jnp.float32) * s_img, 'Wk': jax.random.normal(ks[4], (TEXT_DIM, IMAGE_DIM), jnp.float32) * s_txt, 'bk': jax.random.normal(ks[5], (IMAGE_DIM,), jnp.float32) * s_txt, 'Wv': jax.random.normal(ks[6], (TEXT_DIM, IMAGE_DIM), jnp.float32) * s_txt, 'bv': jax.random.normal(ks[7], (IMAGE_DIM,), jnp.float32) * s_txt, 'W1': jax.random.normal(ks[8], (IMAGE_DIM, 2 * IMAGE_DIM), jnp.float32) * s_img, 'b1': jax.random.normal(ks[9], (2 * IMAGE_DIM,), jnp.float32) * s_img, 'W2': jax.random.normal(ks[10], (2 * IMAGE_DIM, IMAGE_DIM), jnp.float32) * s_ff, 'b2': jax.random.normal(ks[11], (IMAGE_DIM,), jnp.float32) * s_ff}
    _L0_xattn_all = _L0_xattn_setup()
    _L0_xattn_in = {k: v for k, v in _L0_xattn_all.items() if k in ('Wq', 'bq', 'Wk', 'bk', 'Wv', 'bv', 'W1', 'b1', 'W2', 'b2')}
    del _L0_xattn_all

    def _L0_ffn_setup():
        import jax, jax.numpy as jnp
        import numpy as np
        TOP_K = 2
        key = jax.random.key(seed)
        k0, k1, k2, k3, k4 = jax.random.split(key, 5)
        B, S, H, I, E = (1, 1024, 256, 512, 8)
        hidden_states = jax.random.normal(k0, (B, S, H), dtype=jnp.float32)
        wg = jax.random.normal(k1, (E, H), dtype=jnp.float32) * 0.02
        w1 = jax.random.normal(k2, (E, I, H), dtype=jnp.float32) * 0.02
        w3 = jax.random.normal(k3, (E, I, H), dtype=jnp.float32) * 0.02
        w2 = jax.random.normal(k4, (E, H, I), dtype=jnp.float32) * 0.02
        return {'hidden_states': hidden_states, 'wg': wg, 'w1': w1, 'w3': w3, 'w2': w2}
    _L0_ffn_all = _L0_ffn_setup()
    _L0_ffn_in = {k: v for k, v in _L0_ffn_all.items() if k in ('wg', 'w1', 'w3', 'w2')}
    del _L0_ffn_all
    return {'x': x, 'ctx_768': ctx_768, 'L0_attn_w_qkv': _L0_attn_in['w_qkv'], 'L0_attn_w_proj': _L0_attn_in['w_proj'], 'L0_attn_b_proj': _L0_attn_in['b_proj'], 'L0_attn_q_gamma': _L0_attn_in['q_gamma'], 'L0_attn_q_beta': _L0_attn_in['q_beta'], 'L0_attn_k_gamma': _L0_attn_in['k_gamma'], 'L0_attn_k_beta': _L0_attn_in['k_beta'], 'L0_xattn_Wq': _L0_xattn_in['Wq'], 'L0_xattn_bq': _L0_xattn_in['bq'], 'L0_xattn_Wk': _L0_xattn_in['Wk'], 'L0_xattn_bk': _L0_xattn_in['bk'], 'L0_xattn_Wv': _L0_xattn_in['Wv'], 'L0_xattn_bv': _L0_xattn_in['bv'], 'L0_xattn_W1': _L0_xattn_in['W1'], 'L0_xattn_b1': _L0_xattn_in['b1'], 'L0_xattn_W2': _L0_xattn_in['W2'], 'L0_xattn_b2': _L0_xattn_in['b2'], 'L0_ffn_wg': _L0_ffn_in['wg'], 'L0_ffn_w1': _L0_ffn_in['w1'], 'L0_ffn_w3': _L0_ffn_in['w3'], 'L0_ffn_w2': _L0_ffn_in['w2']}

def reference(x, ctx_768, L0_attn_w_qkv, L0_attn_w_proj, L0_attn_b_proj, L0_attn_q_gamma, L0_attn_q_beta, L0_attn_k_gamma, L0_attn_k_beta, L0_xattn_Wq, L0_xattn_bq, L0_xattn_Wk, L0_xattn_bk, L0_xattn_Wv, L0_xattn_bv, L0_xattn_W1, L0_xattn_b1, L0_xattn_W2, L0_xattn_b2, L0_ffn_wg, L0_ffn_w1, L0_ffn_w3, L0_ffn_w2):
    import jax
    import jax.numpy as jnp

    def _L0_attn_ref(x, w_qkv, w_proj, b_proj, q_gamma, q_beta, k_gamma, k_beta):
        import jax, jax.numpy as jnp
        import numpy as np
        DIM = 256
        NUM_HEADS = 16
        HEAD_DIM = DIM // NUM_HEADS
        EPS = 1e-06

        def layer_norm(x, gamma, beta):
            mu = jnp.mean(x, axis=-1, keepdims=True)
            var = jnp.mean(jnp.square(x - mu), axis=-1, keepdims=True)
            return (x - mu) / jnp.sqrt(var + EPS) * gamma + beta

        def apply_rope(q, k):
            seq_len, head_dim = (q.shape[1], q.shape[3])
            half = head_dim // 2
            freq_range = jnp.arange(half, dtype=jnp.float32) / half
            inv_freq = 1.0 / 10000.0 ** freq_range
            t = jnp.arange(seq_len, dtype=jnp.float32)
            freqs = jnp.outer(t, inv_freq)
            emb = jnp.concatenate([freqs, freqs], axis=-1)
            cos = jnp.cos(emb)[None, :, None, :]
            sin = jnp.sin(emb)[None, :, None, :]

            def rotate_half(x):
                x1, x2 = (x[..., :half], x[..., half:])
                return jnp.concatenate([-x2, x1], axis=-1)
            return (q * cos + rotate_half(q) * sin, k * cos + rotate_half(k) * sin)
        B, S, C = x.shape
        H, D = (NUM_HEADS, HEAD_DIM)
        qkv = jnp.einsum('bsc,oc->bso', x, w_qkv).reshape(B, S, 3, H, D)
        q = layer_norm(qkv[:, :, 0], q_gamma, q_beta)
        k = layer_norm(qkv[:, :, 1], k_gamma, k_beta)
        v = qkv[:, :, 2]
        q, k = apply_rope(q, k)
        scale = D ** (-0.5)
        q = q.astype(jnp.float32) * scale
        k = k.astype(jnp.float32)
        v = v.astype(jnp.float32)
        attn = jnp.einsum('bqhd,bkhd->bhqk', q, k)
        attn = jax.nn.softmax(attn, axis=-1)
        out = jnp.einsum('bhqk,bkhd->bqhd', attn, v).reshape(B, S, C)
        out = jnp.einsum('bsc,oc->bso', out, w_proj) + b_proj
        return out

    def _L0_xattn_ref(x, y, Wq, bq, Wk, bk, Wv, bv, W1, b1, W2, b2):
        import jax, jax.numpy as jnp
        import numpy as np
        IMAGE_DIM = 256
        TEXT_DIM = 192
        NUM_HEADS = 16
        HEAD_DIM = IMAGE_DIM // NUM_HEADS
        B, N, _ = x.shape
        M = y.shape[1]
        q = (x @ Wq + bq).reshape(B, N, NUM_HEADS, HEAD_DIM)
        k = (y @ Wk + bk).reshape(B, M, NUM_HEADS, HEAD_DIM)
        v = (y @ Wv + bv).reshape(B, M, NUM_HEADS, HEAD_DIM)
        scale = 1.0 / np.sqrt(HEAD_DIM)
        scores = jnp.einsum('bnhd,bmhd->bhnm', q, k) * scale
        attn = jax.nn.softmax(scores, axis=-1)
        out = jnp.einsum('bhnm,bmhd->bnhd', attn, v).reshape(B, N, IMAGE_DIM)
        h = jax.nn.relu(out @ W1 + b1)
        return h @ W2 + b2

    def _L0_ffn_ref(hidden_states, wg, w1, w3, w2):
        import jax, jax.numpy as jnp
        import numpy as np
        TOP_K = 2
        orig_shape = hidden_states.shape
        H = orig_shape[-1]
        E = wg.shape[0]
        x = hidden_states.reshape(-1, H)
        router_logits = x @ wg.T
        probs = jax.nn.softmax(router_logits, axis=-1)
        topk_w, topk_idx = jax.lax.top_k(probs, TOP_K)
        topk_w = topk_w / jnp.sum(topk_w, axis=-1, keepdims=True)
        expert_w = jnp.sum(jax.nn.one_hot(topk_idx, E, dtype=x.dtype) * topk_w[..., None], axis=1)
        h1 = jnp.einsum('th,eih->tei', x, w1)
        h3 = jnp.einsum('th,eih->tei', x, w3)
        y = jnp.einsum('tei,ehi->teh', jax.nn.silu(h1) * h3, w2)
        out = jnp.einsum('te,teh->th', expert_w, y)
        return out.reshape(orig_shape)
    x = x + _L0_attn_ref(_layernorm(x, axis=-1), L0_attn_w_qkv, L0_attn_w_proj, L0_attn_b_proj, L0_attn_q_gamma, L0_attn_q_beta, L0_attn_k_gamma, L0_attn_k_beta)
    x = x + _L0_xattn_ref(_layernorm(x, axis=-1), ctx_768, L0_xattn_Wq, L0_xattn_bq, L0_xattn_Wk, L0_xattn_bk, L0_xattn_Wv, L0_xattn_bv, L0_xattn_W1, L0_xattn_b1, L0_xattn_W2, L0_xattn_b2)
    x = x + _L0_ffn_ref(_layernorm(x, axis=-1), L0_ffn_wg, L0_ffn_w1, L0_ffn_w3, L0_ffn_w2)
    return x

_drawn_inputs = setup_inputs


def setup_inputs(seed=0):
    import zlib

    import numpy as np

    out = dict(_drawn_inputs(seed))
    spreads = {'L0_attn_b_proj': (0.0, 0.1),
     'L0_attn_q_gamma': (1.0, 0.6),
     'L0_attn_q_beta': (0.0, 0.8),
     'L0_attn_k_gamma': (1.0, 0.6),
     'L0_attn_k_beta': (0.0, 0.8)}
    factors = {'L0_xattn_bq': 6.462,
     'L0_xattn_bk': 8.0,
     'L0_ffn_wg': 4.084,
     'L0_ffn_w1': 3.638,
     'L0_ffn_w3': 3.597,
     'L0_ffn_w2': 3.594}
    for name, (base, spread) in spreads.items():
        noise = np.random.default_rng([zlib.crc32(name.encode()), seed]).standard_normal(out[name].shape)
        drawn = base * np.exp(spread * noise) if base else spread * noise
        out[name] = jnp.asarray(drawn.astype(out[name].dtype))
    for name, factor in factors.items():
        out[name] = (out[name] * factor).astype(out[name].dtype)
    return out
```

```python
from contextlib import ExitStack

import numpy as np

import concourse.bass as bass
from concourse import mybir
from concourse.alu_op_type import AluOpType as ALU

F32, BF16, I32 = mybir.dt.float32, mybir.dt.bfloat16, mybir.dt.int32
ACT = mybir.ActivationFunctionType
X = mybir.AxisListType.X

P = 128
NB, S, D = 8, 256, 256
H, HD = 16, 16
M = 77
TEXT = 192
TT = S // P
KC = D // P
HID = 512
E = 8
TOKENS = NB * S
TERMS = 3
Q_TERM = (0, 0, 0, 1, 1, 2)
K_TERM = (0, 1, 2, 0, 1, 0)
ROWS = HD * len(Q_TERM)
AUG = ROWS + TERMS
GROUP = 4
GROUPS = H // GROUP
LOADS = 16 * 2 * len(Q_TERM)
HEADS = [8 * c + 2 * j + half for c in range(2) for half in range(2) for j in range(4)]
ROW = D + 1 + E
REGION = TOKENS + P
BLOCKS = 2 * TOKENS // P + E - 1
SPARE = E * REGION
LOW = -3.0e38
MAGIC = float(0x5F3759DF)
NEWTON = 3


class Round:

    def __init__(self, own, pair=None):
        self.own, self.pair, self.side = own, pair, own % 2

    def count(self, per, more=0):
        known = per * self.own + more
        return known if self.pair is None else self.pair * (2 * per) + known

    def turns(self, per, more=0):
        known = per * (self.own // 2) + more
        return known if self.pair is None else self.pair * per + known

    def next(self):
        return Round(self.own + 1, self.pair)

    def previous(self):
        return Round(self.own - 1, self.pair)

    @property
    def first(self):
        return self.pair is None and self.own == 0

    @property
    def final(self):
        return self.pair is None and self.own == BLOCKS - 1

    @property
    def last_two(self):
        return self.pair is None and self.own >= BLOCKS - 2

    @property
    def last(self):
        return self.pair is None and self.own == NB - 1


def rounds(eng, body):
    for own in range(2):
        body(Round(own))
    with eng.Fori(0, (NB - 4) // 2) as pair:
        body(Round(2, pair))
        body(Round(3, pair))
    for own in range(NB - 2, NB):
        body(Round(own))


def blocks(eng, body, last=False):
    for own in range(3):
        body(Round(own))
    with eng.Fori(0, (BLOCKS - 3) // 2 - last) as pair:
        body(Round(3, pair))
        body(Round(4, pair))
    if last:
        body(Round(BLOCKS - 2))
        body(Round(BLOCKS - 1))


def wait(eng, sem, value):
    if not isinstance(value, int) or value > 0:
        eng.wait_ge(sem, value)


def decoder_layer(nc, t, out):
    ctx = ExitStack()
    with ctx:
        def sb(name, shape, dt=F32):
            return ctx.enter_context(nc.sbuf_tensor(name, shape, dt))

        def sem(name):
            return ctx.enter_context(nc.semaphore(name))

        qk_terms = nc.dram_tensor("qk_terms", [NB, 2 * TERMS * KC, P, S], BF16, kind="Internal").ap()
        x1_dram = nc.dram_tensor("x1_dram", [NB, P, TT, D], F32, kind="Internal").ap()
        q2_terms = nc.dram_tensor("q2_terms", [NB, TERMS * KC, P, S], BF16, kind="Internal").ap()
        k2_terms = nc.dram_tensor("k2_terms", [NB, TERMS * KC, P, M], BF16, kind="Internal").ap()
        v2_dram = nc.dram_tensor("v2_dram", [NB, M, H * 2 * HD], F32, kind="Internal").ap()
        routed = nc.dram_tensor("routed", [SPARE + P, ROW], F32, kind="Internal").ap()

        early = sb("early", [P, E * 3 * 2 * HID])
        moe = early[:, :].rearrange("p (e n) -> p e n", e=E)
        used = [0]

        def carve(words):
            at = used[0]
            used[0] += words
            assert used[0] <= E * 3 * 2 * HID
            return early[:, at:at + words]

        wqkv = carve(KC * 3 * D).rearrange("p (k n) -> p k n", k=KC)
        xn = [carve(TT * D).rearrange("p (t c) -> p t c", t=TT) for _ in range(2)]
        xnT = [carve(KC * S).rearrange("p (k s) -> p k s", k=KC) for _ in range(2)]
        square = carve(TT * 2 * D).rearrange("p (t c) -> p t c", t=TT)
        normed = carve(TT * 2 * D).rearrange("p (t c) -> p t c", t=TT)
        direct = carve(TT * 2 * D).rearrange("p (t c) -> p t c", t=TT)
        rotated = carve(TT * 2 * D).rearrange("p (t c) -> p t c", t=TT)
        terms = [carve(TT * TERMS * D).bitcast(BF16).rearrange("p (t a c) -> p t a c", t=TT, a=TERMS)
                 for _ in range(2)]
        qkT = [carve(2 * TERMS * KC * S // 2).bitcast(BF16).rearrange("p (n s) -> p n s", s=S)
               for _ in range(2)]
        values = carve(NB * TT * D).rearrange("p (t c) -> p t c", t=NB * TT)
        vpad = [carve(TT * H * 2 * HD).rearrange("p (t h d) -> p t h d", t=TT, h=H) for _ in range(2)]
        ctxT = carve(KC * NB * M).rearrange("p (k m) -> p k m", k=KC)
        wk = carve(KC * D).rearrange("p (k n) -> p k n", k=KC)
        wv = carve(KC * D).rearrange("p (k n) -> p k n", k=KC)
        tables = carve(3 * TT * 2 * HD).rearrange("p (a t q d) -> p a t q d", a=3, t=TT, q=2)
        affine = carve(4 * 2 * HD).rearrange("p (a q d) -> p a q d", a=4, q=2)
        angles = carve(2 * TT * HD).rearrange("p (a t d) -> p a t d", a=2, t=TT)
        wmean = carve(KC * 2 * H).rearrange("p (k g) -> p k g", k=KC)
        spread = carve(TT * 2 * H + TT)

        qst = [sb(f"qst{i}", [P, H, S], BF16) for i in range(2)]
        kst = [sb(f"kst{i}", [P, H, S], BF16) for i in range(2)]
        k2st = [sb(f"k2st{i}", [P, H, M], BF16) for i in range(2)]
        v2pad = [sb(f"v2pad{i}", [P, 1, H, 2 * HD]) for i in range(2)]
        probs = sb("probs", [P, 2, GROUP, 2 * S])
        x_all = probs[:, :, :, :].rearrange("p a b c -> p (a b c)").rearrange("p (t c) -> p t c", c=D)
        k2f = qst[0][:, :, :].rearrange("p h s -> p (h s)").bitcast(F32)[:, 0:KC * NB * M]
        k2parts = qst[1][:, :, :].rearrange("p h s -> p (h s)")[:, 0:TERMS * KC * NB * M].rearrange(
            "p (a c b m) -> p a c b m", a=TERMS, c=KC, b=NB)
        wp = sb("wp", [P, KC, D])
        wq = sb("wq", [P, KC, D])
        w1 = sb("w1", [P, KC, HID])
        w2 = sb("w2", [P, HID // P, D])
        wg = sb("wg", [P, KC, E])
        identf = sb("identf", [P, P])
        ident = sb("ident", [P, P], BF16)
        below = sb("below", [P, P], BF16)
        ones = sb("ones", [P, P], BF16)
        onesrow = sb("onesrow", [P, 2, 2 * HD])
        bias_p = sb("bias_p", [P, D])
        bias_2 = sb("bias_2", [P, D])
        bias_q = sb("bias_q", [P, KC])
        bias_1 = sb("bias_1", [P, HID // P])
        resid = [sb(f"resid{i}", [P, TT, D]) for i in range(2)]
        x_new = [sb(f"x_new{i}", [P, TT, D]) for i in range(2)]
        xn2 = sb("xn2", [P, TT, D])
        xn2T = sb("xn2T", [P, KC, S])
        q2both = sb("q2both", [P, 2 * KC, S])
        q2f, q2rest = q2both[:, 0:KC, :], q2both[:, KC:, :]
        hidT = q2both[:, :, :]
        q2T = [sb(f"q2T{i}", [P, TERMS, KC, S], BF16) for i in range(2)]
        attnT = sb("attnT", [P, 2, S])
        recip = sb("recip", [P, 2, S])
        maxes = sb("maxes", [P, H, TT])
        mrest = sb("mrest", [P, TT, H])
        mterms = sb("mterms", [P, TT, P // H, H], BF16)
        mT = sb("mT", [TERMS * H, S], BF16)
        rows3 = [sb(f"rows3_{i}", [P, TT, ROW]) for i in range(2)]
        token_ids = sb("token_ids", [P, NB * TT], I32)
        logits = sb("logits", [P, TT, E])
        first_of = sb("first_of", [P, E])
        pick = [sb(f"pick{i}", [P, TT, E]) for i in range(2)]
        key = sb("key", [P, TT, E])
        best = [sb(f"best{i}", [P, TT]) for i in range(2)]
        chosen = sb("chosen", [P, TT, E], BF16)
        gap = sb("gap", [P, TT])
        share = [sb(f"share{i}", [P, TT]) for i in range(2)]
        top = sb("top", [P, TT])
        ranks = sb("ranks", [P, TT, E])
        taken = [sb(f"taken{i}", [P, TT, E]) for i in range(2)]
        filled = sb("filled", [P, E])
        posf = sb("posf", [P, TT, 2])
        pos = [sb(f"pos{i}", [P, TT * 2], I32) for i in range(2)]
        tokens = sb("tokens", [P, 1], I32)
        padding = sb("padding", [P, ROW])
        region_at = sb("region_at", [P, E])
        block_at = sb("block_at", [P, BLOCKS])
        filled_i = sb("filled_i", [P, E], I32)
        count_i = sb("count_i", [P, E], I32)
        ends_f = sb("ends_f", [P, E])
        step_f = sb("step_f", [P, E])
        flat_p = probs[:, :, :, :].rearrange("p a b c -> p (a b c)")
        past = flat_p[:, 0:BLOCKS * (E + 1)].rearrange("p (b e) -> p b e", e=E + 1)
        of_block = flat_p[:, 512:512 + BLOCKS * E].rearrange("p (b e) -> p b e", e=E)
        scaled = flat_p[:, 1024:1024 + BLOCKS * E].rearrange("p (b e) -> p b e", e=E)
        block_f = flat_p[:, 1536:1536 + 2 * BLOCKS].rearrange("p (a b) -> p a b", a=2)
        tokens_of = flat_p[:, 2560:2560 + BLOCKS].bitcast(I32)
        block_i = flat_p[:, 2048:2048 + 2 * BLOCKS].rearrange("p (a b) -> p a b", a=2).bitcast(I32)
        flat_q = [q[:, :, :].rearrange("p h s -> p (h s)").bitcast(F32) for q in qst]
        xs = [f[:, 0:ROW] for f in flat_q]
        xsT = [f[:, 288:288 + D].rearrange("p (k c) -> p k c", k=KC) for f in flat_q]
        act1 = [f[:, 544:544 + HID] for f in flat_q]
        hid = [f[:, 1056:1056 + HID] for f in flat_q]
        flat_k = [q[:, :, :].rearrange("p h s -> p (h s)").bitcast(F32) for q in kst]
        hidT2 = [f[:, 0:HID].rearrange("p (k c) -> p k c", k=HID // P) for f in flat_k]
        result = [f[:, 512:512 + D] for f in flat_k]
        gates = [f[:, 768:768 + E] for f in flat_k]
        gate = [f[:, 776:777] for f in flat_k]
        moments = sb("moments", [P, TT, 6])
        stats = sb("stats", [P, TT, 2])
        rstd = sb("rstd", [P, TT])
        newton = sb("newton", [P, TT])
        vareps = sb("vareps", [P, TT])

        bank = [ctx.enter_context(nc.psum_tensor(f"bank{i}", [P, 512], F32)) for i in range(8)]
        bank16 = [b[:, :].bitcast(BF16) for b in bank]

        loaded = sem("loaded")
        x_first, x_rest = sem("x_first"), sem("x_rest")
        s_ones = sem("s_ones")
        s_tab = sem("s_tab")
        s_k2ps, s_k2f, s_k2t, s_k2st = sem("s_k2ps"), sem("s_k2f"), sem("s_k2t"), sem("s_k2st")
        s_zero, s_v2ps, s_v2 = sem("s_zero"), sem("s_v2ps"), sem("s_v2")
        s_v2st = [sem("s_v2st0"), sem("s_v2st1")]
        p_xn = sem("p_xn")
        p_xTps, p_xT = sem("p_xTps"), sem("p_xT")
        p_qk, p_v, p_sq = sem("p_qk"), sem("p_v"), sem("p_sq")
        p_sum, p_root = sem("p_sum"), sem("p_root")
        p_n, p_rot, p_terms = sem("p_n"), sem("p_rot"), sem("p_terms")
        p_vsb = sem("p_vsb")
        p_qTps, p_qT = sem("p_qTps"), sem("p_qT")
        p_store = [sem("p_store0"), sem("p_store1")]

        def attention_sems(tag):
            return {n: sem(f"{tag}_{n}") for n in (
                "sq", "max", "mterms", "mTps", "mT", "st", "exp", "av", "attn", "vpad")} | {
                n: [sem(f"{tag}_{n}{i}") for i in range(2)] for n in ("stack", "aug")}

        A = attention_sems("a")
        a_res = [sem("a_res0"), sem("a_res1")]
        a_resb, a_proj, a_x1, a_var, a_rstd, a_xn = (sem(n) for n in (
            "a_resb", "a_proj", "a_x1", "a_var", "a_rstd", "a_xn"))
        a_x1st = [sem("a_x1st0"), sem("a_x1st1")]
        a_xTps, a_xT, a_q2ps, a_q2f, a_q2t = (sem(n) for n in (
            "a_xTps", "a_xT", "a_q2ps", "a_q2f", "a_q2t"))
        a_q2st = [sem("a_q2st0"), sem("a_q2st1")]

        C = attention_sems("c")
        loaded2 = sem("loaded2")
        c_res = [sem("c_res0"), sem("c_res1")]
        c_v2 = [sem("c_v20"), sem("c_v21")]
        c_out = [sem("c_out0"), sem("c_out1")]
        c_moe = sem("c_moe")
        (c_resb, c_h, c_hT, c_y, c_x2, c_var, c_rstd, c_xn, c_xTps, c_xT, c_logit, c_lg, c_mask, c_gap, c_ed,
         c_rank, c_rk, c_pos, c_gates) = (sem("c_" + n) for n in (
             "resb", "h", "hT", "y", "x2", "var", "rstd", "xn", "xTps", "xT", "logit", "lg", "mask", "gap", "ed",
             "rank", "rk", "pos", "gates"))
        c_scatter = [sem("c_scatter0"), sem("c_scatter1")]
        m_filled, m_table, m_pad = sem("m_filled"), sem("m_table"), sem("m_pad")
        m_xs = [sem("m_xs0"), sem("m_xs1")]
        m_xTps, m_xT, m_h, m_silu, m_hid, m_hTps, m_hT, m_y, m_res, m_gate = (sem("m_" + n) for n in (
            "xTps", "xT", "h", "silu", "hid", "hTps", "hT", "y", "res", "gate"))
        m_added = sem("m_added")

        block = ctx.enter_context(nc.Block())

        weights = [("wqkv", wqkv), ("angles", angles), ("affine", affine), ("identf", identf[:]),
                   ("ident", ident[:]), ("ctxT", ctxT), ("wk", wk), ("wv", wv), ("wp", wp[:]), ("wq", wq[:]), ("bias_q", bias_q[:]),
                   ("bias_p", bias_p[:])]
        later = [("w1", w1[:]), ("w2", w2[:]), ("wg", wg[:]), ("below", below[:]), ("bias_2", bias_2[:]),
                 ("bias_1", bias_1[:]), ("ones", ones[:]), ("token_ids", token_ids[:]),
                 ("first_of", first_of[:]), ("region_at", region_at[:]), ("block_at", block_at[:]),
                 ("padding", padding[:])]

        def rsqrt_on_pool(pool, n=TT):
            for step in range(NEWTON):
                if step:
                    pool.drain()
                nc.gpsimd.tensor_tensor(newton[:], rstd[:], rstd[:], ALU.mult)
                pool.drain()
                nc.gpsimd.tensor_tensor(newton[:], newton[:], vareps[:], ALU.mult)
                pool.drain()
                nc.gpsimd.tensor_scalar(newton[:], newton[:], -0.5, 1.5, ALU.mult, ALU.add)
                pool.drain()
                last = nc.gpsimd.tensor_tensor(rstd[:], rstd[:], newton[:], ALU.mult)
            return last

        def moments_of(dve, src, eps):
            for tt in range(TT):
                nc.vector.bn_stats(moments[:, tt, :], src[:, tt, :])
            dve.drain()
            for tt in range(TT):
                nc.vector.bn_aggr(stats[:, tt, :], moments[:, tt, :])
            dve.drain()
            nc.vector.tensor_scalar(vareps[:], stats[:, :, 1], eps, None, ALU.add)
            dve.drain()
            return nc.vector.tensor_scalar(rstd[:].bitcast(I32), vareps[:].bitcast(I32), -0.5, MAGIC,
                                           ALU.mult, ALU.add)

        def norm_into(dst, src):
            for tt in range(TT):
                last = nc.vector.tensor_scalar(dst[:, tt, 0:D], src[:, tt, :], stats[:, tt, 0:1],
                                               rstd[:, tt:tt + 1], ALU.subtract, ALU.mult)
            return last


        def pe_score(pe, A, r, slot, keys, kstk):
            h = HEADS[slot]
            if slot == 0:
                pe.wait_ge(A["stack"][r.side], r.turns(LOADS, LOADS))
            wait(pe, A["max"], r.count(H, slot - 1))
            for qt in range(TT):
                last = nc.tensor.matmul(bank[slot % 2][:, qt * keys:(qt + 1) * keys],
                                        qst[r.side][0:ROWS, h, qt * P:(qt + 1) * P],
                                        kstk[r.side][0:ROWS, h, :], start=True, stop=True)
            last.then_inc(A["sq"], 1)

        def dve_max(dve, A, r, slot, keys):
            dve.wait_ge(A["sq"], r.count(H, slot + 1))
            if slot == 0:
                wait(dve, A["mterms"], r.count(1))
            nc.vector.tensor_reduce(maxes[:, HEADS[slot], :],
                                    bank[slot % 2][:, 0:TT * keys].rearrange("p (t k) -> p t k", t=TT),
                                    axis=X, op=ALU.max).then_inc(A["max"], 1)

        def dve_split_max(dve, A, r):
            dve.drain()
            wait(dve, A["mTps"], r.count(1))
            nc.vector.tensor_scalar(mrest[:], maxes[:, :, :].rearrange("p h t -> p t h"), -1.0, None, ALU.mult)
            for a in range(TERMS):
                dve.drain()
                last = nc.vector.tensor_copy(mterms[:, :, a, :], mrest[:])
                if a < TERMS - 1:
                    dve.drain()
                    nc.vector.tensor_tensor(mrest[:], mrest[:], mterms[:, :, a, :], ALU.subtract)
            last.then_inc(A["mterms"], 1)

        def pe_max_rows(pe, A, r):
            pe.wait_ge(A["mterms"], r.count(1, 1))
            wait(pe, A["mT"], r.count(1))
            for qt in range(TT):
                last = nc.tensor.transpose(bank16[7][:, qt * P:(qt + 1) * P],
                                           mterms[:, qt, :, :].rearrange("p a h -> p (a h)"), ident[:])
            last.then_inc(A["mTps"], 1)

        def act_max_rows(act, A, r):
            act.wait_ge(A["mTps"], r.count(1, 1))
            if not (r.pair is None and r.own == 0):
                act.wait_ge(A["aug"][1 - r.side], r.previous().turns(16 * TERMS, 16 * TERMS))
            nc.scalar.copy(mT[:], bank16[7][0:TERMS * H, 0:S]).then_inc(A["mT"], 1)

        def sp_max_rows(sp, A, r):
            sp.wait_ge(A["mT"], r.count(1, 1))
            for a in range(TERMS):
                sp.dma_start(qst[r.side][ROWS + a:ROWS + a + 1, :, :], mT[a * H:(a + 1) * H, :]
                             ).then_inc(A["aug"][r.side], 16)

        def pe_exponents(pe, A, r, g, keys, kstk):
            tiles, size = (keys + P - 1) // P, min(P, keys)
            for slot in range(g * GROUP, (g + 1) * GROUP):
                if slot == 0:
                    pe.wait_ge(A["aug"][r.side], r.turns(16 * TERMS, 16 * TERMS))
                wait(pe, A["exp"], r.count(H, slot - 1))
                for kt in range(tiles):
                    last = nc.tensor.matmul(bank[2 + slot % 2][0:size, kt * S:(kt + 1) * S],
                                            kstk[r.side][0:AUG, HEADS[slot], kt * P:kt * P + size],
                                            qst[r.side][0:AUG, HEADS[slot], :], start=True, stop=True)
                last.then_inc(A["st"], 1)

        def act_exp(act, A, r, g, keys):
            tiles, size = (keys + P - 1) // P, min(P, keys)
            wait(act, A["av"], r.count(GROUPS, g - 1))
            for slot in range(g * GROUP, (g + 1) * GROUP):
                act.wait_ge(A["st"], r.count(H, slot + 1))
                nc.scalar.activation(probs[0:size, g % 2, slot % GROUP, 0:tiles * S],
                                     bank[2 + slot % 2][0:size, 0:tiles * S], ACT.Exp).then_inc(A["exp"], 1)

        def pe_values(pe, A, r, g, keys, vp):
            tiles, size = (keys + P - 1) // P, min(P, keys)
            chunk, half = g // 2, g % 2
            pe.wait_ge(A["exp"], r.count(H, (g + 1) * GROUP))
            if g == 0:
                wait(pe, A["attn"], r.count(1))
            for kt in range(tiles):
                for kind in range(2):
                    for j in range(GROUP):
                        lhs = (vp[r.side][0:size, kt, HEADS[g * GROUP + j], :] if kind == 0
                               else onesrow[0:size, half, :])
                        last = nc.tensor.matmul(
                            bank[4 + kind][32 * j:32 * j + 32, chunk * S:(chunk + 1) * S], lhs,
                            probs[0:size, g % 2, j, kt * S:(kt + 1) * S],
                            start=(half == 0 and kt == 0), stop=(half == 1 and kt == tiles - 1),
                            skip_group_check=True)
            last.then_inc(A["av"], 1)

        def dve_attn(dve, A, r, next_done):
            dve.wait_ge(A["av"], r.count(GROUPS, GROUPS))
            wait(dve, next_done, r.count(1))
            nc.vector.reciprocal(recip[:], bank[5][:, :].rearrange("p (c s) -> p c s", c=2))
            dve.drain()
            nc.vector.tensor_tensor(attnT[:], bank[4][:, :].rearrange("p (c s) -> p c s", c=2),
                                    recip[:], ALU.mult).then_inc(A["attn"], 1)

        @block.sync
        def _(sp):
            for name, tile in weights[:6]:
                sp.dma_start(tile, t[name]).then_inc(loaded, 16)
            sp.dma_start(x_all[:, 0:2 * TT, :], t["x"][:, 0:2 * TT, :]).then_inc(x_first, 16)
            for name, tile in weights[6:]:
                sp.dma_start(tile, t[name]).then_inc(loaded, 16)
            sp.dma_start(x_all[:, 2 * TT:, :], t["x"][:, 2 * TT:, :]).then_inc(x_rest, 16)
            for name, tile in later:
                sp.dma_start(tile, t[name]).then_inc(loaded2, 16)

            for b in range(NB):
                sp.wait_ge(s_v2, b + 1)
                sp.dma_start(v2_dram[b], v2pad[b % 2][0:M, 0, :, :].rearrange("p h d -> p (h d)")
                             ).then_inc(s_v2st[b % 2], 16)
            sp.wait_ge(s_k2t, 1)
            for a in range(TERMS):
                for c in range(KC):
                    sp.dma_start(k2_terms[:, a * KC + c, :, :].rearrange("b p m -> p b m"),
                                 k2parts[:, a, c, :, :]).then_inc(s_k2st, 16)

            def project(r):
                sp.wait_ge(p_qT, r.count(2 * TT, 2 * TT))
                sp.dma_start(qk_terms[r.count(1)].rearrange("n p s -> p n s"), qkT[r.side]
                             ).then_inc(p_store[r.side], 16)
            rounds(sp, project)

            sp.wait_ge(s_k2st, 16 * TERMS * KC)

            def load_stack(r):
                wait(sp, A["st"], r.count(H, -H))
                for stk, order, base in ((qst, Q_TERM, 0), (kst, K_TERM, TERMS * KC)):
                    for s, a in enumerate(order):
                        parts = qk_terms[r.count(1)][base + a * KC:base + (a + 1) * KC]
                        sp.dma_start(stk[r.side][s * HD:(s + 1) * HD, :, :],
                                     parts.rearrange("c (h d) s -> d (c h) s", d=HD)
                                     ).then_inc(A["stack"][r.side], 16)

            def residual(r):
                wait(sp, a_x1, r.count(1, -1))
                sp.dma_start(resid[r.side][:], t["x"][:, bass.ds(r.count(TT), TT), :]
                             ).then_inc(a_res[r.side], 16)

            def store_tail(r):
                sp.wait_ge(a_x1, r.count(1, 1))
                sp.dma_start(x1_dram[r.count(1)], x_new[r.side][:]).then_inc(a_x1st[r.side], 16)
                sp.wait_ge(a_q2t, r.count(1, 1))
                sp.dma_start(q2_terms[r.count(1)].rearrange("n p s -> p n s"),
                             q2T[r.side][:, :, :, :].rearrange("p a c s -> p (a c) s")
                             ).then_inc(a_q2st[r.side], 16)

            sp.wait_ge(p_store[0], 16)
            load_stack(Round(0))
            for i in range(2):
                sp.wait_ge(p_store[i], 16 * NB // 2)
            sp_max_rows(sp, A, Round(0))

            def self_round(r):
                if not r.last:
                    load_stack(r.next())
                residual(r)
                if not r.last:
                    sp_max_rows(sp, A, r.next())
                if not r.first:
                    store_tail(r.previous())
            rounds(sp, self_round)
            store_tail(Round(NB - 1))

            for i in range(2):
                sp.wait_ge(s_v2st[i], 16 * NB // 2)
                sp.wait_ge(a_x1st[i], 16 * NB // 2)
                sp.wait_ge(a_q2st[i], 16 * NB // 2)
            sp.wait_ge(A["av"], GROUPS * NB)
            sp.wait_ge(a_xTps, NB)

            def load_stack2(r):
                wait(sp, C["st"], r.count(H, -H))
                for s in range(len(Q_TERM)):
                    for stk, terms_dram, a in ((qst, q2_terms, Q_TERM[s]), (k2st, k2_terms, K_TERM[s])):
                        parts = terms_dram[r.count(1)][a * KC:(a + 1) * KC]
                        sp.dma_start(stk[r.side][s * HD:(s + 1) * HD, :, :],
                                     parts.rearrange("c (h d) s -> d (c h) s", d=HD)
                                     ).then_inc(C["stack"][r.side], 16)

            def load_values2(r):
                wait(sp, C["av"], r.count(GROUPS, -GROUPS))
                sp.dma_start(v2pad[r.side][0:M, 0, :, :].rearrange("p h d -> p (h d)"), v2_dram[r.count(1)]
                             ).then_inc(c_v2[r.side], 16)
                wait(sp, c_x2, r.count(1, -1))
                sp.dma_start(resid[r.side][:], x1_dram[r.count(1)]).then_inc(c_res[r.side], 16)

            def store_out(r):
                sp.wait_ge(c_x2, r.count(1, 1))
                sp.dma_start(out[bass.ds(r.count(S), S), :].rearrange("(t p) c -> p t c", p=P),
                             x_new[r.side][:]).then_inc(c_out[r.side], 16)

            load_stack2(Round(0))
            sp_max_rows(sp, C, Round(0))

            def cross_round(r):
                if not r.last:
                    load_stack2(r.next())
                load_values2(r)
                sp.dma_start(moe[:, bass.ds(r.count(1), 1), :], t["moe"][:, bass.ds(r.count(1), 1), :]
                             ).then_inc(c_moe, 16)
                if not r.last:
                    sp_max_rows(sp, C, r.next())
                if not r.first:
                    store_out(r.previous())
            rounds(sp, cross_round)
            store_out(Round(NB - 1))

            sp.dma_start(routed[SPARE:SPARE + P, :], padding[:]).then_inc(m_pad, 16)
            sp.wait_ge(m_filled, 1)
            for e in range(E):
                at = sp.value_load(filled_i[0:1, e:e + 1], min_val=e * REGION, max_val=e * REGION + TOKENS)
                sp.dma_start(routed[bass.ds(at, P), :], padding[:]).then_inc(m_pad, 16)
            sp.wait_ge(m_pad, 16 * (E + 1))
            for i in range(2):
                sp.wait_ge(c_scatter[i], 16 * 2 * TT * NB // 2)
            sp.wait_ge(m_table, 1)

            def block_rows(r):
                at = sp.value_load(block_i[0:1, 0, bass.ds(r.count(1), 1)], min_val=0, max_val=SPARE)
                wait(sp, m_gate, r.count(1, -1))
                wait(sp, m_xTps, r.count(1, -1))
                sp.dma_start(xs[r.side], routed[bass.ds(at, P), :]).then_inc(m_xs[r.side], 16)
            blocks(sp, block_rows)

        @block.gpsimd
        def _(pool):
            for tile in (vpad[0], vpad[1], v2pad[0][:], v2pad[1][:], onesrow[:], mterms[:]):
                last = nc.gpsimd.memset(tile, 0.0)
            last.then_inc(s_zero, 1)
            pool.wait_ge(s_zero, 1)
            for half in range(2):
                nc.gpsimd.memset(onesrow[:, half, half * HD:(half + 1) * HD], 1.0)
            for stk in kst + k2st:
                pool.drain()
                last = nc.gpsimd.memset(stk[ROWS:AUG, :, :], 1.0)
            last.then_inc(s_ones, 1)

            pool.drain()
            pool.wait_ge(s_k2f, 4)
            flat = k2parts.rearrange("p a c b m -> p a (c b m)")
            for a in range(TERMS):
                last = nc.gpsimd.tensor_copy(flat[:, a, :], k2f)
                if a < TERMS - 1:
                    pool.drain()
                    nc.gpsimd.tensor_tensor(k2f, k2f, flat[:, a, :], ALU.subtract)
                    pool.drain()
            last.then_inc(s_k2t, 1)

            pool.wait_ge(s_tab, 1)

            def rotate(r):
                wait(pool, p_terms, r.count(1))
                for tt in range(TT):
                    pool.wait_ge(p_n, r.count(TT, tt + 1))
                    src = normed[:, tt, :].rearrange("p (q h d) -> p q h d", q=2, h=H)
                    dst = rotated[:, tt, :].rearrange("p (q h d) -> p q h d", q=2, h=H)
                    for lo, hi in ((0, HD // 2), (HD // 2, 0)):
                        turn = tables[:, 1, tt, :, lo:lo + HD // 2].unsqueeze(2).broadcast_to([P, 2, H, HD // 2])
                        nc.gpsimd.tensor_tensor(dst[:, :, :, lo:lo + HD // 2], src[:, :, :, hi:hi + HD // 2],
                                                turn, ALU.mult)
                    pool.drain()
                    shift = tables[:, 2, tt, :, :].unsqueeze(2).broadcast_to([P, 2, H, HD])
                    nc.gpsimd.tensor_tensor(dst, dst, shift, ALU.add).then_inc(p_rot, 1)
            rounds(pool, rotate)

            def spread_values(r):
                pool.wait_ge(p_vsb, r.count(1, 1))
                wait(pool, A["av"], r.count(GROUPS, -GROUPS))
                src = values[:, bass.ds(r.count(TT), TT), :].rearrange("p t (h two d) -> p t h two d", two=2, d=HD)
                dst = vpad[r.side].rearrange("p t (h two) d -> p t h two d", two=2)
                for half in range(2):
                    last = nc.gpsimd.tensor_copy(dst[:, :, :, half, half * HD:(half + 1) * HD],
                                                 src[:, :, :, half, :])
                last.then_inc(A["vpad"], 1)

            def self_round(r):
                if not r.last:
                    spread_values(r.next())
                pool.wait_ge(a_res[r.side], r.turns(16, 16))
                nc.gpsimd.tensor_tensor(resid[r.side][:], resid[r.side][:],
                                        bias_p[:, :].unsqueeze(1).broadcast_to([P, TT, D]),
                                        ALU.add).then_inc(a_resb, 1)
                if not r.first:
                    pool.wait_ge(a_var, r.previous().count(1, 1))
                    rsqrt_on_pool(pool).then_inc(a_rstd, 1)
            spread_values(Round(0))
            rounds(pool, self_round)
            pool.wait_ge(a_var, NB)
            rsqrt_on_pool(pool).then_inc(a_rstd, 1)

            pool.wait_ge(loaded2, 16 * len(later))

            def send(r):
                pool.wait_ge(c_pos, r.count(1, 1))
                pool.wait_ge(c_xn, r.count(1, 1))
                nc.gpsimd.tensor_tensor(rows3[r.side][:, :, D + 1:], pick[0][:], pick[1][:],
                                        ALU.add).then_inc(c_gates, 1)
                pool.drain()
                for tt in range(TT):
                    for i in range(2):
                        at = tt * 2 + i
                        nc.gpsimd.indirect_dma_start(
                            out=routed, in_=rows3[r.side][:, tt, :], in_offset=None,
                            out_offset=bass.IndirectOffsetOnAxis(ap=pos[r.side][:, at:at + 1], axis=0),
                        ).then_inc(c_scatter[r.side], 16)

            def cross_round(r):
                pool.wait_ge(c_res[r.side], r.turns(16, 16))
                nc.gpsimd.tensor_tensor(resid[r.side][:], resid[r.side][:],
                                        bias_2[:, :].unsqueeze(1).broadcast_to([P, TT, D]),
                                        ALU.add).then_inc(c_resb, 1)
                if not r.first:
                    pool.wait_ge(c_var, r.previous().count(1, 1))
                    rsqrt_on_pool(pool).then_inc(c_rstd, 1)
                if not (r.pair is None and r.own < 2):
                    send(r.previous().previous())
            rounds(pool, cross_round)
            pool.wait_ge(c_var, NB)
            rsqrt_on_pool(pool).then_inc(c_rstd, 1)
            send(Round(NB - 2))
            send(Round(NB - 1))

            for i in range(2):
                pool.wait_ge(c_out[i], 16 * NB // 2)

            def add_rows(r):
                wait(pool, m_added, r.count(16))
                pool.wait_ge(m_res, r.count(1, 1))
                nc.gpsimd.tensor_tensor(tokens[:], tokens_of[:, bass.ds(r.count(1), 1)],
                                        onesrow[:, 0, HD:HD + 1].bitcast(I32), ALU.add)
                pool.drain()
                nc.gpsimd.indirect_dma_start(
                    out=out, in_=result[r.side], in_offset=None,
                    out_offset=bass.IndirectOffsetOnAxis(ap=tokens[:], axis=0),
                    bounds_check=TOKENS - 1, oob_is_err=False, compute_op=ALU.add).then_inc(m_added, 16)
            blocks(pool, add_rows)
            pool.wait_ge(m_added, 16 * BLOCKS)

        @block.scalar
        def _(act):
            for i in range(4):
                act.wait_ge(s_k2ps, i + 1)
                nc.scalar.copy(k2f[:, i * (NB * M // 2):(i + 1) * (NB * M // 2)],
                               bank[(5, 7)[i % 2]][:, 0:NB * M // 2]).then_inc(s_k2f, 1)
            act.wait_ge(s_ones, 1)
            for b in range(NB):
                act.wait_ge(s_v2ps, b + 1)
                if b >= 2:
                    act.wait_ge(s_v2st[b % 2], 16 * (b // 2))
                src = bank[(5, 7)[b % 2]][0:M, 0:D].rearrange("p (h two d) -> p h two d", two=2, d=HD)
                dst = v2pad[b % 2][0:M, 0, :, :].rearrange("p (h two) d -> p h two d", two=2)
                for half in range(2):
                    last = nc.scalar.copy(dst[:, :, half, half * HD:(half + 1) * HD], src[:, :, half, :])
                last.then_inc(s_v2, 1)

            def evacuate_xT(r):
                act.wait_ge(p_xTps, r.count(1, 1))
                wait(act, p_v, r.count(1, -1))
                nc.scalar.copy(xnT[r.side], bank[6][:, :].rearrange("p (k s) -> p k s", k=KC)).then_inc(p_xT, 1)

            act.wait_ge(p_sum, 1)
            nc.scalar.activation(spread[:, TT * 2 * H:], spread[:, TT * 2 * H:], ACT.Sqrt).then_inc(p_root, 1)
            evacuate_xT(Round(0))

            def project(r):
                wait(act, p_sum, r.count(1, 1))
                for tt in range(TT):
                    act.wait_ge(p_qk, r.count(TT, tt + 1))
                    nc.scalar.activation(square[:, tt, :], bank[tt][:, :], ACT.Square).then_inc(p_sq, 1)
                act.wait_ge(p_v, r.count(1, 1))
                nc.scalar.copy(values[:, bass.ds(r.count(TT), TT), :],
                               bank[4][:, :].rearrange("p (t c) -> p t c", t=TT)).then_inc(p_vsb, 1)
                act.wait_ge(p_sum, r.count(1, 2))
                n = TT * 2 * H + (0 if r.last else TT)
                nc.scalar.activation(spread[:, 0:n], spread[:, 0:n], ACT.Sqrt).then_inc(p_root, 1)
                if not r.last:
                    evacuate_xT(r.next())
                wait(act, p_store[r.side], r.turns(16))
                for tt in range(TT):
                    for qk in range(2):
                        i = 2 * tt + qk
                        act.wait_ge(p_qTps, r.count(2 * TT, i + 1))
                        nc.scalar.copy(
                            qkT[r.side].rearrange("p (q n) s -> p q n s", q=2)[:, qk, :, tt * P:(tt + 1) * P],
                            bank16[2 + i % 2][:, 0:TERMS * KC * P].rearrange("p (n s) -> p n s", s=P)
                        ).then_inc(p_qT, 1)
            rounds(act, project)

            def tail(r, step):
                if step == 2:
                    act.wait_ge(a_xTps, r.count(1, 1))
                    wait(act, a_q2ps, r.count(1))
                    nc.scalar.copy(xn2T[:], bank[7][:, :].rearrange("p (k s) -> p k s", k=KC)).then_inc(a_xT, 1)
                if step == 3:
                    act.wait_ge(a_q2ps, r.count(1, 1))
                    wait(act, a_q2t, r.count(1))
                    for c in range(KC):
                        last = nc.scalar.activation(q2f[:, c, :], bank[6][:, c * S:(c + 1) * S], ACT.Identity,
                                                    bias=bias_q[:, c:c + 1], scale=HD ** -0.5)
                    last.then_inc(a_q2f, 1)

            act_max_rows(act, A, Round(0))

            def self_round(r):
                for g in range(GROUPS):
                    act_exp(act, A, r, g, S)
                    if not r.first:
                        tail(r.previous(), g)
                if not r.last:
                    act_max_rows(act, A, r.next())
            rounds(act, self_round)
            for step in range(GROUPS):
                tail(Round(NB - 1), step)

            def tail(r, step):
                if step == 0:
                    act.wait_ge(c_h, r.count(1, 1))
                    wait(act, c_y, r.count(1))
                    for c in range(HID // P):
                        last = nc.scalar.activation(hidT[:, c, :], bank[6 + c // 2][:, (c % 2) * S:(c % 2 + 1) * S],
                                                    ACT.Relu, bias=bias_1[:, c:c + 1])
                    last.then_inc(c_hT, 1)
                if step == 3:
                    act.wait_ge(c_xTps, r.count(1, 1))
                    wait(act, c_logit, r.count(1))
                    nc.scalar.copy(xn2T[:], bank[7][:, :].rearrange("p (k s) -> p k s", k=KC)).then_inc(c_xT, 1)

            def shares(r):
                act.wait_ge(c_gap, r.count(1, 1))
                nc.scalar.activation(share[1][:], gap[:], ACT.Exp).then_inc(c_ed, 1)

            act.wait_ge(loaded2, 16 * len(later))
            act.wait_ge(a_q2t, NB)
            act_max_rows(act, C, Round(0))

            def cross_round(r):
                for g in range(GROUPS):
                    act_exp(act, C, r, g, M)
                    if not r.first:
                        tail(r.previous(), g)
                    if g == 1 and not (r.pair is None and r.own < 2):
                        shares(r.previous().previous())
                if not r.last:
                    act_max_rows(act, C, r.next())
            rounds(act, cross_round)
            for g in range(GROUPS):
                tail(Round(NB - 1), g)
                if g == 1:
                    shares(Round(NB - 2))
            shares(Round(NB - 1))

            def rows_in(r):
                act.wait_ge(m_xTps, r.count(1, 1))
                wait(act, m_h, r.count(2, -2))
                nc.scalar.copy(xsT[r.side], bank[0][:, 0:D].rearrange("p (k c) -> p k c", k=KC)).then_inc(m_xT, 1)

            def silu(r):
                act.wait_ge(m_h, r.count(2, 1))
                wait(act, m_hid, r.count(1, -1))
                nc.scalar.activation(act1[r.side], bank[2 + 2 * r.side][:, :], ACT.Silu).then_inc(m_silu, 1)

            def hidden(r):
                act.wait_ge(m_hTps, r.count(1, 1))
                wait(act, m_y, r.count(1, -1))
                nc.scalar.copy(hidT2[r.side], bank[1][:, :].rearrange("p (k c) -> p k c", k=HID // P)
                               ).then_inc(m_hT, 1)

            rows_in(Round(0))
            rows_in(Round(1))
            silu(Round(0))

            def expert_block(r):
                if not r.final:
                    silu(r.next())
                hidden(r)
                if not r.last_two:
                    rows_in(r.next().next())
            blocks(act, expert_block, last=True)

        @block.vector
        def _(dve):
            dve.wait_ge(loaded, 16 * len(weights))
            for k in range(KC):
                nc.vector.tensor_reduce(wmean[:, k, :], wqkv[:, k, 0:2 * D].rearrange("p (g d) -> p g d", d=HD),
                                        axis=X, op=ALU.add)
            dve.drain()
            nc.vector.tensor_scalar(wmean, wmean, 1.0 / HD, None, ALU.mult)
            dve.drain()
            for k in range(KC):
                w = wqkv[:, k, 0:2 * D].rearrange("p (g d) -> p g d", d=HD)
                last = nc.vector.tensor_tensor(w, w, wmean[:, k, :].unsqueeze(2).broadcast_to([P, 2 * H, HD]),
                                               ALU.subtract)
            last.then_inc(s_tab, 1)
            dve.drain()
            for tt in range(TT):
                cos = angles[:, 0, tt, :].unsqueeze(1).broadcast_to([P, 2, HD])
                sin = angles[:, 1, tt, :].unsqueeze(1).broadcast_to([P, 2, HD])
                nc.vector.tensor_tensor(tables[:, 0, tt, :, :], affine[:, 0, :, :], cos, ALU.mult)
                nc.vector.tensor_tensor(tables[:, 1, tt, :, :], affine[:, 1, :, :], sin, ALU.mult)
                nc.vector.tensor_tensor(tables[:, 2, tt, :, :], affine[:, 2, :, :], cos, ALU.mult)
                nc.vector.tensor_tensor(wmean[:, tt, :].rearrange("p (q d) -> p q d", q=2), affine[:, 3, :, :],
                                        sin, ALU.mult)
            dve.drain()
            for tt in range(TT):
                nc.vector.tensor_tensor(tables[:, 2, tt, :, :], tables[:, 2, tt, :, :],
                                        wmean[:, tt, :].rearrange("p (q d) -> p q d", q=2), ALU.add)
            dve.drain()
            for a in range(3):
                last = nc.vector.tensor_scalar(tables[:, a, :, 0, :], tables[:, a, :, 0, :], HD ** -0.5, None,
                                               ALU.mult)
            last.then_inc(s_tab, 1)

            def row_variance(r):
                if r.pair is None and r.own == 0:
                    dve.wait_ge(x_first, 16)
                if r.own == 2:
                    dve.wait_ge(x_rest, 16)
                rows = x_all[:, bass.ds(r.count(TT), TT), :]
                for tt in range(TT):
                    nc.vector.bn_stats(moments[:, tt, :], rows[:, tt, :])
                dve.drain()
                for tt in range(TT):
                    nc.vector.bn_aggr(stats[:, tt, :], moments[:, tt, :])
                dve.drain()
                return nc.vector.tensor_scalar(spread[:, TT * 2 * H:], stats[:, :, 1], 1e-5, None, ALU.add)

            def norm_rows(r):
                rows = x_all[:, bass.ds(r.count(TT), TT), :]
                wait(dve, p_xTps, r.count(1, -1))
                for tt in range(TT):
                    at = TT * 2 * H + tt
                    last = nc.vector.tensor_scalar(xn[r.side][:, tt, :], rows[:, tt, :], stats[:, tt, 0:1],
                                                   spread[:, at:at + 1], ALU.subtract, ALU.mult)
                last.then_inc(p_xn, 1)

            row_variance(Round(0)).then_inc(p_sum, 1)
            dve.wait_ge(p_root, 1)
            nc.vector.reciprocal(spread[:, TT * 2 * H:], spread[:, TT * 2 * H:])
            dve.drain()
            norm_rows(Round(0))

            def project(r):
                if not r.last:
                    dve.drain()
                    row_variance(r.next())
                for tt in range(TT):
                    dve.wait_ge(p_sq, r.count(TT, tt + 1))
                    nc.vector.tensor_reduce(spread[:, tt * 2 * H:(tt + 1) * 2 * H],
                                            square[:, tt, :].rearrange("p (g d) -> p g d", d=HD), axis=X, op=ALU.add)
                dve.drain()
                heads = spread[:, 0:TT * 2 * H]
                nc.vector.tensor_scalar(heads, heads, 1.0 / HD, 1e-6, ALU.mult, ALU.add).then_inc(p_sum, 1)
                dve.wait_ge(p_root, r.count(1, 2))
                n = TT * 2 * H + (0 if r.last else TT)
                nc.vector.reciprocal(spread[:, 0:n], spread[:, 0:n])
                dve.drain()
                if not r.last:
                    norm_rows(r.next())
                for tt in range(TT):
                    nc.vector.tensor_tensor(normed[:, tt, :].rearrange("p (g d) -> p g d", d=HD),
                                            bank[tt][:, :].rearrange("p (g d) -> p g d", d=HD),
                                            spread[:, tt * 2 * H:(tt + 1) * 2 * H].unsqueeze(2).broadcast_to(
                                                [P, 2 * H, HD]), ALU.mult).then_inc(p_n, 1)
                dve.drain()
                for tt in range(TT):
                    nc.vector.tensor_tensor(
                        direct[:, tt, :].rearrange("p (q h d) -> p q h d", q=2, h=H),
                        normed[:, tt, :].rearrange("p (q h d) -> p q h d", q=2, h=H),
                        tables[:, 0, tt, :, :].unsqueeze(2).broadcast_to([P, 2, H, HD]), ALU.mult)
                dve.drain()
                dve.wait_ge(p_rot, r.count(TT, TT))
                nc.vector.tensor_tensor(direct, direct, rotated, ALU.add)
                dve.drain()
                wait(dve, p_qTps, r.count(2 * TT, -2 * TT))
                for a in range(TERMS - 1):
                    if a:
                        dve.drain()
                    nc.vector.tensor_copy(terms[r.side][:, :, a, :], direct)
                    dve.drain()
                    last = nc.vector.tensor_tensor(direct if a == 0 else terms[r.side][:, :, 2, :], direct,
                                                   terms[r.side][:, :, a, :], ALU.subtract)
                last.then_inc(p_terms, 1)
            rounds(dve, project)

            def tail(r, step):
                if step == 0:
                    dve.wait_ge(a_proj, r.count(1, 1))
                    dve.wait_ge(a_resb, r.count(1, 1))
                    wait(dve, a_x1st[r.side], r.turns(16))
                    nc.vector.tensor_tensor(x_new[r.side][:], bank[6][:, :].rearrange("p (t c) -> p t c", t=TT),
                                            resid[r.side][:], ALU.add).then_inc(a_x1, 1)
                    dve.drain()
                    moments_of(dve, x_new[r.side], 1e-5).then_inc(a_var, 1)
                if step == 1:
                    dve.wait_ge(a_rstd, r.count(1, 1))
                    wait(dve, a_xTps, r.count(1))
                    norm_into(xn2, x_new[r.side]).then_inc(a_xn, 1)

            def split_queries(r):
                dve.wait_ge(a_q2f, r.count(1, 1))
                wait(dve, a_q2st[r.side], r.turns(16))
                parts = q2T[r.side]
                nc.vector.tensor_copy(parts[:, 0, :, :], q2f)
                dve.drain()
                nc.vector.tensor_tensor(q2rest, q2f, parts[:, 0, :, :], ALU.subtract)
                dve.drain()
                nc.vector.tensor_copy(parts[:, 1, :, :], q2rest)
                dve.drain()
                nc.vector.tensor_tensor(parts[:, 2, :, :], q2rest, parts[:, 1, :, :],
                                        ALU.subtract).then_inc(a_q2t, 1)

            for slot in range(H):
                dve_max(dve, A, Round(0), slot, S)
            dve_split_max(dve, A, Round(0))
            nc.vector.tensor_scalar(bias_q[:], bias_q[:], HD ** -0.5, None, ALU.mult)

            def self_round(r):
                for g in range(GROUPS):
                    if not r.last:
                        for slot in range(g * GROUP, (g + 1) * GROUP):
                            dve_max(dve, A, r.next(), slot, S)
                    if not r.first:
                        tail(r.previous(), g)
                if not r.last:
                    dve_split_max(dve, A, r.next())
                dve_attn(dve, A, r, a_proj)
                if not r.first:
                    split_queries(r.previous())
            rounds(dve, self_round)
            for step in range(2):
                tail(Round(NB - 1), step)
            split_queries(Round(NB - 1))

            def tail(r, step):
                if step == 1:
                    dve.wait_ge(c_y, r.count(1, 1))
                    dve.wait_ge(c_resb, r.count(1, 1))
                    wait(dve, c_out[r.side], r.turns(16))
                    nc.vector.tensor_tensor(x_new[r.side][:], bank[6][:, :].rearrange("p (t c) -> p t c", t=TT),
                                            resid[r.side][:], ALU.add).then_inc(c_x2, 1)
                    dve.drain()
                    moments_of(dve, x_new[r.side], 1e-5).then_inc(c_var, 1)
                if step == 2:
                    dve.wait_ge(c_rstd, r.count(1, 1))
                    wait(dve, c_scatter[r.side], r.turns(16 * 2 * TT))
                    norm_into(rows3[r.side], x_new[r.side]).then_inc(c_xn, 1)

            def choose(r):
                wait(dve, c_gates, r.count(1))
                dve.wait_ge(c_logit, r.count(1, 1))
                nc.vector.tensor_copy(logits[:], bank[6][:, 0:TT * E].rearrange("p (t e) -> p t e", t=TT)
                                      ).then_inc(c_lg, 1)
                for i in range(2):
                    dve.drain()
                    nc.vector.tensor_reduce(best[i][:], logits[:], axis=X, op=ALU.max)
                    dve.drain()
                    nc.vector.tensor_tensor(key[:], logits[:], best[i][:, :].unsqueeze(2).broadcast_to([P, TT, E]),
                                            ALU.is_ge)
                    dve.drain()
                    nc.vector.tensor_tensor(key[:], key[:], first_of[:, :].unsqueeze(1).broadcast_to([P, TT, E]),
                                            ALU.mult)
                    dve.drain()
                    nc.vector.tensor_reduce(top[:], key[:], axis=X, op=ALU.max)
                    dve.drain()
                    nc.vector.tensor_tensor(pick[i][:], key[:], top[:, :].unsqueeze(2).broadcast_to([P, TT, E]),
                                            ALU.is_equal)
                    dve.drain()
                    if i == 0:
                        nc.vector.scalar_tensor_tensor(logits[:], pick[0][:], LOW, logits[:], ALU.mult, ALU.add)
                nc.vector.tensor_tensor(gap[:], best[1][:], best[0][:], ALU.subtract).then_inc(c_gap, 1)
                nc.vector.tensor_tensor(chosen[:], pick[0][:], pick[1][:], ALU.add).then_inc(c_mask, 1)

            def place(r):
                dve.wait_ge(c_ed, r.count(1, 1))
                nc.vector.tensor_scalar(share[0][:], share[1][:], 1.0, None, ALU.add)
                dve.drain()
                nc.vector.reciprocal(share[0][:], share[0][:])
                dve.drain()
                nc.vector.tensor_tensor(share[1][:], share[1][:], share[0][:], ALU.mult)
                dve.wait_ge(c_rank, r.count(1, 1))
                counted = bank[7][:, 0:(TT + 1) * E].rearrange("p (t e) -> p t e", e=E)
                nc.vector.tensor_tensor(ranks[:], counted[:, 0:TT, :],
                                        filled[:, :].unsqueeze(1).broadcast_to([P, TT, E]), ALU.add)
                dve.drain()
                nc.vector.tensor_tensor(filled[:], filled[:], counted[:, TT, :], ALU.add).then_inc(c_rk, 1)
                rows = rows3[r.side]
                nc.vector.tensor_copy(rows[:, :, D:D + 1].bitcast(I32),
                                      token_ids[:, bass.ds(r.count(TT), TT)].unsqueeze(2))
                for i in range(2):
                    nc.vector.tensor_tensor(taken[i][:], pick[i][:], ranks[:], ALU.mult)
                dve.drain()
                for i in range(2):
                    nc.vector.tensor_reduce(posf[:, :, i], taken[i][:], axis=X, op=ALU.add)
                    nc.vector.tensor_tensor(pick[i][:], pick[i][:],
                                            share[i][:, :].unsqueeze(2).broadcast_to([P, TT, E]), ALU.mult)
                dve.drain()
                nc.vector.tensor_copy(pos[r.side][:, :].rearrange("p (t i) -> p t i", t=TT), posf[:]
                                      ).then_inc(c_pos, 1)

            dve.wait_ge(loaded2, 16 * len(later))
            nc.vector.tensor_copy(filled[:], region_at[:])
            for slot in range(H):
                dve_max(dve, C, Round(0), slot, M)
            dve_split_max(dve, C, Round(0))

            def cross_round(r):
                for g in range(GROUPS):
                    if not r.last:
                        for slot in range(g * GROUP, (g + 1) * GROUP):
                            dve_max(dve, C, r.next(), slot, M)
                    if not r.first:
                        tail(r.previous(), g)
                    if g == 2 and not (r.pair is None and r.own < 2):
                        place(r.previous().previous())
                if not r.last:
                    dve_split_max(dve, C, r.next())
                dve_attn(dve, C, r, c_h)
                if not r.first:
                    choose(r.previous())
            rounds(dve, cross_round)
            for g in range(GROUPS):
                tail(Round(NB - 1), g)
                if g == 2:
                    place(Round(NB - 2))
            choose(Round(NB - 1))
            place(Round(NB - 1))

            dve.drain()
            nc.vector.tensor_copy(filled_i[:], filled[:]).then_inc(m_filled, 1)
            nc.vector.tensor_tensor(step_f[:], filled[:], region_at[:], ALU.subtract)
            dve.drain()
            nc.vector.tensor_scalar(count_i[:], step_f[:], float(P - 1), None, ALU.add)
            dve.drain()
            nc.vector.tensor_scalar(count_i[:], count_i[:], 7, None, ALU.arith_shift_right)
            dve.drain()
            nc.vector.tensor_copy(ends_f[:], count_i[:])
            for e in range(1, E):
                dve.drain()
                nc.vector.tensor_tensor(ends_f[:, e:e + 1], ends_f[:, e:e + 1], ends_f[:, e - 1:e], ALU.add)
            dve.drain()
            nc.vector.memset(past[:, :, 0:1], 1.0)
            nc.vector.tensor_tensor(past[:, :, 1:], block_at[:, :].unsqueeze(2).broadcast_to([P, BLOCKS, E]),
                                    ends_f[:, :].unsqueeze(1).broadcast_to([P, BLOCKS, E]), ALU.is_ge)
            nc.vector.tensor_copy(step_f[:], region_at[:])
            dve.drain()
            nc.vector.scalar_tensor_tensor(step_f[:, 1:], ends_f[:, 0:E - 1], -float(P), step_f[:, 1:],
                                           ALU.mult, ALU.add)
            nc.vector.tensor_tensor(of_block, past[:, :, 0:E], past[:, :, 1:], ALU.subtract)
            dve.drain()
            nc.vector.tensor_tensor(scaled, of_block, step_f[:, :].unsqueeze(1).broadcast_to([P, BLOCKS, E]),
                                    ALU.mult)
            nc.vector.tensor_reduce(block_f[:, 1, :], past[:, :, 1:], axis=X, op=ALU.add)
            dve.drain()
            nc.vector.tensor_reduce(block_f[:, 0, :], scaled, axis=X, op=ALU.add)
            nc.vector.tensor_scalar(block_f[:, 1, :], block_f[:, 1, :], float(E - 1), None, ALU.min)
            dve.drain()
            nc.vector.scalar_tensor_tensor(block_f[:, 0, :], block_at[:], float(P), block_f[:, 0, :],
                                           ALU.mult, ALU.add)
            dve.drain()
            nc.vector.tensor_scalar(scaled[:, :, 0], block_f[:, 0, :], -1.0, float(SPARE), ALU.mult, ALU.add)
            dve.drain()
            nc.vector.tensor_tensor(scaled[:, :, 0], scaled[:, :, 0], past[:, :, E], ALU.mult)
            dve.drain()
            nc.vector.tensor_tensor(block_f[:, 0, :], block_f[:, 0, :], scaled[:, :, 0], ALU.add)
            dve.drain()
            nc.vector.tensor_copy(block_i, block_f[:]).then_inc(m_table, 1)

            def read_columns(r):
                dve.wait_ge(m_xs[r.side], r.turns(16, 16))
                nc.vector.tensor_tensor(gates[r.side], xs[r.side][:, D + 1:],
                                        of_block[:, bass.ds(r.count(1), 1), :].rearrange("p o e -> p (o e)"),
                                        ALU.mult)
                dve.drain()
                nc.vector.tensor_copy(tokens_of[:, bass.ds(r.count(1), 1)], xs[r.side][:, D:D + 1].bitcast(I32))
                nc.vector.tensor_reduce(gate[r.side], gates[r.side], axis=X, op=ALU.add).then_inc(m_gate, 1)

            def multiply(r):
                dve.wait_ge(m_silu, r.count(1, 1))
                dve.wait_ge(m_h, r.count(2, 2))
                wait(dve, m_hTps, r.count(1, -1))
                nc.vector.scalar_tensor_tensor(hid[r.side], act1[r.side], gate[r.side], bank[3 + 2 * r.side][:, :],
                                               ALU.mult, ALU.mult).then_inc(m_hid, 1)

            def take_result(r):
                dve.wait_ge(m_y, r.count(1, 1))
                wait(dve, m_added, r.count(16, -16))
                nc.vector.tensor_copy(result[r.side], bank[6 + r.side][:, 0:D]).then_inc(m_res, 1)

            read_columns(Round(0))
            read_columns(Round(1))
            dve.drain()
            multiply(Round(0))

            def expert_block(r):
                if not r.final:
                    multiply(r.next())
                if not r.last_two:
                    read_columns(r.next().next())
                if not r.first:
                    take_result(r.previous())
                dve.drain()
            blocks(dve, expert_block, last=True)
            take_result(Round(BLOCKS - 1))

        @block.tensor
        def _(pe):
            pe.wait_ge(loaded, 16 * len(weights))
            for i in range(4):
                c, half = i // 2, i % 2
                if i >= 2:
                    pe.wait_ge(s_k2f, i - 1)
                for k in range(KC):
                    last = nc.tensor.matmul(bank[(5, 7)[i % 2]][:, 0:NB * M // 2], wk[:, k, c * P:(c + 1) * P],
                                            ctxT[:, k, half * (NB * M // 2):(half + 1) * (NB * M // 2)],
                                            start=(k == 0), stop=(k == KC - 1))
                last.then_inc(s_k2ps, 1)
            pe.wait_ge(s_k2f, 4)
            for b in range(NB):
                if b >= 2:
                    pe.wait_ge(s_v2, b - 1)
                for k in range(KC):
                    last = nc.tensor.matmul(bank[(5, 7)[b % 2]][0:M, 0:D], ctxT[:, k, b * M:(b + 1) * M],
                                            wv[:, k, :], start=(k == 0), stop=(k == KC - 1))
                last.then_inc(s_v2ps, 1)

            def rows_in(r):
                pe.wait_ge(p_xn, r.count(1, 1))
                wait(pe, p_xT, r.count(1))
                for tt in range(TT):
                    for k in range(KC):
                        last = nc.tensor.transpose(bank[6][:, k * S + tt * P:k * S + (tt + 1) * P],
                                                   xn[r.side][:, tt, k * P:(k + 1) * P], identf[:])
                last.then_inc(p_xTps, 1)
                pe.wait_ge(p_xT, r.count(1, 1))
                for tt in range(TT):
                    wait(pe, p_n, r.count(TT, tt - 1))
                    for k in range(KC):
                        last = nc.tensor.matmul(bank[tt][:, :], xnT[r.side][:, k, tt * P:(tt + 1) * P],
                                                wqkv[:, k, 0:2 * D], start=(k == 0), stop=(k == KC - 1))
                    last.then_inc(p_qk, 1)
                wait(pe, p_vsb, r.count(1))
                for tt in range(TT):
                    for k in range(KC):
                        last = nc.tensor.matmul(bank[4][:, tt * D:(tt + 1) * D], xnT[r.side][:, k, tt * P:(tt + 1) * P],
                                                wqkv[:, k, 2 * D:3 * D], start=(k == 0), stop=(k == KC - 1))
                last.then_inc(p_v, 1)

            pe.wait_ge(s_tab, 1)
            rows_in(Round(0))

            def project(r):
                if not r.last:
                    rows_in(r.next())
                pe.wait_ge(p_terms, r.count(1, 1))
                for tt in range(TT):
                    for qk in range(2):
                        i = 2 * tt + qk
                        wait(pe, p_qT, r.count(2 * TT, i - 1))
                        for a in range(TERMS):
                            for c in range(KC):
                                n = a * KC + c
                                last = nc.tensor.transpose(
                                    bank16[2 + i % 2][:, n * P:(n + 1) * P],
                                    terms[r.side][:, tt, a, qk * D + c * P:qk * D + (c + 1) * P], ident[:])
                        last.then_inc(p_qTps, 1)
            rounds(pe, project)

            pe.wait_ge(p_n, TT * NB)
            pe.wait_ge(p_qT, 2 * TT * NB)
            pe.wait_ge(p_vsb, NB)
            pe.wait_ge(s_v2, NB)
            pe.wait_ge(s_ones, 1)

            def tail(r, step):
                if step == 0:
                    pe.wait_ge(A["attn"], r.count(1, 1))
                    wait(pe, a_q2f, r.count(1))
                    for tt in range(TT):
                        for c in range(KC):
                            last = nc.tensor.matmul(bank[6][:, tt * D:(tt + 1) * D], attnT[:, c, tt * P:(tt + 1) * P],
                                                    wp[:, c, :], start=(c == 0), stop=(c == KC - 1))
                    last.then_inc(a_proj, 1)
                if step == 2:
                    pe.wait_ge(a_xn, r.count(1, 1))
                    pe.wait_ge(A["mT"], r.count(1, 1 if r.last else 2))
                    for tt in range(TT):
                        for k in range(KC):
                            last = nc.tensor.transpose(bank[7][:, k * S + tt * P:k * S + (tt + 1) * P],
                                                       xn2[:, tt, k * P:(k + 1) * P], identf[:])
                    last.then_inc(a_xTps, 1)
                if step == 3:
                    pe.wait_ge(a_xT, r.count(1, 1))
                    pe.wait_ge(a_x1, r.count(1, 1))
                    for c in range(KC):
                        for k in range(KC):
                            last = nc.tensor.matmul(bank[6][:, c * S:(c + 1) * S], wq[:, k, c * P:(c + 1) * P],
                                                    xn2T[:, k, :], start=(k == 0), stop=(k == KC - 1))
                    last.then_inc(a_q2ps, 1)

            for slot in range(H):
                pe_score(pe, A, Round(0), slot, S, kst)
            pe_max_rows(pe, A, Round(0))

            def self_round(r):
                for g in range(GROUPS):
                    pe_exponents(pe, A, r, g, S, kst)
                    if not r.last:
                        for slot in range(g * GROUP, (g + 1) * GROUP):
                            pe_score(pe, A, r.next(), slot, S, kst)
                    if not r.first:
                        tail(r.previous(), g)
                    if g == 1:
                        pe.wait_ge(A["vpad"], r.count(1, 1))
                    if g > 0:
                        pe_values(pe, A, r, g - 1, S, vpad)
                if not r.last:
                    wait(pe, a_xT, r.count(1))
                    pe_max_rows(pe, A, r.next())
                pe_values(pe, A, r, GROUPS - 1, S, vpad)
            rounds(pe, self_round)
            for step in range(GROUPS):
                tail(Round(NB - 1), step)

            pe.wait_ge(A["max"], H * NB)
            pe.wait_ge(A["exp"], H * NB)
            pe.wait_ge(A["mT"], NB)
            pe.wait_ge(a_q2f, NB)
            pe.wait_ge(loaded2, 16 * len(later))

            def tail(r, step):
                if step == 0:
                    pe.wait_ge(C["attn"], r.count(1, 1))
                    wait(pe, c_lg, r.count(1))
                    pe.wait_ge(C["mT"], r.count(1, 1 if r.last else 2))
                    for c in range(HID // P):
                        for k in range(KC):
                            last = nc.tensor.matmul(bank[6 + c // 2][:, (c % 2) * S:(c % 2 + 1) * S],
                                                    w1[:, k, c * P:(c + 1) * P], attnT[:, k, :],
                                                    start=(k == 0), stop=(k == KC - 1))
                    last.then_inc(c_h, 1)
                if step == 1:
                    pe.wait_ge(c_hT, r.count(1, 1))
                    for tt in range(TT):
                        for k in range(HID // P):
                            last = nc.tensor.matmul(bank[6][:, tt * D:(tt + 1) * D], hidT[:, k, tt * P:(tt + 1) * P],
                                                    w2[:, k, :], start=(k == 0), stop=(k == HID // P - 1))
                    last.then_inc(c_y, 1)
                if step == 3:
                    pe.wait_ge(c_xn, r.count(1, 1))
                    for tt in range(TT):
                        for k in range(KC):
                            last = nc.tensor.transpose(bank[7][:, k * S + tt * P:k * S + (tt + 1) * P],
                                                       rows3[r.side][:, tt, k * P:(k + 1) * P], identf[:])
                    last.then_inc(c_xTps, 1)

            def route(r):
                pe.wait_ge(c_xT, r.count(1, 1))
                pe.wait_ge(c_x2, r.count(1, 1))
                for tt in range(TT):
                    for k in range(KC):
                        last = nc.tensor.matmul(bank[6][:, tt * E:(tt + 1) * E], xn2T[:, k, tt * P:(tt + 1) * P],
                                                wg[:, k, :], start=(k == 0), stop=(k == KC - 1))
                last.then_inc(c_logit, 1)

            def rank(r):
                pe.wait_ge(c_mask, r.count(1, 1))
                nc.tensor.matmul(bank[7][:, 0:E], below[:], chosen[:, 0, :], start=True, stop=True)
                nc.tensor.matmul(bank[7][:, E:2 * E], below[:], chosen[:, 1, :], start=True, stop=False)
                nc.tensor.matmul(bank[7][:, E:2 * E], ones[:], chosen[:, 0, :], start=False, stop=True)
                nc.tensor.matmul(bank[7][:, 2 * E:3 * E], ones[:], chosen[:, 0, :], start=True, stop=False)
                nc.tensor.matmul(bank[7][:, 2 * E:3 * E], ones[:], chosen[:, 1, :], start=False,
                                 stop=True).then_inc(c_rank, 1)

            for slot in range(H):
                pe_score(pe, C, Round(0), slot, M, k2st)
            pe_max_rows(pe, C, Round(0))

            def cross_round(r):
                for g in range(GROUPS):
                    pe_exponents(pe, C, r, g, M, k2st)
                    if not r.last:
                        for slot in range(g * GROUP, (g + 1) * GROUP):
                            pe_score(pe, C, r.next(), slot, M, k2st)
                    if g == 3 and not (r.pair is None and r.own < 2):
                        pe.wait_ge(c_rk, r.previous().count(1))
                    if not r.first:
                        tail(r.previous(), g)
                    if g == 2 and not (r.pair is None and r.own < 2):
                        rank(r.previous().previous())
                    if g == 1:
                        pe.wait_ge(c_v2[r.side], r.turns(16, 16))
                    if g > 0:
                        pe_values(pe, C, r, g - 1, M, v2pad)
                if not r.last:
                    wait(pe, c_xT, r.count(1))
                    pe_max_rows(pe, C, r.next())
                pe_values(pe, C, r, GROUPS - 1, M, v2pad)
                if not r.first:
                    route(r.previous())
            rounds(pe, cross_round)
            for g in range(GROUPS):
                if g == 3:
                    pe.wait_ge(c_rk, NB - 1)
                tail(Round(NB - 1), g)
                if g == 2:
                    rank(Round(NB - 2))
            route(Round(NB - 1))
            pe.wait_ge(c_xT, NB)
            rank(Round(NB - 1))

            pe.wait_ge(c_moe, 16 * E)
            pe.wait_ge(C["max"], H * NB)
            pe.wait_ge(C["exp"], H * NB)
            pe.wait_ge(C["attn"], NB)
            pe.wait_ge(c_lg, NB)
            pe.wait_ge(c_rk, NB)
            pe.wait_ge(m_table, 1)

            def rows_in(r):
                pe.wait_ge(m_xs[r.side], r.turns(16, 16))
                wait(pe, m_xT, r.count(1))
                for k in range(KC):
                    last = nc.tensor.transpose(bank[0][:, k * P:(k + 1) * P], xs[r.side][:, k * P:(k + 1) * P],
                                               identf[:])
                last.then_inc(m_xTps, 1)

            def first_layer(r):
                expert = pe.value_load(block_i[0:1, 1, bass.ds(r.count(1), 1)], min_val=0, max_val=E - 1)
                pe.wait_ge(m_xT, r.count(1, 1))
                wait(pe, m_hid, r.count(1, -1))
                for i in range(2):
                    for k in range(KC):
                        at = (i * KC + k) * HID
                        last = nc.tensor.matmul(bank[2 + 2 * r.side + i][:, :], xsT[r.side][:, k, :],
                                                moe[:, bass.ds(expert, 1), at:at + HID].rearrange("p o n -> p (o n)"),
                                                start=(k == 0), stop=(k == KC - 1))
                    last.then_inc(m_h, 1)

            def turn_hidden(r):
                pe.wait_ge(m_hid, r.count(1, 1))
                wait(pe, m_hT, r.count(1))
                for k in range(HID // P):
                    last = nc.tensor.transpose(bank[1][:, k * P:(k + 1) * P], hid[r.side][:, k * P:(k + 1) * P],
                                               identf[:])
                last.then_inc(m_hTps, 1)

            def second_layer(r):
                expert = pe.value_load(block_i[0:1, 1, bass.ds(r.count(1), 1)], min_val=0, max_val=E - 1)
                pe.wait_ge(m_hT, r.count(1, 1))
                wait(pe, m_res, r.count(1, -1))
                for k in range(HID // P):
                    at = 2 * KC * HID + k * D
                    last = nc.tensor.matmul(bank[6 + r.side][:, 0:D], hidT2[r.side][:, k, :],
                                            moe[:, bass.ds(expert, 1), at:at + D].rearrange("p o n -> p (o n)"),
                                            start=(k == 0), stop=(k == HID // P - 1))
                last.then_inc(m_y, 1)

            rows_in(Round(0))
            rows_in(Round(1))
            first_layer(Round(0))

            def expert_block(r):
                if not r.final:
                    first_layer(r.next())
                turn_hidden(r)
                if not r.last_two:
                    rows_in(r.next().next())
                if not r.first:
                    second_layer(r.previous())
            blocks(pe, expert_block, last=True)
            second_layer(Round(BLOCKS - 1))


def layouts(x, ctx, w):
    def rows(a, pieces):
        return np.ascontiguousarray(a.reshape(pieces, P, -1).transpose(1, 0, 2))

    def spread(a):
        return np.ascontiguousarray(np.broadcast_to(a, (P,) + a.shape))

    swap = np.r_[HD // 2:HD, 0:HD // 2]
    freq = 1.0 / np.float32(10000.0) ** (np.arange(HD // 2, dtype=np.float32) / np.float32(HD // 2))
    emb = np.outer(np.arange(S, dtype=np.float32), freq.astype(np.float32)).astype(np.float32)
    emb = np.concatenate([emb, emb], -1)
    sign = np.where(np.arange(HD) < HD // 2, -1.0, 1.0)
    cos = np.cos(emb).astype(np.float32).reshape(TT, P, HD).transpose(1, 0, 2)
    sin = (np.sin(emb) * sign).astype(np.float32).reshape(TT, P, HD).transpose(1, 0, 2)
    gamma = np.stack([w["attn_q_gamma"], w["attn_k_gamma"]])
    beta = np.stack([w["attn_q_beta"], w["attn_k_beta"]])
    pad = KC * P - TEXT - 1

    def padded(weight, bias):
        return rows(np.concatenate([weight, bias[None], np.zeros((pad, D), np.float32)]), KC)

    columns = ctx.reshape(NB * M, TEXT).T
    bf16 = mybir.dt.np(BF16)
    token = np.arange(P)
    padding = np.zeros((P, ROW), np.int32)
    padding[:, D] = TOKENS + token
    up = [w["ffn_" + n].transpose(0, 2, 1).reshape(E, KC, P, HID) for n in ("w1", "w3")]
    down = w["ffn_w2"].transpose(0, 2, 1).reshape(E, HID // P, P, D)
    experts = [a.transpose(2, 0, 1, 3).reshape(P, E, -1) for a in (*up, down)]
    return {
        "moe": np.ascontiguousarray(np.concatenate(experts, -1)),
        "w1": rows(w["xattn_W1"], KC),
        "w2": rows(w["xattn_W2"], HID // P),
        "wg": rows(w["ffn_wg"].T, KC),
        "bias_1": np.ascontiguousarray(w["xattn_b1"].reshape(HID // P, P).T),
        "bias_2": spread(w["xattn_b2"]),
        "below": np.triu(np.ones((P, P)), 1).astype(bf16),
        "ones": np.ones((P, P), bf16),
        "token_ids": (np.arange(NB * TT)[None, :] * P + token[:, None]).astype(np.int32),
        "first_of": spread(np.arange(E, 0, -1).astype(np.float32)),
        "region_at": spread((np.arange(E) * REGION).astype(np.float32)),
        "block_at": spread(np.arange(BLOCKS).astype(np.float32)),
        "padding": padding.view(np.float32),
        "x": rows(x.reshape(TOKENS, D), NB * TT),
        "wqkv": rows(w["attn_w_qkv"].T, KC),
        "angles": np.ascontiguousarray(np.stack([cos, sin], 1)),
        "affine": spread(np.stack([gamma, gamma[:, swap], beta, beta[:, swap]])),
        "identf": np.eye(P, dtype=np.float32),
        "ident": np.eye(P).astype(bf16),
        "ctxT": rows(np.concatenate([columns, np.ones((1, NB * M), np.float32),
                                     np.zeros((pad, NB * M), np.float32)]), KC),
        "wk": padded(w["xattn_Wk"], w["xattn_bk"]),
        "wv": padded(w["xattn_Wv"], w["xattn_bv"]),
        "wp": rows(w["attn_w_proj"].T, KC),
        "wq": rows(w["xattn_Wq"], KC),
        "bias_q": np.ascontiguousarray(w["xattn_bq"].reshape(KC, P).T),
        "bias_p": spread(w["attn_b_proj"]),
    }


def kernel(**inputs):
    import concourse.bacc as bacc
    from concourse.bass_utils import run_bass_kernel_spmd

    given = {k: np.asarray(v) for k, v in inputs.items()}
    arrays = layouts(given["x"], given["ctx_768"],
                     {k[3:]: v for k, v in given.items() if k.startswith("L0_")})
    nc = bacc.Bacc("TRN2", target_bir_lowering=False, num_devices=1)
    tiles = {k: nc.dram_tensor("in_" + k, a.shape, mybir.dt.from_np(a.dtype), kind="ExternalInput").ap()
             for k, a in arrays.items()}
    out = nc.dram_tensor("out", (TOKENS, D), F32, kind="ExternalOutput").ap()
    decoder_layer(nc, tiles, out)
    result = run_bass_kernel_spmd(nc, [{"in_" + k: a for k, a in arrays.items()}], core_ids=[0])
    return result.results[0]["out"].reshape(NB, S, D)
```

```python
from contextlib import ExitStack

import numpy as np

import concourse.bass as bass
from concourse import mybir
from concourse.alu_op_type import AluOpType as ALU

F32, BF16, I32 = mybir.dt.float32, mybir.dt.bfloat16, mybir.dt.int32
ACT = mybir.ActivationFunctionType
X = mybir.AxisListType.X

P = 128
NB, S, D = 8, 256, 256
H, HD = 16, 16
M = 77
TEXT = 192
TT = S // P
KC = D // P
HID = 512
E = 8
TOKENS = NB * S
TERMS = 3
PRODUCTS = 6
STORED = 4
Q_STORES = ((0, 0, 3), (3, 0, 1))
K_STORES = ((0, 2, 1), (1, 0, 1), (2, 0, 2))
Q_LOADS = ((0, 0, 4), (4, 0, 2))
K_LOADS = ((0, 0, 4), (4, 2, 2))
ROWS = HD * PRODUCTS
AUG = ROWS + TERMS
GROUP = 4
GROUPS = H // GROUP
HALF = H // 2
LOADS = 16 * (len(Q_LOADS) + len(K_LOADS))
STORES = 16 * (len(Q_STORES) + len(K_STORES))
SCORED = (range(0, 6), range(6, 12), range(12, H), range(0))
HEADS = [8 * c + 2 * j + half for c in range(2) for half in range(2) for j in range(4)]
ROW = D + 1 + E
REGION = TOKENS + P
BLOCKS = 2 * TOKENS // P + E - 1
SPARE = E * REGION
LOW = -3.0e38
MAGIC = float(0x5F3759DF)
NEWTON = 3


class Round:

    def __init__(self, own, pair=None):
        self.own, self.pair, self.side = own, pair, own % 2

    def count(self, per, more=0):
        known = per * self.own + more
        return known if self.pair is None else self.pair * (2 * per) + known

    def turns(self, per, more=0):
        known = per * (self.own // 2) + more
        return known if self.pair is None else self.pair * per + known

    def next(self):
        return Round(self.own + 1, self.pair)

    def previous(self):
        return Round(self.own - 1, self.pair)

    @property
    def first(self):
        return self.pair is None and self.own == 0

    @property
    def final(self):
        return self.pair is None and self.own == BLOCKS - 1

    def at(self, shift):
        if self.pair is None and not 0 <= self.own + shift < NB:
            return None
        return Round(self.own + shift, self.pair)

    @property
    def last_two(self):
        return self.pair is None and self.own >= BLOCKS - 2

    @property
    def last(self):
        return self.pair is None and self.own == NB - 1


def rounds(eng, body, after=0):
    for own in range(2):
        body(Round(own))
    with eng.Fori(0, (NB - 4) // 2) as pair:
        body(Round(2, pair))
        body(Round(3, pair))
    for own in range(NB - 2, NB + after):
        body(Round(own))


def blocks(eng, body, last=False):
    for own in range(3):
        body(Round(own))
    with eng.Fori(0, (BLOCKS - 3) // 2 - last) as pair:
        body(Round(3, pair))
        body(Round(4, pair))
    if last:
        body(Round(BLOCKS - 2))
        body(Round(BLOCKS - 1))


def wait(eng, sem, value):
    if not isinstance(value, int) or value > 0:
        eng.wait_ge(sem, value)


def decoder_layer(nc, t, out):
    ctx = ExitStack()
    with ctx:
        def sb(name, shape, dt=F32):
            return ctx.enter_context(nc.sbuf_tensor(name, shape, dt))

        def sem(name):
            return ctx.enter_context(nc.semaphore(name))

        qk_terms = nc.dram_tensor("qk_terms", [NB, 2, STORED, D, S], BF16, kind="Internal").ap()
        x1_dram = nc.dram_tensor("x1_dram", [NB, P, TT, D], F32, kind="Internal").ap()
        q2_terms = nc.dram_tensor("q2_terms", [NB, STORED, D, S], BF16, kind="Internal").ap()
        k2_terms = nc.dram_tensor("k2_terms", [NB, STORED, D, M], BF16, kind="Internal").ap()
        v2_dram = nc.dram_tensor("v2_dram", [NB, M, H * 2 * HD], F32, kind="Internal").ap()
        routed = nc.dram_tensor("routed", [SPARE + P, ROW], F32, kind="Internal").ap()

        early = sb("early", [P, E * 3 * 2 * HID])
        moe = early[:, :].rearrange("p (e n) -> p e n", e=E)
        used = [0]

        def carve(words):
            at = used[0]
            used[0] += words
            assert used[0] <= E * 3 * 2 * HID
            return early[:, at:at + words]

        wqkv = carve(KC * 3 * D).rearrange("p (k n) -> p k n", k=KC)
        xn = [carve(TT * D).rearrange("p (t c) -> p t c", t=TT) for _ in range(2)]
        xnT = [carve(KC * S).rearrange("p (k s) -> p k s", k=KC) for _ in range(2)]
        square = carve(TT * 2 * D).rearrange("p (t c) -> p t c", t=TT)
        normed = carve(TT * 2 * D).rearrange("p (t c) -> p t c", t=TT)
        direct = carve(TT * 2 * D).rearrange("p (t c) -> p t c", t=TT)
        rotated = carve(TT * 2 * D).rearrange("p (t c) -> p t c", t=TT)
        terms = [carve(TT * TERMS * D).bitcast(BF16).rearrange("p (t a c) -> p t a c", t=TT, a=TERMS)
                 for _ in range(2)]
        qkT = [carve(2 * TERMS * KC * S // 2).bitcast(BF16).rearrange("p (q a c s) -> p q a c s", q=2, a=TERMS, s=S)
               for _ in range(2)]
        values = carve(NB * TT * D).rearrange("p (t c) -> p t c", t=NB * TT)
        vpad = [carve(TT * H * 2 * HD).rearrange("p (t h d) -> p t h d", t=TT, h=H) for _ in range(2)]
        ctxT = carve(KC * NB * M).rearrange("p (k m) -> p k m", k=KC)
        wk = carve(KC * D).rearrange("p (k n) -> p k n", k=KC)
        wv = carve(KC * D).rearrange("p (k n) -> p k n", k=KC)
        tables = carve(3 * TT * 2 * HD).rearrange("p (a t q d) -> p a t q d", a=3, t=TT, q=2)
        affine = carve(4 * 2 * HD).rearrange("p (a q d) -> p a q d", a=4, q=2)
        angles = carve(2 * TT * HD).rearrange("p (a t d) -> p a t d", a=2, t=TT)
        wmean = carve(KC * 2 * H).rearrange("p (k g) -> p k g", k=KC)
        spread = carve(TT * 2 * H + TT)

        qst = [sb(f"qst{i}", [P, H, S], BF16) for i in range(2)]
        kst = [sb(f"kst{i}", [P, H, S], BF16) for i in range(2)]
        k2st = [sb(f"k2st{i}", [P, H, M], BF16) for i in range(2)]
        v2pad = [sb(f"v2pad{i}", [P, 1, H, 2 * HD]) for i in range(2)]
        probs = sb("probs", [P, 2, GROUP, 2 * S])
        x_all = probs[:, :, :, :].rearrange("p a b c -> p (a b c)").rearrange("p (t c) -> p t c", c=D)
        k2f = qst[0][:, :, :].rearrange("p h s -> p (h s)").bitcast(F32)[:, 0:KC * NB * M]
        k2parts = qst[1][:, :, :].rearrange("p h s -> p (h s)")[:, 0:TERMS * KC * NB * M].rearrange(
            "p (a c b m) -> p a c b m", a=TERMS, c=KC, b=NB)
        wp = sb("wp", [P, KC, D])
        wq = sb("wq", [P, KC, D])
        w1 = sb("w1", [P, KC, HID])
        w2 = sb("w2", [P, HID // P, D])
        wg = sb("wg", [P, KC, E])
        identf = sb("identf", [P, P])
        ident = sb("ident", [P, P], BF16)
        below = sb("below", [P, P], BF16)
        ones = sb("ones", [P, P], BF16)
        onesrow = sb("onesrow", [P, 2, 2 * HD])
        bias_p = sb("bias_p", [P, D])
        bias_2 = sb("bias_2", [P, D])
        bias_q = sb("bias_q", [P, KC])
        bias_1 = sb("bias_1", [P, HID // P])
        resid = [sb(f"resid{i}", [P, TT, D]) for i in range(2)]
        x_new = [sb(f"x_new{i}", [P, TT, D]) for i in range(2)]
        xn2 = sb("xn2", [P, TT, D])
        xn2T = sb("xn2T", [P, KC, S])
        q2both = sb("q2both", [P, 2 * KC, S])
        q2f, q2rest = q2both[:, 0:KC, :], q2both[:, KC:, :]
        hidT = q2both[:, :, :]
        q2T = [sb(f"q2T{i}", [P, TERMS, KC, S], BF16) for i in range(2)]
        attnT = sb("attnT", [P, 2, S])
        recip = sb("recip", [P, 2, S])
        maxes = sb("maxes", [P, H, TT])
        mrest = sb("mrest", [P, TT, H])
        mterms = sb("mterms", [P, TT, P // H, H], BF16)
        mT = sb("mT", [TERMS * H, S], BF16)
        rows3 = [sb(f"rows3_{i}", [P, TT, ROW]) for i in range(2)]
        token_ids = sb("token_ids", [P, NB * TT], I32)
        logits = sb("logits", [P, TT, E])
        first_of = sb("first_of", [P, E])
        pick = [sb(f"pick{i}", [P, TT, E]) for i in range(2)]
        key = sb("key", [P, TT, E])
        best = [sb(f"best{i}", [P, TT]) for i in range(2)]
        chosen = sb("chosen", [P, TT, E], BF16)
        gap = sb("gap", [P, TT])
        share = [sb(f"share{i}", [P, TT]) for i in range(2)]
        top = sb("top", [P, TT])
        ranks = sb("ranks", [P, TT, E])
        taken = [sb(f"taken{i}", [P, TT, E]) for i in range(2)]
        filled = sb("filled", [P, E])
        posf = sb("posf", [P, TT, 2])
        pos = [sb(f"pos{i}", [P, TT * 2], I32) for i in range(2)]
        tokens = sb("tokens", [P, 1], I32)
        padding = sb("padding", [P, ROW])
        region_at = sb("region_at", [P, E])
        block_at = sb("block_at", [P, BLOCKS])
        filled_i = sb("filled_i", [P, E], I32)
        count_i = sb("count_i", [P, E], I32)
        ends_f = sb("ends_f", [P, E])
        step_f = sb("step_f", [P, E])
        flat_p = probs[:, :, :, :].rearrange("p a b c -> p (a b c)")
        past = flat_p[:, 0:BLOCKS * (E + 1)].rearrange("p (b e) -> p b e", e=E + 1)
        of_block = flat_p[:, 512:512 + BLOCKS * E].rearrange("p (b e) -> p b e", e=E)
        scaled = flat_p[:, 1024:1024 + BLOCKS * E].rearrange("p (b e) -> p b e", e=E)
        block_f = flat_p[:, 1536:1536 + 2 * BLOCKS].rearrange("p (a b) -> p a b", a=2)
        tokens_of = flat_p[:, 2560:2560 + BLOCKS].bitcast(I32)
        block_i = flat_p[:, 2048:2048 + 2 * BLOCKS].rearrange("p (a b) -> p a b", a=2).bitcast(I32)
        flat_q = [q[:, :, :].rearrange("p h s -> p (h s)").bitcast(F32) for q in qst]
        xs = [f[:, 0:ROW] for f in flat_q]
        xsT = [f[:, 288:288 + D].rearrange("p (k c) -> p k c", k=KC) for f in flat_q]
        act1 = [f[:, 544:544 + HID] for f in flat_q]
        hid = [f[:, 1056:1056 + HID] for f in flat_q]
        flat_k = [q[:, :, :].rearrange("p h s -> p (h s)").bitcast(F32) for q in kst]
        hidT2 = [f[:, 0:HID].rearrange("p (k c) -> p k c", k=HID // P) for f in flat_k]
        result = [f[:, 512:512 + D] for f in flat_k]
        gates = [f[:, 768:768 + E] for f in flat_k]
        gate = [f[:, 776:777] for f in flat_k]
        moments = sb("moments", [P, TT, 6])
        stats = sb("stats", [P, TT, 2])
        rstd = sb("rstd", [P, TT])
        newton = sb("newton", [P, TT])
        vareps = sb("vareps", [P, TT])

        bank = [ctx.enter_context(nc.psum_tensor(f"bank{i}", [P, 512], F32)) for i in range(8)]
        bank16 = [b[:, :].bitcast(BF16) for b in bank]

        loaded = sem("loaded")
        x_first, x_rest = sem("x_first"), sem("x_rest")
        s_ones = sem("s_ones")
        s_tab = sem("s_tab")
        s_k2ps, s_k2f, s_k2t, s_k2st = sem("s_k2ps"), sem("s_k2f"), sem("s_k2t"), sem("s_k2st")
        s_zero, s_v2ps, s_v2 = sem("s_zero"), sem("s_v2ps"), sem("s_v2")
        s_v2st = [sem("s_v2st0"), sem("s_v2st1")]
        p_xn = sem("p_xn")
        p_xTps, p_xT = sem("p_xTps"), sem("p_xT")
        p_qk, p_v, p_sq = sem("p_qk"), sem("p_v"), sem("p_sq")
        p_sum, p_root = sem("p_sum"), sem("p_root")
        p_n, p_rot, p_terms = sem("p_n"), sem("p_rot"), sem("p_terms")
        p_vsb = sem("p_vsb")
        p_qTps, p_qT = sem("p_qTps"), sem("p_qT")
        p_store = [sem("p_store0"), sem("p_store1")]

        def attention_sems(tag):
            return {n: sem(f"{tag}_{n}") for n in (
                "sq", "max", "mterms", "mTps", "mT", "st", "exp", "av", "attn", "vpad")} | {
                "aug": [sem(f"{tag}_aug{i}") for i in range(2)],
                "stack": [[sem(f"{tag}_stack{i}{half}") for half in range(2)] for i in range(2)]}

        A = attention_sems("a")
        a_res = [sem("a_res0"), sem("a_res1")]
        a_resb, a_proj, a_x1, a_var, a_rstd, a_xn = (sem(n) for n in (
            "a_resb", "a_proj", "a_x1", "a_var", "a_rstd", "a_xn"))
        a_x1st = [sem("a_x1st0"), sem("a_x1st1")]
        a_xTps, a_xT, a_q2ps, a_q2f, a_q2t = (sem(n) for n in (
            "a_xTps", "a_xT", "a_q2ps", "a_q2f", "a_q2t"))
        a_q2st = [sem("a_q2st0"), sem("a_q2st1")]

        C = attention_sems("c")
        loaded2 = sem("loaded2")
        c_res = [sem("c_res0"), sem("c_res1")]
        c_v2 = [sem("c_v20"), sem("c_v21")]
        c_out = [sem("c_out0"), sem("c_out1")]
        c_moe = sem("c_moe")
        (c_resb, c_h, c_hT, c_y, c_x2, c_var, c_rstd, c_xn, c_xTps, c_xT, c_logit, c_lg, c_mask, c_gap, c_ed,
         c_rank, c_rk, c_pos, c_gates) = (sem("c_" + n) for n in (
             "resb", "h", "hT", "y", "x2", "var", "rstd", "xn", "xTps", "xT", "logit", "lg", "mask", "gap", "ed",
             "rank", "rk", "pos", "gates"))
        c_scatter = [sem("c_scatter0"), sem("c_scatter1")]
        m_filled, m_table, m_pad = sem("m_filled"), sem("m_table"), sem("m_pad")
        m_xs = [sem("m_xs0"), sem("m_xs1")]
        m_xTps, m_xT, m_h, m_silu, m_hid, m_hTps, m_hT, m_y, m_res, m_gate = (sem("m_" + n) for n in (
            "xTps", "xT", "h", "silu", "hid", "hTps", "hT", "y", "res", "gate"))
        m_added = sem("m_added")

        block = ctx.enter_context(nc.Block())

        weights = [("wqkv", wqkv), ("angles", angles), ("affine", affine), ("identf", identf[:]),
                   ("ident", ident[:]), ("ctxT", ctxT), ("wk", wk), ("wv", wv), ("wp", wp[:]), ("wq", wq[:]), ("bias_q", bias_q[:]),
                   ("bias_p", bias_p[:])]
        later = [("w1", w1[:]), ("w2", w2[:]), ("wg", wg[:]), ("below", below[:]), ("bias_2", bias_2[:]),
                 ("bias_1", bias_1[:]), ("ones", ones[:]), ("token_ids", token_ids[:]),
                 ("first_of", first_of[:]), ("region_at", region_at[:]), ("block_at", block_at[:]),
                 ("padding", padding[:])]

        def rsqrt_on_pool(pool, n=TT):
            for step in range(NEWTON):
                if step:
                    pool.drain()
                nc.gpsimd.tensor_tensor(newton[:], rstd[:], rstd[:], ALU.mult)
                pool.drain()
                nc.gpsimd.tensor_tensor(newton[:], newton[:], vareps[:], ALU.mult)
                pool.drain()
                nc.gpsimd.tensor_scalar(newton[:], newton[:], -0.5, 1.5, ALU.mult, ALU.add)
                pool.drain()
                last = nc.gpsimd.tensor_tensor(rstd[:], rstd[:], newton[:], ALU.mult)
            return last

        def moments_of(dve, src, eps):
            for tt in range(TT):
                nc.vector.bn_stats(moments[:, tt, :], src[:, tt, :])
            dve.drain()
            for tt in range(TT):
                nc.vector.bn_aggr(stats[:, tt, :], moments[:, tt, :])
            dve.drain()
            nc.vector.tensor_scalar(vareps[:], stats[:, :, 1], eps, None, ALU.add)
            dve.drain()
            return nc.vector.tensor_scalar(rstd[:].bitcast(I32), vareps[:].bitcast(I32), -0.5, MAGIC,
                                           ALU.mult, ALU.add)

        def norm_into(dst, src):
            for tt in range(TT):
                last = nc.vector.tensor_scalar(dst[:, tt, 0:D], src[:, tt, :], stats[:, tt, 0:1],
                                               rstd[:, tt:tt + 1], ALU.subtract, ALU.mult)
            return last


        def pe_score(pe, A, r, slot, keys, kstk):
            h = HEADS[slot]
            if slot % HALF == 0:
                pe.wait_ge(A["stack"][r.side][slot // HALF], r.turns(LOADS, LOADS))
            if slot == 0:
                wait(pe, A["mT"], r.count(1))
            wait(pe, A["max"], r.count(H, slot - 1))
            for qt in range(TT):
                last = nc.tensor.matmul(bank[slot % 2][:, qt * keys:(qt + 1) * keys],
                                        qst[r.side][0:ROWS, h, qt * P:(qt + 1) * P],
                                        kstk[r.side][0:ROWS, h, :], start=True, stop=True)
            last.then_inc(A["sq"], 1)

        def dve_max(dve, A, r, slot, keys):
            dve.wait_ge(A["sq"], r.count(H, slot + 1))
            if slot == 0:
                wait(dve, A["mterms"], r.count(1))
            nc.vector.tensor_reduce(maxes[:, HEADS[slot], :],
                                    bank[slot % 2][:, 0:TT * keys].rearrange("p (t k) -> p t k", t=TT),
                                    axis=X, op=ALU.max).then_inc(A["max"], 1)

        def dve_split_max(dve, A, r):
            dve.drain()
            wait(dve, A["mTps"], r.count(1))
            nc.vector.tensor_scalar(mrest[:], maxes[:, :, :].rearrange("p h t -> p t h"), -1.0, None, ALU.mult)
            for a in range(TERMS):
                dve.drain()
                last = nc.vector.tensor_copy(mterms[:, :, a, :], mrest[:])
                if a < TERMS - 1:
                    dve.drain()
                    nc.vector.tensor_tensor(mrest[:], mrest[:], mterms[:, :, a, :], ALU.subtract)
            last.then_inc(A["mterms"], 1)

        def pe_max_rows(pe, A, r):
            pe.wait_ge(A["mterms"], r.count(1, 1))
            for qt in range(TT):
                last = nc.tensor.transpose(bank16[0][:, qt * P:(qt + 1) * P],
                                           mterms[:, qt, :, :].rearrange("p a h -> p (a h)"), ident[:])
            last.then_inc(A["mTps"], 1)

        def act_max_rows(act, A, r):
            act.wait_ge(A["mTps"], r.count(1, 1))
            if not (r.pair is None and r.own == 0):
                act.wait_ge(A["aug"][1 - r.side], r.previous().turns(16 * TERMS, 16 * TERMS))
            nc.scalar.copy(mT[:], bank16[0][0:TERMS * H, 0:S]).then_inc(A["mT"], 1)

        def sp_max_rows(sp, A, r):
            sp.wait_ge(A["mT"], r.count(1, 1))
            for a in range(TERMS):
                sp.dma_start(qst[r.side][ROWS + a:ROWS + a + 1, :, :], mT[a * H:(a + 1) * H, :]
                             ).then_inc(A["aug"][r.side], 16)

        def store_parts(sp, dst, parts, stores, done):
            for group, part, n in stores:
                sp.dma_start(dst[group:group + n].rearrange("a (c p) s -> p a c s", p=P),
                             parts[:, part:part + n]).then_inc(done, 16)

        def load_half(sp, A, r, half, q_dram, k_dram, kstk):
            wait(sp, A["st"], r.count(H, (half + 1) * HALF - 2 * H))
            for stk, terms_dram, loads in ((qst, q_dram, Q_LOADS), (kstk, k_dram, K_LOADS)):
                for to, at, n in loads:
                    src = terms_dram[at:at + n].rearrange("a (d h) s -> (a d) h s", h=H)
                    sp.dma_start(stk[r.side][to * HD:(to + n) * HD, half * HALF:(half + 1) * HALF, :],
                                 src[:, half * HALF:(half + 1) * HALF, :]).then_inc(A["stack"][r.side][half], 16)

        def pe_exponents(pe, A, r, slots, keys, kstk):
            tiles, size = (keys + P - 1) // P, min(P, keys)
            for slot in slots:
                if slot == 0:
                    pe.wait_ge(A["aug"][r.side], r.turns(16 * TERMS, 16 * TERMS))
                wait(pe, A["exp"], r.count(H, slot - 1))
                for kt in range(tiles):
                    last = nc.tensor.matmul(bank[2 + slot % 2][0:size, kt * S:(kt + 1) * S],
                                            kstk[r.side][0:AUG, HEADS[slot], kt * P:kt * P + size],
                                            qst[r.side][0:AUG, HEADS[slot], :], start=True, stop=True)
                last.then_inc(A["st"], 1)

        def act_exp(act, A, r, slots, keys):
            tiles, size = (keys + P - 1) // P, min(P, keys)
            for slot in slots:
                g = slot // GROUP
                if slot % GROUP == 0:
                    wait(act, A["av"], r.count(GROUPS, g - 1))
                act.wait_ge(A["st"], r.count(H, slot + 1))
                nc.scalar.activation(probs[0:size, g % 2, slot % GROUP, 0:tiles * S],
                                     bank[2 + slot % 2][0:size, 0:tiles * S], ACT.Exp).then_inc(A["exp"], 1)

        def pe_values(pe, A, r, g, kind, keys, vp):
            tiles, size = (keys + P - 1) // P, min(P, keys)
            chunk, half = g // 2, g % 2
            if kind == 0:
                pe.wait_ge(A["exp"], r.count(H, (g + 1) * GROUP))
                if half == 0:
                    wait(pe, A["attn"], r.count(2, chunk - 1))
            for kt in range(tiles):
                for j in range(GROUP):
                    lhs = (vp[r.side][0:size, kt, HEADS[g * GROUP + j], :] if kind == 0
                           else onesrow[0:size, half, :])
                    last = nc.tensor.matmul(
                        bank[4 + chunk][32 * j:32 * j + 32, kind * S:(kind + 1) * S], lhs,
                        probs[0:size, g % 2, j, kt * S:(kt + 1) * S],
                        start=(kind == 0 and half == 0 and kt == 0),
                        stop=(half == 1 and kt == tiles - 1),
                        skip_group_check=True)
            if kind == 1:
                last.then_inc(A["av"], 1)

        def pe_round(pe, A, r, keys, kstk, vp, values_ready, early, late):
            for g in range(GROUPS):
                first = g * GROUP
                scores = list(SCORED[g]) if r.at(1) and r.at(0) else []
                values = (r.at(0), g - 1) if g else (r.at(-1), GROUPS - 1)
                if r.at(0):
                    pe_exponents(pe, A, r, (first, first + 1), keys, kstk)
                for slot in scores[0:2]:
                    pe_score(pe, A, r.at(1), slot, keys, kstk)
                if g == GROUPS - 1 and r.at(0) and r.at(1):
                    pe_max_rows(pe, A, r.at(1))
                early(r, g)
                if values[0]:
                    if values[1] == 0:
                        values_ready(values[0])
                    pe_values(pe, A, *values, 0, keys, vp)
                if r.at(0):
                    pe_exponents(pe, A, r, (first + 2, first + 3), keys, kstk)
                for slot in scores[2:]:
                    pe_score(pe, A, r.at(1), slot, keys, kstk)
                late(r, g)
                if values[0]:
                    pe_values(pe, A, *values, 1, keys, vp)

        def act_round(act, A, r, keys, late):
            for g in range(GROUPS):
                if r.at(0):
                    act_exp(act, A, r, range(g * GROUP, g * GROUP + 2), keys)
                    if g == GROUPS - 1 and r.at(1):
                        act_max_rows(act, A, r.at(1))
                    act_exp(act, A, r, range(g * GROUP + 2, (g + 1) * GROUP), keys)
                late(r, g)

        def dve_round(dve, A, r, keys, next_done, late):
            for g in range(GROUPS):
                if r.at(0) and r.at(1):
                    for slot in SCORED[g]:
                        dve_max(dve, A, r.at(1), slot, keys)
                    if g == GROUPS - 2:
                        dve_split_max(dve, A, r.at(1))
                if g == GROUPS - 1 and r.at(0):
                    dve_attn(dve, A, r, 0, next_done)
                late(r, g)
                if g == 0 and r.at(-1):
                    dve_attn(dve, A, r.at(-1), 1, next_done)

        def dve_attn(dve, A, r, chunk, next_done):
            dve.wait_ge(A["av"], r.count(GROUPS, 2 * chunk + 2))
            if chunk == 0:
                wait(dve, next_done, r.count(1))
            nc.vector.reciprocal(recip[:, chunk, :], bank[4 + chunk][:, S:])
            dve.drain()
            nc.vector.tensor_tensor(attnT[:, chunk, :], bank[4 + chunk][:, 0:S], recip[:, chunk, :], ALU.mult
                                    ).then_inc(A["attn"], 1)

        @block.sync
        def _(sp):
            for name, tile in weights[:6]:
                sp.dma_start(tile, t[name]).then_inc(loaded, 16)
            sp.dma_start(x_all[:, 0:2 * TT, :], t["x"][:, 0:2 * TT, :]).then_inc(x_first, 16)
            for name, tile in weights[6:]:
                sp.dma_start(tile, t[name]).then_inc(loaded, 16)
            sp.dma_start(x_all[:, 2 * TT:, :], t["x"][:, 2 * TT:, :]).then_inc(x_rest, 16)
            for name, tile in later:
                sp.dma_start(tile, t[name]).then_inc(loaded2, 16)

            for b in range(NB):
                sp.wait_ge(s_v2, b + 1)
                sp.dma_start(v2_dram[b], v2pad[b % 2][0:M, 0, :, :].rearrange("p h d -> p (h d)")
                             ).then_inc(s_v2st[b % 2], 16)
            sp.wait_ge(s_k2t, 1)
            for a in range(TERMS):
                for c in range(KC):
                    for group, part, n in K_STORES:
                        if part <= a < part + n:
                            sp.dma_start(k2_terms[:, group + a - part, c * P:(c + 1) * P, :].rearrange("b p m -> p b m"),
                                         k2parts[:, a, c, :, :]).then_inc(s_k2st, 16)

            def project(r):
                sp.wait_ge(p_qT, r.count(2 * TT, 2 * TT))
                for qk, stores in enumerate((Q_STORES, K_STORES)):
                    store_parts(sp, qk_terms[r.count(1)][qk], qkT[r.side][:, qk], stores, p_store[r.side])
            rounds(sp, project)

            sp.wait_ge(s_k2st, 16 * STORED * KC)

            def load(r, half):
                load_half(sp, A, r, half, qk_terms[r.count(1)][0], qk_terms[r.count(1)][1], kst)

            def residual(r):
                wait(sp, a_x1, r.count(1, -1))
                sp.dma_start(resid[r.side][:], t["x"][:, bass.ds(r.count(TT), TT), :]
                             ).then_inc(a_res[r.side], 16)

            def store_residual(r):
                sp.wait_ge(a_x1, r.count(1, 1))
                sp.dma_start(x1_dram[r.count(1)], x_new[r.side][:]).then_inc(a_x1st[r.side], 16)

            def store_queries(r):
                sp.wait_ge(a_q2t, r.count(1, 1))
                store_parts(sp, q2_terms[r.count(1)], q2T[r.side], Q_STORES, a_q2st[r.side])

            sp.wait_ge(p_store[0], STORES)
            load(Round(0), 0)
            load(Round(0), 1)
            for i in range(2):
                sp.wait_ge(p_store[i], STORES * NB // 2)
            load(Round(1), 0)
            sp_max_rows(sp, A, Round(0))

            def self_round(r):
                if r.at(0) and r.at(1):
                    load(r.at(1), 1)
                if r.at(0):
                    residual(r)
                if r.at(-1):
                    store_residual(r.at(-1))
                if r.at(0) and r.at(2):
                    load(r.at(2), 0)
                if r.at(0) and r.at(1):
                    sp_max_rows(sp, A, r.at(1))
                if r.at(-2):
                    store_queries(r.at(-2))
            rounds(sp, self_round, after=2)

            for i in range(2):
                sp.wait_ge(s_v2st[i], 16 * NB // 2)
                sp.wait_ge(a_x1st[i], 16 * NB // 2)
                sp.wait_ge(a_q2st[i], 16 * len(Q_STORES) * NB // 2)
            sp.wait_ge(A["av"], GROUPS * NB)
            sp.wait_ge(a_xTps, NB)

            def load(r, half):
                load_half(sp, C, r, half, q2_terms[r.count(1)], k2_terms[r.count(1)], k2st)

            def load_values2(r):
                wait(sp, C["av"], r.count(GROUPS, -GROUPS))
                sp.dma_start(v2pad[r.side][0:M, 0, :, :].rearrange("p h d -> p (h d)"), v2_dram[r.count(1)]
                             ).then_inc(c_v2[r.side], 16)
                wait(sp, c_x2, r.count(1, -1))
                sp.dma_start(resid[r.side][:], x1_dram[r.count(1)]).then_inc(c_res[r.side], 16)

            def store_out(r):
                sp.wait_ge(c_x2, r.count(1, 1))
                sp.dma_start(out[bass.ds(r.count(S), S), :].rearrange("(t p) c -> p t c", p=P),
                             x_new[r.side][:]).then_inc(c_out[r.side], 16)

            load(Round(0), 0)
            load(Round(0), 1)
            load(Round(1), 0)
            sp_max_rows(sp, C, Round(0))

            def cross_round(r):
                if r.at(0) and r.at(1):
                    load(r.at(1), 1)
                if r.at(0):
                    load_values2(r)
                    sp.dma_start(moe[:, bass.ds(r.count(1), 1), :], t["moe"][:, bass.ds(r.count(1), 1), :]
                                 ).then_inc(c_moe, 16)
                if r.at(-2):
                    store_out(r.at(-2))
                if r.at(0) and r.at(2):
                    load(r.at(2), 0)
                if r.at(0) and r.at(1):
                    sp_max_rows(sp, C, r.at(1))
            rounds(sp, cross_round, after=2)

            sp.dma_start(routed[SPARE:SPARE + P, :], padding[:]).then_inc(m_pad, 16)
            sp.wait_ge(m_filled, 1)
            for e in range(E):
                at = sp.value_load(filled_i[0:1, e:e + 1], min_val=e * REGION, max_val=e * REGION + TOKENS)
                sp.dma_start(routed[bass.ds(at, P), :], padding[:]).then_inc(m_pad, 16)
            sp.wait_ge(m_pad, 16 * (E + 1))
            for i in range(2):
                sp.wait_ge(c_scatter[i], 16 * 2 * TT * NB // 2)
            sp.wait_ge(m_table, 1)

            def block_rows(r):
                at = sp.value_load(block_i[0:1, 0, bass.ds(r.count(1), 1)], min_val=0, max_val=SPARE)
                wait(sp, m_gate, r.count(1, -1))
                wait(sp, m_xTps, r.count(1, -1))
                sp.dma_start(xs[r.side], routed[bass.ds(at, P), :]).then_inc(m_xs[r.side], 16)
            blocks(sp, block_rows)

        @block.gpsimd
        def _(pool):
            for tile in (vpad[0], vpad[1], v2pad[0][:], v2pad[1][:], onesrow[:], mterms[:]):
                last = nc.gpsimd.memset(tile, 0.0)
            last.then_inc(s_zero, 1)
            pool.wait_ge(s_zero, 1)
            for half in range(2):
                nc.gpsimd.memset(onesrow[:, half, half * HD:(half + 1) * HD], 1.0)
            for stk in kst + k2st:
                pool.drain()
                last = nc.gpsimd.memset(stk[ROWS:AUG, :, :], 1.0)
            last.then_inc(s_ones, 1)

            pool.drain()
            pool.wait_ge(s_k2f, 4)
            flat = k2parts.rearrange("p a c b m -> p a (c b m)")
            for a in range(TERMS):
                last = nc.gpsimd.tensor_copy(flat[:, a, :], k2f)
                if a < TERMS - 1:
                    pool.drain()
                    nc.gpsimd.tensor_tensor(k2f, k2f, flat[:, a, :], ALU.subtract)
                    pool.drain()
            last.then_inc(s_k2t, 1)

            pool.wait_ge(s_tab, 1)

            def rotate(r):
                wait(pool, p_terms, r.count(1))
                for tt in range(TT):
                    pool.wait_ge(p_n, r.count(TT, tt + 1))
                    src = normed[:, tt, :].rearrange("p (q d h) -> p q d h", q=2, h=H)
                    dst = rotated[:, tt, :].rearrange("p (q d h) -> p q d h", q=2, h=H)
                    for lo, hi in ((0, HD // 2), (HD // 2, 0)):
                        turn = tables[:, 1, tt, :, lo:lo + HD // 2].unsqueeze(3).broadcast_to([P, 2, HD // 2, H])
                        nc.gpsimd.tensor_tensor(dst[:, :, lo:lo + HD // 2, :], src[:, :, hi:hi + HD // 2, :],
                                                turn, ALU.mult)
                    pool.drain()
                    shift = tables[:, 2, tt, :, :].unsqueeze(3).broadcast_to([P, 2, HD, H])
                    nc.gpsimd.tensor_tensor(dst, dst, shift, ALU.add).then_inc(p_rot, 1)
            rounds(pool, rotate)

            def spread_values(r):
                pool.wait_ge(p_vsb, r.count(1, 1))
                wait(pool, A["av"], r.count(GROUPS, -GROUPS))
                src = values[:, bass.ds(r.count(TT), TT), :].rearrange("p t (h two d) -> p t h two d", two=2, d=HD)
                dst = vpad[r.side].rearrange("p t (h two) d -> p t h two d", two=2)
                for half in range(2):
                    last = nc.gpsimd.tensor_copy(dst[:, :, :, half, half * HD:(half + 1) * HD],
                                                 src[:, :, :, half, :])
                last.then_inc(A["vpad"], 1)

            def self_round(r):
                if r.at(0) and r.at(1):
                    spread_values(r.at(1))
                if r.at(0):
                    pool.wait_ge(a_res[r.side], r.turns(16, 16))
                    nc.gpsimd.tensor_tensor(resid[r.side][:], resid[r.side][:],
                                            bias_p[:, :].unsqueeze(1).broadcast_to([P, TT, D]),
                                            ALU.add).then_inc(a_resb, 1)
                if r.at(-1):
                    pool.wait_ge(a_var, r.at(-1).count(1, 1))
                    rsqrt_on_pool(pool).then_inc(a_rstd, 1)
            spread_values(Round(0))
            rounds(pool, self_round, after=1)

            pool.wait_ge(loaded2, 16 * len(later))

            def send(r):
                pool.wait_ge(c_pos, r.count(1, 1))
                pool.wait_ge(c_xn, r.count(1, 1))
                nc.gpsimd.tensor_tensor(rows3[r.side][:, :, D + 1:], pick[0][:], pick[1][:],
                                        ALU.add).then_inc(c_gates, 1)
                pool.drain()
                for tt in range(TT):
                    for i in range(2):
                        at = tt * 2 + i
                        nc.gpsimd.indirect_dma_start(
                            out=routed, in_=rows3[r.side][:, tt, :], in_offset=None,
                            out_offset=bass.IndirectOffsetOnAxis(ap=pos[r.side][:, at:at + 1], axis=0),
                        ).then_inc(c_scatter[r.side], 16)

            def cross_round(r):
                if r.at(0):
                    pool.wait_ge(c_res[r.side], r.turns(16, 16))
                    nc.gpsimd.tensor_tensor(resid[r.side][:], resid[r.side][:],
                                            bias_2[:, :].unsqueeze(1).broadcast_to([P, TT, D]),
                                            ALU.add).then_inc(c_resb, 1)
                if r.at(-1):
                    pool.wait_ge(c_var, r.at(-1).count(1, 1))
                    rsqrt_on_pool(pool).then_inc(c_rstd, 1)
                if r.at(-2):
                    send(r.at(-2))
            rounds(pool, cross_round, after=2)

            for i in range(2):
                pool.wait_ge(c_out[i], 16 * NB // 2)

            def add_rows(r):
                wait(pool, m_added, r.count(16))
                pool.wait_ge(m_res, r.count(1, 1))
                nc.gpsimd.tensor_tensor(tokens[:], tokens_of[:, bass.ds(r.count(1), 1)],
                                        onesrow[:, 0, HD:HD + 1].bitcast(I32), ALU.add)
                pool.drain()
                nc.gpsimd.indirect_dma_start(
                    out=out, in_=result[r.side], in_offset=None,
                    out_offset=bass.IndirectOffsetOnAxis(ap=tokens[:], axis=0),
                    bounds_check=TOKENS - 1, oob_is_err=False, compute_op=ALU.add).then_inc(m_added, 16)
            blocks(pool, add_rows)
            pool.wait_ge(m_added, 16 * BLOCKS)

        @block.scalar
        def _(act):
            for i in range(4):
                act.wait_ge(s_k2ps, i + 1)
                nc.scalar.copy(k2f[:, i * (NB * M // 2):(i + 1) * (NB * M // 2)],
                               bank[(5, 7)[i % 2]][:, 0:NB * M // 2]).then_inc(s_k2f, 1)
            act.wait_ge(s_ones, 1)
            for b in range(NB):
                act.wait_ge(s_v2ps, b + 1)
                if b >= 2:
                    act.wait_ge(s_v2st[b % 2], 16 * (b // 2))
                src = bank[(5, 7)[b % 2]][0:M, 0:D].rearrange("p (h two d) -> p h two d", two=2, d=HD)
                dst = v2pad[b % 2][0:M, 0, :, :].rearrange("p (h two) d -> p h two d", two=2)
                for half in range(2):
                    last = nc.scalar.copy(dst[:, :, half, half * HD:(half + 1) * HD], src[:, :, half, :])
                last.then_inc(s_v2, 1)

            def evacuate_xT(r):
                act.wait_ge(p_xTps, r.count(1, 1))
                wait(act, p_v, r.count(1, -1))
                nc.scalar.copy(xnT[r.side], bank[6][:, :].rearrange("p (k s) -> p k s", k=KC)).then_inc(p_xT, 1)

            act.wait_ge(p_sum, 1)
            nc.scalar.activation(spread[:, TT * 2 * H:], spread[:, TT * 2 * H:], ACT.Sqrt).then_inc(p_root, 1)
            evacuate_xT(Round(0))

            def project(r):
                wait(act, p_sum, r.count(1, 1))
                for tt in range(TT):
                    act.wait_ge(p_qk, r.count(TT, tt + 1))
                    nc.scalar.activation(square[:, tt, :], bank[tt][:, :], ACT.Square).then_inc(p_sq, 1)
                act.wait_ge(p_v, r.count(1, 1))
                nc.scalar.copy(values[:, bass.ds(r.count(TT), TT), :],
                               bank[4][:, :].rearrange("p (t c) -> p t c", t=TT)).then_inc(p_vsb, 1)
                act.wait_ge(p_sum, r.count(1, 2))
                n = TT * 2 * H + (0 if r.last else TT)
                nc.scalar.activation(spread[:, 0:n], spread[:, 0:n], ACT.Sqrt).then_inc(p_root, 1)
                if not r.last:
                    evacuate_xT(r.next())
                wait(act, p_store[r.side], r.turns(STORES))
                for tt in range(TT):
                    for qk in range(2):
                        i = 2 * tt + qk
                        act.wait_ge(p_qTps, r.count(2 * TT, i + 1))
                        nc.scalar.copy(
                            qkT[r.side][:, qk, :, :, tt * P:(tt + 1) * P],
                            bank16[2 + i % 2][:, 0:TERMS * KC * P].rearrange("p (a c s) -> p a c s", a=TERMS, s=P)
                        ).then_inc(p_qT, 1)
            rounds(act, project)

            def late(r, g):
                if g == 0 and r.at(-2):
                    r = r.at(-2)
                    act.wait_ge(a_q2ps, r.count(1, 1))
                    wait(act, a_q2t, r.count(1))
                    for c in range(KC):
                        last = nc.scalar.activation(q2f[:, c, :], bank[6][:, c * S:(c + 1) * S], ACT.Identity,
                                                    bias=bias_q[:, c:c + 1], scale=HD ** -0.5)
                    last.then_inc(a_q2f, 1)
                if g == 3 and r.at(-1):
                    r = r.at(-1)
                    act.wait_ge(a_xTps, r.count(1, 1))
                    wait(act, a_q2ps, r.count(1))
                    nc.scalar.copy(xn2T[:], bank[7][:, :].rearrange("p (k s) -> p k s", k=KC)).then_inc(a_xT, 1)

            act_max_rows(act, A, Round(0))
            rounds(act, lambda r: act_round(act, A, r, S, late), after=2)

            def late(r, g):
                if g == 0 and r.at(-2):
                    r = r.at(-2)
                    act.wait_ge(c_xTps, r.count(1, 1))
                    wait(act, c_logit, r.count(1))
                    nc.scalar.copy(xn2T[:], bank[7][:, :].rearrange("p (k s) -> p k s", k=KC)).then_inc(c_xT, 1)
                if g == 1 and r.at(-1):
                    r = r.at(-1)
                    act.wait_ge(c_h, r.count(1, 1))
                    wait(act, c_y, r.count(1))
                    for c in range(HID // P):
                        last = nc.scalar.activation(hidT[:, c, :], bank[6 + c // 2][:, (c % 2) * S:(c % 2 + 1) * S],
                                                    ACT.Relu, bias=bias_1[:, c:c + 1])
                    last.then_inc(c_hT, 1)
                if g == 2 and r.at(-2):
                    act.wait_ge(c_gap, r.at(-2).count(1, 1))
                    nc.scalar.activation(share[1][:], gap[:], ACT.Exp).then_inc(c_ed, 1)

            act.wait_ge(loaded2, 16 * len(later))
            act.wait_ge(a_q2t, NB)
            act_max_rows(act, C, Round(0))
            rounds(act, lambda r: act_round(act, C, r, M, late), after=2)

            def rows_in(r):
                act.wait_ge(m_xTps, r.count(1, 1))
                wait(act, m_h, r.count(2, -2))
                nc.scalar.copy(xsT[r.side], bank[0][:, 0:D].rearrange("p (k c) -> p k c", k=KC)).then_inc(m_xT, 1)

            def silu(r):
                act.wait_ge(m_h, r.count(2, 1))
                wait(act, m_hid, r.count(1, -1))
                nc.scalar.activation(act1[r.side], bank[2 + 2 * r.side][:, :], ACT.Silu).then_inc(m_silu, 1)

            def hidden(r):
                act.wait_ge(m_hTps, r.count(1, 1))
                wait(act, m_y, r.count(1, -1))
                nc.scalar.copy(hidT2[r.side], bank[1][:, :].rearrange("p (k c) -> p k c", k=HID // P)
                               ).then_inc(m_hT, 1)

            rows_in(Round(0))
            rows_in(Round(1))
            silu(Round(0))

            def expert_block(r):
                if not r.final:
                    silu(r.next())
                hidden(r)
                if not r.last_two:
                    rows_in(r.next().next())
            blocks(act, expert_block, last=True)

        @block.vector
        def _(dve):
            dve.wait_ge(loaded, 16 * len(weights))
            for k in range(KC):
                nc.vector.tensor_reduce(wmean[:, k, :].rearrange("p (q h) -> p q h", q=2),
                                        wqkv[:, k, 0:2 * D].rearrange("p (q d h) -> p q h d", q=2, h=H),
                                        axis=X, op=ALU.add)
            dve.drain()
            nc.vector.tensor_scalar(wmean, wmean, 1.0 / HD, None, ALU.mult)
            dve.drain()
            for k in range(KC):
                w = wqkv[:, k, 0:2 * D].rearrange("p (q d h) -> p q d h", q=2, h=H)
                mean = wmean[:, k, :].rearrange("p (q h) -> p q h", q=2).unsqueeze(2).broadcast_to([P, 2, HD, H])
                last = nc.vector.tensor_tensor(w, w, mean, ALU.subtract)
            last.then_inc(s_tab, 1)
            dve.drain()
            for tt in range(TT):
                cos = angles[:, 0, tt, :].unsqueeze(1).broadcast_to([P, 2, HD])
                sin = angles[:, 1, tt, :].unsqueeze(1).broadcast_to([P, 2, HD])
                nc.vector.tensor_tensor(tables[:, 0, tt, :, :], affine[:, 0, :, :], cos, ALU.mult)
                nc.vector.tensor_tensor(tables[:, 1, tt, :, :], affine[:, 1, :, :], sin, ALU.mult)
                nc.vector.tensor_tensor(tables[:, 2, tt, :, :], affine[:, 2, :, :], cos, ALU.mult)
                nc.vector.tensor_tensor(wmean[:, tt, :].rearrange("p (q d) -> p q d", q=2), affine[:, 3, :, :],
                                        sin, ALU.mult)
            dve.drain()
            for tt in range(TT):
                nc.vector.tensor_tensor(tables[:, 2, tt, :, :], tables[:, 2, tt, :, :],
                                        wmean[:, tt, :].rearrange("p (q d) -> p q d", q=2), ALU.add)
            dve.drain()
            for a in range(3):
                last = nc.vector.tensor_scalar(tables[:, a, :, 0, :], tables[:, a, :, 0, :], HD ** -0.5, None,
                                               ALU.mult)
            last.then_inc(s_tab, 1)

            def row_variance(r):
                if r.pair is None and r.own == 0:
                    dve.wait_ge(x_first, 16)
                if r.own == 2:
                    dve.wait_ge(x_rest, 16)
                rows = x_all[:, bass.ds(r.count(TT), TT), :]
                for tt in range(TT):
                    nc.vector.bn_stats(moments[:, tt, :], rows[:, tt, :])
                dve.drain()
                for tt in range(TT):
                    nc.vector.bn_aggr(stats[:, tt, :], moments[:, tt, :])
                dve.drain()
                return nc.vector.tensor_scalar(spread[:, TT * 2 * H:], stats[:, :, 1], 1e-5, None, ALU.add)

            def norm_rows(r):
                rows = x_all[:, bass.ds(r.count(TT), TT), :]
                wait(dve, p_xTps, r.count(1, -1))
                for tt in range(TT):
                    at = TT * 2 * H + tt
                    last = nc.vector.tensor_scalar(xn[r.side][:, tt, :], rows[:, tt, :], stats[:, tt, 0:1],
                                                   spread[:, at:at + 1], ALU.subtract, ALU.mult)
                last.then_inc(p_xn, 1)

            row_variance(Round(0)).then_inc(p_sum, 1)
            dve.wait_ge(p_root, 1)
            nc.vector.reciprocal(spread[:, TT * 2 * H:], spread[:, TT * 2 * H:])
            dve.drain()
            norm_rows(Round(0))

            def project(r):
                if not r.last:
                    dve.drain()
                    row_variance(r.next())
                for tt in range(TT):
                    dve.wait_ge(p_sq, r.count(TT, tt + 1))
                    nc.vector.tensor_reduce(spread[:, tt * 2 * H:(tt + 1) * 2 * H].rearrange("p (q h) -> p q h", q=2),
                                            square[:, tt, :].rearrange("p (q d h) -> p q h d", q=2, h=H),
                                            axis=X, op=ALU.add)
                dve.drain()
                heads = spread[:, 0:TT * 2 * H]
                nc.vector.tensor_scalar(heads, heads, 1.0 / HD, 1e-6, ALU.mult, ALU.add).then_inc(p_sum, 1)
                dve.wait_ge(p_root, r.count(1, 2))
                n = TT * 2 * H + (0 if r.last else TT)
                nc.vector.reciprocal(spread[:, 0:n], spread[:, 0:n])
                dve.drain()
                if not r.last:
                    norm_rows(r.next())
                for tt in range(TT):
                    inverse = spread[:, tt * 2 * H:(tt + 1) * 2 * H].rearrange("p (q h) -> p q h", q=2)
                    nc.vector.tensor_tensor(normed[:, tt, :].rearrange("p (q d h) -> p q d h", q=2, h=H),
                                            bank[tt][:, :].rearrange("p (q d h) -> p q d h", q=2, h=H),
                                            inverse.unsqueeze(2).broadcast_to([P, 2, HD, H]), ALU.mult
                                            ).then_inc(p_n, 1)
                dve.drain()
                for tt in range(TT):
                    nc.vector.tensor_tensor(
                        direct[:, tt, :].rearrange("p (q d h) -> p q d h", q=2, h=H),
                        normed[:, tt, :].rearrange("p (q d h) -> p q d h", q=2, h=H),
                        tables[:, 0, tt, :, :].unsqueeze(3).broadcast_to([P, 2, HD, H]), ALU.mult)
                dve.drain()
                dve.wait_ge(p_rot, r.count(TT, TT))
                nc.vector.tensor_tensor(direct, direct, rotated, ALU.add)
                dve.drain()
                wait(dve, p_qTps, r.count(2 * TT, -2 * TT))
                for a in range(TERMS - 1):
                    if a:
                        dve.drain()
                    nc.vector.tensor_copy(terms[r.side][:, :, a, :], direct)
                    dve.drain()
                    last = nc.vector.tensor_tensor(direct if a == 0 else terms[r.side][:, :, 2, :], direct,
                                                   terms[r.side][:, :, a, :], ALU.subtract)
                last.then_inc(p_terms, 1)
            rounds(dve, project)

            def split_queries(r):
                dve.wait_ge(a_q2f, r.count(1, 1))
                wait(dve, a_q2st[r.side], r.turns(16 * len(Q_STORES)))
                parts = q2T[r.side]
                nc.vector.tensor_copy(parts[:, 0, :, :], q2f)
                dve.drain()
                nc.vector.tensor_tensor(q2rest, q2f, parts[:, 0, :, :], ALU.subtract)
                dve.drain()
                nc.vector.tensor_copy(parts[:, 1, :, :], q2rest)
                dve.drain()
                nc.vector.tensor_tensor(parts[:, 2, :, :], q2rest, parts[:, 1, :, :],
                                        ALU.subtract).then_inc(a_q2t, 1)

            for slot in range(H):
                dve_max(dve, A, Round(0), slot, S)
            dve_split_max(dve, A, Round(0))
            nc.vector.tensor_scalar(bias_q[:], bias_q[:], HD ** -0.5, None, ALU.mult)

            def late(r, g):
                if g == 1 and r.at(-1):
                    r = r.at(-1)
                    dve.wait_ge(a_proj, r.count(1, 1))
                    dve.wait_ge(a_resb, r.count(1, 1))
                    wait(dve, a_x1st[r.side], r.turns(16))
                    nc.vector.tensor_tensor(x_new[r.side][:], bank[6][:, :].rearrange("p (t c) -> p t c", t=TT),
                                            resid[r.side][:], ALU.add).then_inc(a_x1, 1)
                    dve.drain()
                    moments_of(dve, x_new[r.side], 1e-5).then_inc(a_var, 1)
                elif g == 2:
                    if r.at(-1):
                        dve.wait_ge(a_rstd, r.at(-1).count(1, 1))
                        wait(dve, a_xTps, r.at(-1).count(1))
                        norm_into(xn2, x_new[r.at(-1).side]).then_inc(a_xn, 1)
                    if r.at(-2):
                        split_queries(r.at(-2))
            rounds(dve, lambda r: dve_round(dve, A, r, S, a_proj, late), after=2)

            def choose(r):
                wait(dve, c_gates, r.count(1))
                dve.wait_ge(c_logit, r.count(1, 1))
                nc.vector.tensor_copy(logits[:], bank[6][:, 0:TT * E].rearrange("p (t e) -> p t e", t=TT)
                                      ).then_inc(c_lg, 1)
                for i in range(2):
                    dve.drain()
                    nc.vector.tensor_reduce(best[i][:], logits[:], axis=X, op=ALU.max)
                    dve.drain()
                    nc.vector.tensor_tensor(key[:], logits[:], best[i][:, :].unsqueeze(2).broadcast_to([P, TT, E]),
                                            ALU.is_ge)
                    dve.drain()
                    nc.vector.tensor_tensor(key[:], key[:], first_of[:, :].unsqueeze(1).broadcast_to([P, TT, E]),
                                            ALU.mult)
                    dve.drain()
                    nc.vector.tensor_reduce(top[:], key[:], axis=X, op=ALU.max)
                    dve.drain()
                    nc.vector.tensor_tensor(pick[i][:], key[:], top[:, :].unsqueeze(2).broadcast_to([P, TT, E]),
                                            ALU.is_equal)
                    dve.drain()
                    if i == 0:
                        nc.vector.scalar_tensor_tensor(logits[:], pick[0][:], LOW, logits[:], ALU.mult, ALU.add)
                nc.vector.tensor_tensor(gap[:], best[1][:], best[0][:], ALU.subtract).then_inc(c_gap, 1)
                nc.vector.tensor_tensor(chosen[:], pick[0][:], pick[1][:], ALU.add).then_inc(c_mask, 1)

            def place(r):
                dve.wait_ge(c_ed, r.count(1, 1))
                nc.vector.tensor_scalar(share[0][:], share[1][:], 1.0, None, ALU.add)
                dve.drain()
                nc.vector.reciprocal(share[0][:], share[0][:])
                dve.drain()
                nc.vector.tensor_tensor(share[1][:], share[1][:], share[0][:], ALU.mult)
                dve.wait_ge(c_rank, r.count(1, 1))
                counted = bank[7][:, 0:(TT + 1) * E].rearrange("p (t e) -> p t e", e=E)
                nc.vector.tensor_tensor(ranks[:], counted[:, 0:TT, :],
                                        filled[:, :].unsqueeze(1).broadcast_to([P, TT, E]), ALU.add)
                dve.drain()
                nc.vector.tensor_tensor(filled[:], filled[:], counted[:, TT, :], ALU.add).then_inc(c_rk, 1)
                rows = rows3[r.side]
                nc.vector.tensor_copy(rows[:, :, D:D + 1].bitcast(I32),
                                      token_ids[:, bass.ds(r.count(TT), TT)].unsqueeze(2))
                for i in range(2):
                    nc.vector.tensor_tensor(taken[i][:], pick[i][:], ranks[:], ALU.mult)
                dve.drain()
                for i in range(2):
                    nc.vector.tensor_reduce(posf[:, :, i], taken[i][:], axis=X, op=ALU.add)
                    nc.vector.tensor_tensor(pick[i][:], pick[i][:],
                                            share[i][:, :].unsqueeze(2).broadcast_to([P, TT, E]), ALU.mult)
                dve.drain()
                nc.vector.tensor_copy(pos[r.side][:, :].rearrange("p (t i) -> p t i", t=TT), posf[:]
                                      ).then_inc(c_pos, 1)

            dve.wait_ge(loaded2, 16 * len(later))
            nc.vector.tensor_copy(filled[:], region_at[:])
            for slot in range(H):
                dve_max(dve, C, Round(0), slot, M)
            dve_split_max(dve, C, Round(0))

            def late(r, g):
                if g == 0 and r.at(-2):
                    r = r.at(-2)
                    dve.wait_ge(c_rstd, r.count(1, 1))
                    wait(dve, c_scatter[r.side], r.turns(16 * 2 * TT))
                    norm_into(rows3[r.side], x_new[r.side]).then_inc(c_xn, 1)
                if g == 1 and r.at(-2):
                    choose(r.at(-2))
                if g == 3:
                    if r.at(-1):
                        before = r.at(-1)
                        dve.wait_ge(c_y, before.count(1, 1))
                        dve.wait_ge(c_resb, before.count(1, 1))
                        wait(dve, c_out[before.side], before.turns(16))
                        nc.vector.tensor_tensor(x_new[before.side][:],
                                                bank[6][:, :].rearrange("p (t c) -> p t c", t=TT),
                                                resid[before.side][:], ALU.add).then_inc(c_x2, 1)
                        dve.drain()
                        moments_of(dve, x_new[before.side], 1e-5).then_inc(c_var, 1)
                    if r.at(-2):
                        place(r.at(-2))
            rounds(dve, lambda r: dve_round(dve, C, r, M, c_h, late), after=2)

            dve.drain()
            nc.vector.tensor_copy(filled_i[:], filled[:]).then_inc(m_filled, 1)
            nc.vector.tensor_tensor(step_f[:], filled[:], region_at[:], ALU.subtract)
            dve.drain()
            nc.vector.tensor_scalar(count_i[:], step_f[:], float(P - 1), None, ALU.add)
            dve.drain()
            nc.vector.tensor_scalar(count_i[:], count_i[:], 7, None, ALU.arith_shift_right)
            dve.drain()
            nc.vector.tensor_copy(ends_f[:], count_i[:])
            for e in range(1, E):
                dve.drain()
                nc.vector.tensor_tensor(ends_f[:, e:e + 1], ends_f[:, e:e + 1], ends_f[:, e - 1:e], ALU.add)
            dve.drain()
            nc.vector.memset(past[:, :, 0:1], 1.0)
            nc.vector.tensor_tensor(past[:, :, 1:], block_at[:, :].unsqueeze(2).broadcast_to([P, BLOCKS, E]),
                                    ends_f[:, :].unsqueeze(1).broadcast_to([P, BLOCKS, E]), ALU.is_ge)
            nc.vector.tensor_copy(step_f[:], region_at[:])
            dve.drain()
            nc.vector.scalar_tensor_tensor(step_f[:, 1:], ends_f[:, 0:E - 1], -float(P), step_f[:, 1:],
                                           ALU.mult, ALU.add)
            nc.vector.tensor_tensor(of_block, past[:, :, 0:E], past[:, :, 1:], ALU.subtract)
            dve.drain()
            nc.vector.tensor_tensor(scaled, of_block, step_f[:, :].unsqueeze(1).broadcast_to([P, BLOCKS, E]),
                                    ALU.mult)
            nc.vector.tensor_reduce(block_f[:, 1, :], past[:, :, 1:], axis=X, op=ALU.add)
            dve.drain()
            nc.vector.tensor_reduce(block_f[:, 0, :], scaled, axis=X, op=ALU.add)
            nc.vector.tensor_scalar(block_f[:, 1, :], block_f[:, 1, :], float(E - 1), None, ALU.min)
            dve.drain()
            nc.vector.scalar_tensor_tensor(block_f[:, 0, :], block_at[:], float(P), block_f[:, 0, :],
                                           ALU.mult, ALU.add)
            dve.drain()
            nc.vector.tensor_scalar(scaled[:, :, 0], block_f[:, 0, :], -1.0, float(SPARE), ALU.mult, ALU.add)
            dve.drain()
            nc.vector.tensor_tensor(scaled[:, :, 0], scaled[:, :, 0], past[:, :, E], ALU.mult)
            dve.drain()
            nc.vector.tensor_tensor(block_f[:, 0, :], block_f[:, 0, :], scaled[:, :, 0], ALU.add)
            dve.drain()
            nc.vector.tensor_copy(block_i, block_f[:]).then_inc(m_table, 1)

            def read_columns(r):
                dve.wait_ge(m_xs[r.side], r.turns(16, 16))
                nc.vector.tensor_tensor(gates[r.side], xs[r.side][:, D + 1:],
                                        of_block[:, bass.ds(r.count(1), 1), :].rearrange("p o e -> p (o e)"),
                                        ALU.mult)
                dve.drain()
                nc.vector.tensor_copy(tokens_of[:, bass.ds(r.count(1), 1)], xs[r.side][:, D:D + 1].bitcast(I32))
                nc.vector.tensor_reduce(gate[r.side], gates[r.side], axis=X, op=ALU.add).then_inc(m_gate, 1)

            def multiply(r):
                dve.wait_ge(m_silu, r.count(1, 1))
                dve.wait_ge(m_h, r.count(2, 2))
                wait(dve, m_hTps, r.count(1, -1))
                nc.vector.scalar_tensor_tensor(hid[r.side], act1[r.side], gate[r.side], bank[3 + 2 * r.side][:, :],
                                               ALU.mult, ALU.mult).then_inc(m_hid, 1)

            def take_result(r):
                dve.wait_ge(m_y, r.count(1, 1))
                wait(dve, m_added, r.count(16, -16))
                nc.vector.tensor_copy(result[r.side], bank[6 + r.side][:, 0:D]).then_inc(m_res, 1)

            read_columns(Round(0))
            read_columns(Round(1))
            dve.drain()
            multiply(Round(0))

            def expert_block(r):
                if not r.final:
                    multiply(r.next())
                if not r.last_two:
                    read_columns(r.next().next())
                if not r.first:
                    take_result(r.previous())
                dve.drain()
            blocks(dve, expert_block, last=True)
            take_result(Round(BLOCKS - 1))

        @block.tensor
        def _(pe):
            pe.wait_ge(loaded, 16 * len(weights))
            for i in range(4):
                c, half = i // 2, i % 2
                if i >= 2:
                    pe.wait_ge(s_k2f, i - 1)
                for k in range(KC):
                    last = nc.tensor.matmul(bank[(5, 7)[i % 2]][:, 0:NB * M // 2], wk[:, k, c * P:(c + 1) * P],
                                            ctxT[:, k, half * (NB * M // 2):(half + 1) * (NB * M // 2)],
                                            start=(k == 0), stop=(k == KC - 1))
                last.then_inc(s_k2ps, 1)
            pe.wait_ge(s_k2f, 4)
            for b in range(NB):
                if b >= 2:
                    pe.wait_ge(s_v2, b - 1)
                for k in range(KC):
                    last = nc.tensor.matmul(bank[(5, 7)[b % 2]][0:M, 0:D], ctxT[:, k, b * M:(b + 1) * M],
                                            wv[:, k, :], start=(k == 0), stop=(k == KC - 1))
                last.then_inc(s_v2ps, 1)

            def rows_in(r):
                pe.wait_ge(p_xn, r.count(1, 1))
                wait(pe, p_xT, r.count(1))
                for tt in range(TT):
                    for k in range(KC):
                        last = nc.tensor.transpose(bank[6][:, k * S + tt * P:k * S + (tt + 1) * P],
                                                   xn[r.side][:, tt, k * P:(k + 1) * P], identf[:])
                last.then_inc(p_xTps, 1)
                pe.wait_ge(p_xT, r.count(1, 1))
                for tt in range(TT):
                    wait(pe, p_n, r.count(TT, tt - 1))
                    for k in range(KC):
                        last = nc.tensor.matmul(bank[tt][:, :], xnT[r.side][:, k, tt * P:(tt + 1) * P],
                                                wqkv[:, k, 0:2 * D], start=(k == 0), stop=(k == KC - 1))
                    last.then_inc(p_qk, 1)
                wait(pe, p_vsb, r.count(1))
                for tt in range(TT):
                    for k in range(KC):
                        last = nc.tensor.matmul(bank[4][:, tt * D:(tt + 1) * D], xnT[r.side][:, k, tt * P:(tt + 1) * P],
                                                wqkv[:, k, 2 * D:3 * D], start=(k == 0), stop=(k == KC - 1))
                last.then_inc(p_v, 1)

            pe.wait_ge(s_tab, 1)
            rows_in(Round(0))

            def project(r):
                if not r.last:
                    rows_in(r.next())
                pe.wait_ge(p_terms, r.count(1, 1))
                for tt in range(TT):
                    for qk in range(2):
                        i = 2 * tt + qk
                        wait(pe, p_qT, r.count(2 * TT, i - 1))
                        for a in range(TERMS):
                            for c in range(KC):
                                n = a * KC + c
                                last = nc.tensor.transpose(
                                    bank16[2 + i % 2][:, n * P:(n + 1) * P],
                                    terms[r.side][:, tt, a, qk * D + c * P:qk * D + (c + 1) * P], ident[:])
                        last.then_inc(p_qTps, 1)
            rounds(pe, project)

            pe.wait_ge(p_n, TT * NB)
            pe.wait_ge(p_qT, 2 * TT * NB)
            pe.wait_ge(p_vsb, NB)
            pe.wait_ge(s_v2, NB)
            pe.wait_ge(s_ones, 1)

            def early(r, g):
                pass

            def late(r, g):
                if g == 0 and r.at(-2):
                    r = r.at(-2)
                    pe.wait_ge(a_xT, r.count(1, 1))
                    pe.wait_ge(a_x1, r.count(1, 1))
                    for c in range(KC):
                        for k in range(KC):
                            last = nc.tensor.matmul(bank[6][:, c * S:(c + 1) * S], wq[:, k, c * P:(c + 1) * P],
                                                    xn2T[:, k, :], start=(k == 0), stop=(k == KC - 1))
                    last.then_inc(a_q2ps, 1)
                if g == 1 and r.at(-1):
                    r = r.at(-1)
                    pe.wait_ge(A["attn"], r.count(2, 2))
                    wait(pe, a_q2f, r.count(1))
                    for tt in range(TT):
                        for c in range(KC):
                            last = nc.tensor.matmul(bank[6][:, tt * D:(tt + 1) * D], attnT[:, c, tt * P:(tt + 1) * P],
                                                    wp[:, c, :], start=(c == 0), stop=(c == KC - 1))
                    last.then_inc(a_proj, 1)
                if g == 3 and r.at(-1):
                    r = r.at(-1)
                    pe.wait_ge(a_xn, r.count(1, 1))
                    wait(pe, a_xT, r.count(1))
                    for tt in range(TT):
                        for k in range(KC):
                            last = nc.tensor.transpose(bank[7][:, k * S + tt * P:k * S + (tt + 1) * P],
                                                       xn2[:, tt, k * P:(k + 1) * P], identf[:])
                    last.then_inc(a_xTps, 1)

            def values_ready(r):
                pe.wait_ge(A["vpad"], r.count(1, 1))

            for slot in range(H):
                pe_score(pe, A, Round(0), slot, S, kst)
            pe_max_rows(pe, A, Round(0))

            rounds(pe, lambda r: pe_round(pe, A, r, S, kst, vpad, values_ready, early, late), after=2)

            pe.wait_ge(A["max"], H * NB)
            pe.wait_ge(A["exp"], H * NB)
            pe.wait_ge(A["mT"], NB)
            pe.wait_ge(a_q2f, NB)
            pe.wait_ge(loaded2, 16 * len(later))

            def early(r, g):
                if g == 1 and r.at(-2):
                    route(r.at(-2))
                if g == 3 and r.at(-2):
                    rank(r.at(-2))

            def late(r, g):
                if g == 0 and r.at(-2):
                    r = r.at(-2)
                    pe.wait_ge(c_xn, r.count(1, 1))
                    for tt in range(TT):
                        for k in range(KC):
                            last = nc.tensor.transpose(bank[7][:, k * S + tt * P:k * S + (tt + 1) * P],
                                                       rows3[r.side][:, tt, k * P:(k + 1) * P], identf[:])
                    last.then_inc(c_xTps, 1)
                if g == 1 and r.at(-1):
                    r = r.at(-1)
                    pe.wait_ge(C["attn"], r.count(2, 2))
                    wait(pe, c_lg, r.count(1))
                    wait(pe, c_xT, r.count(1))
                    for c in range(HID // P):
                        for k in range(KC):
                            last = nc.tensor.matmul(bank[6 + c // 2][:, (c % 2) * S:(c % 2 + 1) * S],
                                                    w1[:, k, c * P:(c + 1) * P], attnT[:, k, :],
                                                    start=(k == 0), stop=(k == KC - 1))
                    last.then_inc(c_h, 1)
                if g == 2 and r.at(-1):
                    pe.wait_ge(c_hT, r.at(-1).count(1, 1))
                    for tt in range(TT):
                        for k in range(HID // P):
                            last = nc.tensor.matmul(bank[6][:, tt * D:(tt + 1) * D], hidT[:, k, tt * P:(tt + 1) * P],
                                                    w2[:, k, :], start=(k == 0), stop=(k == HID // P - 1))
                    last.then_inc(c_y, 1)

            def values_ready(r):
                pe.wait_ge(c_v2[r.side], r.turns(16, 16))

            def route(r):
                pe.wait_ge(c_xT, r.count(1, 1))
                pe.wait_ge(c_x2, r.count(1, 1))
                for tt in range(TT):
                    for k in range(KC):
                        last = nc.tensor.matmul(bank[6][:, tt * E:(tt + 1) * E], xn2T[:, k, tt * P:(tt + 1) * P],
                                                wg[:, k, :], start=(k == 0), stop=(k == KC - 1))
                last.then_inc(c_logit, 1)

            def rank(r):
                pe.wait_ge(c_mask, r.count(1, 1))
                pe.wait_ge(c_hT, r.count(1, 1 if r.last else 2))
                nc.tensor.matmul(bank[7][:, 0:E], below[:], chosen[:, 0, :], start=True, stop=True)
                nc.tensor.matmul(bank[7][:, E:2 * E], below[:], chosen[:, 1, :], start=True, stop=False)
                nc.tensor.matmul(bank[7][:, E:2 * E], ones[:], chosen[:, 0, :], start=False, stop=True)
                nc.tensor.matmul(bank[7][:, 2 * E:3 * E], ones[:], chosen[:, 0, :], start=True, stop=False)
                nc.tensor.matmul(bank[7][:, 2 * E:3 * E], ones[:], chosen[:, 1, :], start=False,
                                 stop=True).then_inc(c_rank, 1)

            for slot in range(H):
                pe_score(pe, C, Round(0), slot, M, k2st)
            pe_max_rows(pe, C, Round(0))

            rounds(pe, lambda r: pe_round(pe, C, r, M, k2st, v2pad, values_ready, early, late), after=2)

            pe.wait_ge(c_moe, 16 * E)
            pe.wait_ge(C["max"], H * NB)
            pe.wait_ge(C["exp"], H * NB)
            pe.wait_ge(C["attn"], 2 * NB)
            pe.wait_ge(c_lg, NB)
            pe.wait_ge(c_rk, NB)
            pe.wait_ge(m_table, 1)

            def rows_in(r):
                pe.wait_ge(m_xs[r.side], r.turns(16, 16))
                wait(pe, m_xT, r.count(1))
                for k in range(KC):
                    last = nc.tensor.transpose(bank[0][:, k * P:(k + 1) * P], xs[r.side][:, k * P:(k + 1) * P],
                                               identf[:])
                last.then_inc(m_xTps, 1)

            def first_layer(r):
                expert = pe.value_load(block_i[0:1, 1, bass.ds(r.count(1), 1)], min_val=0, max_val=E - 1)
                pe.wait_ge(m_xT, r.count(1, 1))
                wait(pe, m_hid, r.count(1, -1))
                for i in range(2):
                    for k in range(KC):
                        at = (i * KC + k) * HID
                        last = nc.tensor.matmul(bank[2 + 2 * r.side + i][:, :], xsT[r.side][:, k, :],
                                                moe[:, bass.ds(expert, 1), at:at + HID].rearrange("p o n -> p (o n)"),
                                                start=(k == 0), stop=(k == KC - 1))
                    last.then_inc(m_h, 1)

            def turn_hidden(r):
                pe.wait_ge(m_hid, r.count(1, 1))
                wait(pe, m_hT, r.count(1))
                for k in range(HID // P):
                    last = nc.tensor.transpose(bank[1][:, k * P:(k + 1) * P], hid[r.side][:, k * P:(k + 1) * P],
                                               identf[:])
                last.then_inc(m_hTps, 1)

            def second_layer(r):
                expert = pe.value_load(block_i[0:1, 1, bass.ds(r.count(1), 1)], min_val=0, max_val=E - 1)
                pe.wait_ge(m_hT, r.count(1, 1))
                wait(pe, m_res, r.count(1, -1))
                for k in range(HID // P):
                    at = 2 * KC * HID + k * D
                    last = nc.tensor.matmul(bank[6 + r.side][:, 0:D], hidT2[r.side][:, k, :],
                                            moe[:, bass.ds(expert, 1), at:at + D].rearrange("p o n -> p (o n)"),
                                            start=(k == 0), stop=(k == HID // P - 1))
                last.then_inc(m_y, 1)

            rows_in(Round(0))
            rows_in(Round(1))
            first_layer(Round(0))

            def expert_block(r):
                if not r.final:
                    first_layer(r.next())
                turn_hidden(r)
                if not r.last_two:
                    rows_in(r.next().next())
                if not r.first:
                    second_layer(r.previous())
            blocks(pe, expert_block, last=True)
            second_layer(Round(BLOCKS - 1))


def layouts(x, ctx, w):
    def rows(a, pieces):
        return np.ascontiguousarray(a.reshape(pieces, P, -1).transpose(1, 0, 2))

    def spread(a):
        return np.ascontiguousarray(np.broadcast_to(a, (P,) + a.shape))

    swap = np.r_[HD // 2:HD, 0:HD // 2]
    freq = 1.0 / np.float32(10000.0) ** (np.arange(HD // 2, dtype=np.float32) / np.float32(HD // 2))
    emb = np.outer(np.arange(S, dtype=np.float32), freq.astype(np.float32)).astype(np.float32)
    emb = np.concatenate([emb, emb], -1)
    sign = np.where(np.arange(HD) < HD // 2, -1.0, 1.0)
    cos = np.cos(emb).astype(np.float32).reshape(TT, P, HD).transpose(1, 0, 2)
    sin = (np.sin(emb) * sign).astype(np.float32).reshape(TT, P, HD).transpose(1, 0, 2)
    by_channel = np.arange(D).reshape(H, HD).T.reshape(-1)
    by_channel3 = np.concatenate([by_channel, D + by_channel, np.arange(2 * D, 3 * D)])
    gamma = np.stack([w["attn_q_gamma"], w["attn_k_gamma"]])
    beta = np.stack([w["attn_q_beta"], w["attn_k_beta"]])
    pad = KC * P - TEXT - 1

    def padded(weight, bias):
        return rows(np.concatenate([weight, bias[None], np.zeros((pad, D), np.float32)]), KC)

    columns = ctx.reshape(NB * M, TEXT).T
    bf16 = mybir.dt.np(BF16)
    token = np.arange(P)
    padding = np.zeros((P, ROW), np.int32)
    padding[:, D] = TOKENS + token
    up = [w["ffn_" + n].transpose(0, 2, 1).reshape(E, KC, P, HID) for n in ("w1", "w3")]
    down = w["ffn_w2"].transpose(0, 2, 1).reshape(E, HID // P, P, D)
    experts = [a.transpose(2, 0, 1, 3).reshape(P, E, -1) for a in (*up, down)]
    return {
        "moe": np.ascontiguousarray(np.concatenate(experts, -1)),
        "w1": rows(w["xattn_W1"], KC),
        "w2": rows(w["xattn_W2"], HID // P),
        "wg": rows(w["ffn_wg"].T, KC),
        "bias_1": np.ascontiguousarray(w["xattn_b1"].reshape(HID // P, P).T),
        "bias_2": spread(w["xattn_b2"]),
        "below": np.triu(np.ones((P, P)), 1).astype(bf16),
        "ones": np.ones((P, P), bf16),
        "token_ids": (np.arange(NB * TT)[None, :] * P + token[:, None]).astype(np.int32),
        "first_of": spread(np.arange(E, 0, -1).astype(np.float32)),
        "region_at": spread((np.arange(E) * REGION).astype(np.float32)),
        "block_at": spread(np.arange(BLOCKS).astype(np.float32)),
        "padding": padding.view(np.float32),
        "x": rows(x.reshape(TOKENS, D), NB * TT),
        "wqkv": rows(w["attn_w_qkv"][by_channel3].T, KC),
        "angles": np.ascontiguousarray(np.stack([cos, sin], 1)),
        "affine": spread(np.stack([gamma, gamma[:, swap], beta, beta[:, swap]])),
        "identf": np.eye(P, dtype=np.float32),
        "ident": np.eye(P).astype(bf16),
        "ctxT": rows(np.concatenate([columns, np.ones((1, NB * M), np.float32),
                                     np.zeros((pad, NB * M), np.float32)]), KC),
        "wk": padded(w["xattn_Wk"][:, by_channel], w["xattn_bk"][by_channel]),
        "wv": padded(w["xattn_Wv"], w["xattn_bv"]),
        "wp": rows(w["attn_w_proj"].T, KC),
        "wq": rows(w["xattn_Wq"][:, by_channel], KC),
        "bias_q": np.ascontiguousarray(w["xattn_bq"][by_channel].reshape(KC, P).T),
        "bias_p": spread(w["attn_b_proj"]),
    }


def kernel(**inputs):
    import concourse.bacc as bacc
    from concourse.bass_utils import run_bass_kernel_spmd

    given = {k: np.asarray(v) for k, v in inputs.items()}
    arrays = layouts(given["x"], given["ctx_768"],
                     {k[3:]: v for k, v in given.items() if k.startswith("L0_")})
    nc = bacc.Bacc("TRN2", target_bir_lowering=False, num_devices=1)
    tiles = {k: nc.dram_tensor("in_" + k, a.shape, mybir.dt.from_np(a.dtype), kind="ExternalInput").ap()
             for k, a in arrays.items()}
    out = nc.dram_tensor("out", (TOKENS, D), F32, kind="ExternalOutput").ap()
    decoder_layer(nc, tiles, out)
    result = run_bass_kernel_spmd(nc, [{"in_" + k: a for k, a in arrays.items()}], core_ids=[0])
    return result.results[0]["out"].reshape(NB, S, D)
```

```python
from contextlib import ExitStack

import numpy as np

import concourse.bass as bass
from concourse import mybir
from concourse.alu_op_type import AluOpType as ALU

F32, BF16, I32 = mybir.dt.float32, mybir.dt.bfloat16, mybir.dt.int32
ACT = mybir.ActivationFunctionType
X = mybir.AxisListType.X

P = 128
NB, S, D = 8, 256, 256
H, HD = 16, 16
M = 77
TEXT = 192
TT = S // P
KC = D // P
HID = 512
E = 8
TOKENS = NB * S
TERMS = 3
PRODUCTS = 6
STORED = 4
Q_STORES = ((0, 0, 3), (3, 0, 1))
K_STORES = ((0, 2, 1), (1, 0, 1), (2, 0, 2))
Q_LOADS = ((0, 0, 4), (4, 0, 2))
K_LOADS = ((0, 0, 4), (4, 2, 2))
ROWS = HD * PRODUCTS
AUG = ROWS + TERMS
GROUP = 4
GROUPS = H // GROUP
HALF = H // 2
LOADS = 16 * (len(Q_LOADS) + len(K_LOADS))
STORES = 16 * (len(Q_STORES) + len(K_STORES))
SELF_SCORED = (range(0, 5), range(5, 12), range(12, H), range(0))
CROSS_SCORED = (range(0, 8), range(8, 12), range(12, H), range(0))
HEADS = [8 * c + 2 * j + half for c in range(2) for half in range(2) for j in range(4)]
ROW = D + 1 + E
REGION = TOKENS + P
BLOCKS = 2 * TOKENS // P + E - 1
SPARE = E * REGION
LOW = -3.0e38
MAGIC = float(0x5F3759DF)
NEWTON = 3


class Round:

    def __init__(self, own, pair=None):
        self.own, self.pair, self.side = own, pair, own % 2

    def count(self, per, more=0):
        known = per * self.own + more
        return known if self.pair is None else self.pair * (2 * per) + known

    def turns(self, per, more=0):
        known = per * (self.own // 2) + more
        return known if self.pair is None else self.pair * per + known

    def next(self):
        return Round(self.own + 1, self.pair)

    def previous(self):
        return Round(self.own - 1, self.pair)

    @property
    def first(self):
        return self.pair is None and self.own == 0

    @property
    def final(self):
        return self.pair is None and self.own == BLOCKS - 1

    def at(self, shift):
        if self.pair is None and not 0 <= self.own + shift < NB:
            return None
        return Round(self.own + shift, self.pair)

    @property
    def opening(self):
        return self.pair is None and self.own < 2

    @property
    def last_two(self):
        return self.pair is None and self.own >= BLOCKS - 2

    @property
    def last(self):
        return self.pair is None and self.own == NB - 1


def rounds(eng, body, after=0):
    for own in range(2):
        body(Round(own))
    with eng.Fori(0, (NB - 4) // 2) as pair:
        body(Round(2, pair))
        body(Round(3, pair))
    for own in range(NB - 2, NB + after):
        body(Round(own))


def blocks(eng, body, last=False):
    for own in range(3):
        body(Round(own))
    with eng.Fori(0, (BLOCKS - 3) // 2 - last) as pair:
        body(Round(3, pair))
        body(Round(4, pair))
    if last:
        body(Round(BLOCKS - 2))
        body(Round(BLOCKS - 1))


def wait(eng, sem, value):
    if not isinstance(value, int) or value > 0:
        eng.wait_ge(sem, value)


def decoder_layer(nc, t, out):
    ctx = ExitStack()
    with ctx:
        def sb(name, shape, dt=F32):
            return ctx.enter_context(nc.sbuf_tensor(name, shape, dt))

        def sem(name):
            return ctx.enter_context(nc.semaphore(name))

        qk_terms = nc.dram_tensor("qk_terms", [NB, 2, STORED, D, S], BF16, kind="Internal").ap()
        x1_dram = nc.dram_tensor("x1_dram", [NB, P, TT, D], F32, kind="Internal").ap()
        q2_terms = nc.dram_tensor("q2_terms", [NB, STORED, D, S], BF16, kind="Internal").ap()
        k2_terms = nc.dram_tensor("k2_terms", [NB, STORED, D, M], BF16, kind="Internal").ap()
        v2_dram = nc.dram_tensor("v2_dram", [NB, M, H * 2 * HD], F32, kind="Internal").ap()
        routed = nc.dram_tensor("routed", [SPARE + P, ROW], F32, kind="Internal").ap()

        early = sb("early", [P, E * 3 * 2 * HID])
        moe = early[:, :].rearrange("p (e n) -> p e n", e=E)
        used = [0]

        def carve(words):
            at = used[0]
            used[0] += words
            assert used[0] <= E * 3 * 2 * HID
            return early[:, at:at + words]

        wqkv = carve(KC * 3 * D).rearrange("p (k n) -> p k n", k=KC)
        xn = [carve(TT * D).rearrange("p (t c) -> p t c", t=TT) for _ in range(2)]
        xnT = [carve(KC * S).rearrange("p (k s) -> p k s", k=KC) for _ in range(2)]
        square = carve(TT * 2 * D).rearrange("p (t c) -> p t c", t=TT)
        normed = carve(TT * 2 * D).rearrange("p (t c) -> p t c", t=TT)
        direct = carve(TT * 2 * D).rearrange("p (t c) -> p t c", t=TT)
        rotated = carve(TT * 2 * D).rearrange("p (t c) -> p t c", t=TT)
        terms = [carve(TT * TERMS * D).bitcast(BF16).rearrange("p (t a c) -> p t a c", t=TT, a=TERMS)
                 for _ in range(2)]
        qkT = [carve(2 * TERMS * KC * S // 2).bitcast(BF16).rearrange("p (q a c s) -> p q a c s", q=2, a=TERMS, s=S)
               for _ in range(2)]
        ctxT = carve(KC * NB * M).rearrange("p (k m) -> p k m", k=KC)
        wk = carve(KC * D).rearrange("p (k n) -> p k n", k=KC)
        wv = carve(KC * D).rearrange("p (k n) -> p k n", k=KC)
        assert used[0] >= (NB - 4) * 3 * 2 * HID
        values = carve(NB * TT * D).rearrange("p (t c) -> p t c", t=NB * TT)
        vpad = [carve(TT * H * 2 * HD).rearrange("p (t h d) -> p t h d", t=TT, h=H) for _ in range(2)]
        tables = carve(3 * TT * 2 * HD).rearrange("p (a t q d) -> p a t q d", a=3, t=TT, q=2)
        affine = carve(4 * 2 * HD).rearrange("p (a q d) -> p a q d", a=4, q=2)
        angles = carve(2 * TT * HD).rearrange("p (a t d) -> p a t d", a=2, t=TT)
        wmean = carve(KC * 2 * H).rearrange("p (k g) -> p k g", k=KC)
        spread = carve(TT * 2 * H)
        row_stats = carve(NB * TT * 2).rearrange("p (t a) -> p t a", a=2)
        row_rstd = carve(NB * TT)


        qst = [sb(f"qst{i}", [P, H, S], BF16) for i in range(2)]
        kst = [sb(f"kst{i}", [P, H, S], BF16) for i in range(2)]
        k2st = [sb(f"k2st{i}", [P, H, M], BF16) for i in range(2)]
        v2pad = [sb(f"v2pad{i}", [P, 1, H, 2 * HD]) for i in range(2)]
        probs = sb("probs", [P, 2, GROUP, 2 * S])
        v2_stage = [v[:, 0, :, :] for v in v2pad] + [v[:, tt, :, :] for v in vpad for tt in range(TT)]
        x_all = probs[:, :, :, :].rearrange("p a b c -> p (a b c)").rearrange("p (t c) -> p t c", c=D)
        k2f = qst[0][:, :, :].rearrange("p h s -> p (h s)").bitcast(F32)[:, 0:KC * NB * M]
        k2parts = qst[1][:, :, :].rearrange("p h s -> p (h s)")[:, 0:TERMS * KC * NB * M].rearrange(
            "p (a c b m) -> p a c b m", a=TERMS, c=KC, b=NB)
        wp = sb("wp", [P, KC, D])
        wq = sb("wq", [P, KC, D])
        w1 = sb("w1", [P, KC, HID])
        w2 = sb("w2", [P, HID // P, D])
        wg = sb("wg", [P, KC, E])
        identf = sb("identf", [P, P])
        ident = sb("ident", [P, P], BF16)
        below = sb("below", [P, P], BF16)
        ones = sb("ones", [P, P], BF16)
        onesrow = sb("onesrow", [P, 2, 2 * HD])
        bias_p = sb("bias_p", [P, D])
        bias_2 = sb("bias_2", [P, D])
        bias_q = sb("bias_q", [P, KC])
        bias_1 = sb("bias_1", [P, HID // P])
        resid = [sb(f"resid{i}", [P, TT, D]) for i in range(2)]
        x_new = [sb(f"x_new{i}", [P, TT, D]) for i in range(2)]
        xn2 = sb("xn2", [P, TT, D])
        xn2T = sb("xn2T", [P, KC, S])
        q2both = sb("q2both", [P, 2 * KC, S])
        q2f, q2rest = q2both[:, 0:KC, :], q2both[:, KC:, :]
        hidT = q2both[:, :, :]
        q2T = [sb(f"q2T{i}", [P, TERMS, KC, S], BF16) for i in range(2)]
        attnT = sb("attnT", [P, 2, S])
        recip = sb("recip", [P, 2, S])
        maxes = sb("maxes", [P, H, TT])
        mrest = sb("mrest", [P, TT, H])
        mterms = sb("mterms", [P, TT, P // H, H], BF16)
        mT = sb("mT", [TERMS * H, S], BF16)
        rows3 = [sb(f"rows3_{i}", [P, TT, ROW]) for i in range(2)]
        token_ids = sb("token_ids", [P, NB * TT], I32)
        logits = sb("logits", [P, TT, E])
        first_of = sb("first_of", [P, E])
        pick = [sb(f"pick{i}", [P, TT, E]) for i in range(2)]
        key = sb("key", [P, TT, E])
        best = [sb(f"best{i}", [P, TT]) for i in range(2)]
        chosen = sb("chosen", [P, TT, E], BF16)
        gap = sb("gap", [P, TT])
        share = [sb(f"share{i}", [P, TT]) for i in range(2)]
        top = sb("top", [P, TT])
        ranks = sb("ranks", [P, TT, E])
        taken = [sb(f"taken{i}", [P, TT, E]) for i in range(2)]
        filled = sb("filled", [P, E])
        posf = sb("posf", [P, TT, 2])
        pos = [sb(f"pos{i}", [P, TT * 2], I32) for i in range(2)]
        tokens = sb("tokens", [P, 1], I32)
        padding = sb("padding", [P, ROW])
        region_at = sb("region_at", [P, E])
        block_at = sb("block_at", [P, BLOCKS])
        filled_i = sb("filled_i", [P, E], I32)
        count_i = sb("count_i", [P, E], I32)
        ends_f = sb("ends_f", [P, E])
        step_f = sb("step_f", [P, E])
        flat_p = probs[:, :, :, :].rearrange("p a b c -> p (a b c)")
        past = flat_p[:, 0:BLOCKS * (E + 1)].rearrange("p (b e) -> p b e", e=E + 1)
        of_block = flat_p[:, 512:512 + BLOCKS * E].rearrange("p (b e) -> p b e", e=E)
        scaled = flat_p[:, 1024:1024 + BLOCKS * E].rearrange("p (b e) -> p b e", e=E)
        block_f = flat_p[:, 1536:1536 + 2 * BLOCKS].rearrange("p (a b) -> p a b", a=2)
        tokens_of = flat_p[:, 2560:2560 + BLOCKS].bitcast(I32)
        block_i = flat_p[:, 2048:2048 + 2 * BLOCKS].rearrange("p (a b) -> p a b", a=2).bitcast(I32)
        flat_q = [q[:, :, :].rearrange("p h s -> p (h s)").bitcast(F32) for q in qst]
        xs = [f[:, 0:ROW] for f in flat_q]
        xsT = [f[:, 288:288 + D].rearrange("p (k c) -> p k c", k=KC) for f in flat_q]
        act1 = [f[:, 544:544 + HID] for f in flat_q]
        hid = [f[:, 1056:1056 + HID] for f in flat_q]
        flat_k = [q[:, :, :].rearrange("p h s -> p (h s)").bitcast(F32) for q in kst]
        hidT2 = [f[:, 0:HID].rearrange("p (k c) -> p k c", k=HID // P) for f in flat_k]
        result = [f[:, 512:512 + D] for f in flat_k]
        gates = [f[:, 768:768 + E] for f in flat_k]
        gate = [f[:, 776:777] for f in flat_k]
        moments = sb("moments", [P, TT, 6])
        row_moments = carve(4 * TT * 6).rearrange("p (t a) -> p t a", a=6)
        stats = sb("stats", [P, TT, 2])
        rstd = sb("rstd", [P, TT])
        newton = sb("newton", [P, TT])
        vareps = sb("vareps", [P, TT])

        bank = [ctx.enter_context(nc.psum_tensor(f"bank{i}", [P, 512], F32)) for i in range(8)]
        bank16 = [b[:, :].bitcast(BF16) for b in bank]

        QK_BANKS = ((0, 1), (5, 7))
        ROW_GROUPS = (slice(0, 2 * TT), slice(2 * TT, NB * TT))

        loaded = sem("loaded")
        loaded_ctx = sem("loaded_ctx")
        x_first, x_rest = sem("x_first"), sem("x_rest")
        s_ones = sem("s_ones")
        s_tab = sem("s_tab")
        s_k2ps, s_k2f, s_k2t, s_k2st = sem("s_k2ps"), sem("s_k2f"), sem("s_k2t"), sem("s_k2st")
        s_zero, s_v2ps, s_v2 = sem("s_zero"), sem("s_v2ps"), sem("s_v2")
        s_v2st = [sem("s_v2st0"), sem("s_v2st1")]
        p_xn = sem("p_xn")
        p_xTps, p_xT = sem("p_xTps"), sem("p_xT")
        p_qk, p_v, p_sq = sem("p_qk"), sem("p_v"), sem("p_sq")
        p_rows, p_sum, p_root = sem("p_rows"), sem("p_sum"), sem("p_root")
        p_n, p_rot, p_terms = sem("p_n"), sem("p_rot"), sem("p_terms")
        p_vsb = sem("p_vsb")
        p_qTps, p_qT = sem("p_qTps"), sem("p_qT")
        p_store = [sem("p_store0"), sem("p_store1")]

        def attention_sems(tag):
            return {n: sem(f"{tag}_{n}") for n in (
                "sq", "max", "mterms", "mTps", "mT", "st", "exp", "av", "attn", "vpad")} | {
                "aug": [sem(f"{tag}_aug{i}") for i in range(2)],
                "stack": [[sem(f"{tag}_stack{i}{half}") for half in range(2)] for i in range(2)]}

        def last_scored(scored):
            return max(g for g in range(GROUPS) if len(scored[g]))

        A = attention_sems("a") | {"keys": S, "kst": kst, "values": vpad}
        a_res = [sem("a_res0"), sem("a_res1")]
        a_resb, a_proj, a_x1, a_var, a_rstd, a_xn = (sem(n) for n in (
            "a_resb", "a_proj", "a_x1", "a_var", "a_rstd", "a_xn"))
        a_x1st = [sem("a_x1st0"), sem("a_x1st1")]
        a_xTps, a_xT, a_q2ps, a_q2f, a_q2t = (sem(n) for n in (
            "a_xTps", "a_xT", "a_q2ps", "a_q2f", "a_q2t"))
        a_q2st = [sem("a_q2st0"), sem("a_q2st1")]

        C = attention_sems("c") | {"keys": M, "kst": k2st, "values": v2pad}
        before = A
        loaded2 = sem("loaded2")
        c_res = [sem("c_res0"), sem("c_res1")]
        c_v2 = [sem("c_v20"), sem("c_v21")]
        c_out = [sem("c_out0"), sem("c_out1")]
        c_moe = sem("c_moe")
        (c_resb, c_h, c_hT, c_y, c_x2, c_var, c_rstd, c_xn, c_xTps, c_xT, c_logit, c_lg, c_mask, c_gap, c_ed,
         c_rank, c_rk, c_pos, c_gates) = (sem("c_" + n) for n in (
             "resb", "h", "hT", "y", "x2", "var", "rstd", "xn", "xTps", "xT", "logit", "lg", "mask", "gap", "ed",
             "rank", "rk", "pos", "gates"))
        c_scatter = [sem("c_scatter0"), sem("c_scatter1")]
        m_filled, m_table = sem("m_filled"), sem("m_table")
        m_pad = [sem("m_pad_sp"), sem("m_pad_act")]
        m_xs = [sem("m_xs0"), sem("m_xs1")]
        m_xTps, m_xT, m_h, m_silu, m_hid, m_hTps, m_hT, m_y, m_res, m_gate = (sem("m_" + n) for n in (
            "xTps", "xT", "h", "silu", "hid", "hTps", "hT", "y", "res", "gate"))
        m_added = sem("m_added")

        block = ctx.enter_context(nc.Block())

        context = [("ctxT", ctxT), ("wk", wk), ("wv", wv)]
        weights = [("wqkv", wqkv), ("identf", identf[:]), ("angles", angles), ("affine", affine),
                   ("ident", ident[:])]
        later = [("wp", wp[:]), ("wq", wq[:]), ("bias_q", bias_q[:]), ("bias_p", bias_p[:]), ("w1", w1[:]), ("w2", w2[:]), ("wg", wg[:]), ("below", below[:]), ("bias_2", bias_2[:]),
                 ("bias_1", bias_1[:]), ("ones", ones[:]), ("token_ids", token_ids[:]),
                 ("first_of", first_of[:]), ("region_at", region_at[:]), ("block_at", block_at[:]),
                 ("padding", padding[:])]

        def rsqrt_on_pool(pool, n=TT):
            for step in range(NEWTON):
                if step:
                    pool.drain()
                nc.gpsimd.tensor_tensor(newton[:], rstd[:], rstd[:], ALU.mult)
                pool.drain()
                nc.gpsimd.tensor_tensor(newton[:], newton[:], vareps[:], ALU.mult)
                pool.drain()
                nc.gpsimd.tensor_scalar(newton[:], newton[:], -0.5, 1.5, ALU.mult, ALU.add)
                pool.drain()
                last = nc.gpsimd.tensor_tensor(rstd[:], rstd[:], newton[:], ALU.mult)
            return last

        def moments_of(dve, src, eps):
            for tt in range(TT):
                nc.vector.bn_stats(moments[:, tt, :], src[:, tt, :])
            dve.drain()
            for tt in range(TT):
                nc.vector.bn_aggr(stats[:, tt, :], moments[:, tt, :])
            dve.drain()
            nc.vector.tensor_scalar(vareps[:], stats[:, :, 1], eps, None, ALU.add)
            dve.drain()
            return nc.vector.tensor_scalar(rstd[:].bitcast(I32), vareps[:].bitcast(I32), -0.5, MAGIC,
                                           ALU.mult, ALU.add)

        def norm_into(dst, src):
            for tt in range(TT):
                last = nc.vector.tensor_scalar(dst[:, tt, 0:D], src[:, tt, :], stats[:, tt, 0:1],
                                               rstd[:, tt:tt + 1], ALU.subtract, ALU.mult)
            return last


        def pe_score(pe, A, r, slot):
            h, keys, kstk = HEADS[slot], A["keys"], A["kst"]
            if slot == 0 and A is C and r.first:
                pe.wait_ge(before["max"], H * NB)
                pe.wait_ge(before["mT"], NB)
            if slot % HALF == 0:
                pe.wait_ge(A["stack"][r.side][slot // HALF], r.turns(LOADS, LOADS))
            if slot == 0:
                wait(pe, A["mT"], r.count(1))
            wait(pe, A["max"], r.count(H, slot - 1))
            for qt in range(TT):
                last = nc.tensor.matmul(bank[slot % 2][:, qt * keys:(qt + 1) * keys],
                                        qst[r.side][0:ROWS, h, qt * P:(qt + 1) * P],
                                        kstk[r.side][0:ROWS, h, :], start=True, stop=True)
            last.then_inc(A["sq"], 1)

        def dve_max(dve, A, r, slot):
            keys = A["keys"]
            if slot == 0 and A is C and r.first:
                dve.wait_ge(before["mterms"], NB)
            dve.wait_ge(A["sq"], r.count(H, slot + 1))
            if slot == 0:
                wait(dve, A["mterms"], r.count(1))
            nc.vector.tensor_reduce(maxes[:, HEADS[slot], :],
                                    bank[slot % 2][:, 0:TT * keys].rearrange("p (t k) -> p t k", t=TT),
                                    axis=X, op=ALU.max).then_inc(A["max"], 1)

        def dve_split_max(dve, A, r):
            if A is C and r.first:
                dve.wait_ge(before["mTps"], NB)
            dve.drain()
            wait(dve, A["mTps"], r.count(1))
            nc.vector.tensor_scalar(mrest[:], maxes[:, :, :].rearrange("p h t -> p t h"), -1.0, None, ALU.mult)
            for a in range(TERMS):
                dve.drain()
                last = nc.vector.tensor_copy(mterms[:, :, a, :], mrest[:])
                if a < TERMS - 1:
                    dve.drain()
                    nc.vector.tensor_tensor(mrest[:], mrest[:], mterms[:, :, a, :], ALU.subtract)
            last.then_inc(A["mterms"], 1)

        def pe_max_rows(pe, A, r):
            pe.wait_ge(A["mterms"], r.count(1, 1))
            for qt in range(TT):
                last = nc.tensor.transpose(bank16[0][:, qt * P:(qt + 1) * P],
                                           mterms[:, qt, :, :].rearrange("p a h -> p (a h)"), ident[:])
            last.then_inc(A["mTps"], 1)

        def act_max_rows(act, A, r):
            if A is C and r.first:
                act.wait_ge(before["aug"][1], 16 * TERMS * (NB // 2))
            act.wait_ge(A["mTps"], r.count(1, 1))
            if not (r.pair is None and r.own == 0):
                act.wait_ge(A["aug"][1 - r.side], r.previous().turns(16 * TERMS, 16 * TERMS))
            nc.scalar.copy(mT[:], bank16[0][0:TERMS * H, 0:S]).then_inc(A["mT"], 1)

        def sp_max_rows(sp, A, r):
            sp.wait_ge(A["mT"], r.count(1, 1))
            for a in range(TERMS):
                sp.dma_start(qst[r.side][ROWS + a:ROWS + a + 1, :, :], mT[a * H:(a + 1) * H, :]
                             ).then_inc(A["aug"][r.side], 16)

        def store_parts(sp, dst, parts, stores, done):
            for group, part, n in stores:
                sp.dma_start(dst[group:group + n].rearrange("a (c p) s -> p a c s", p=P),
                             parts[:, part:part + n]).then_inc(done, 16)

        def load_half(sp, A, r, half, q_dram, k_dram, kstk):
            wait(sp, A["st"], r.count(H, (half + 1) * HALF - 2 * H))
            for stk, terms_dram, loads in ((qst, q_dram, Q_LOADS), (kstk, k_dram, K_LOADS)):
                for to, at, n in loads:
                    src = terms_dram[at:at + n].rearrange("a (d h) s -> (a d) h s", h=H)
                    sp.dma_start(stk[r.side][to * HD:(to + n) * HD, half * HALF:(half + 1) * HALF, :],
                                 src[:, half * HALF:(half + 1) * HALF, :]).then_inc(A["stack"][r.side][half], 16)

        def pe_exponents(pe, A, r, slots):
            keys, kstk = A["keys"], A["kst"]
            tiles, size = (keys + P - 1) // P, min(P, keys)
            for slot in slots:
                if slot == 0:
                    pe.wait_ge(A["aug"][r.side], r.turns(16 * TERMS, 16 * TERMS))
                wait(pe, A["exp"], r.count(H, slot - 1))
                for kt in range(tiles):
                    last = nc.tensor.matmul(bank[2 + slot % 2][0:size, kt * S:(kt + 1) * S],
                                            kstk[r.side][0:AUG, HEADS[slot], kt * P:kt * P + size],
                                            qst[r.side][0:AUG, HEADS[slot], :], start=True, stop=True)
                last.then_inc(A["st"], 1)

        def act_exp(act, A, r, slots):
            keys = A["keys"]
            tiles, size = (keys + P - 1) // P, min(P, keys)
            for slot in slots:
                g = slot // GROUP
                if slot % GROUP == 0:
                    wait(act, A["av"], r.count(GROUPS, g - 1))
                act.wait_ge(A["st"], r.count(H, slot + 1))
                nc.scalar.activation(probs[0:size, g % 2, slot % GROUP, 0:tiles * S],
                                     bank[2 + slot % 2][0:size, 0:tiles * S], ACT.Exp).then_inc(A["exp"], 1)

        def pe_values(pe, A, r, g, kind):
            keys, vp = A["keys"], A["values"]
            tiles, size = (keys + P - 1) // P, min(P, keys)
            chunk, half = g // 2, g % 2
            if kind == 0:
                pe.wait_ge(A["exp"], r.count(H, (g + 1) * GROUP))
                if half == 0:
                    wait(pe, A["attn"], r.count(2, chunk - 1))
            for kt in range(tiles):
                for j in range(GROUP):
                    lhs = (vp[r.side][0:size, kt, HEADS[g * GROUP + j], :] if kind == 0
                           else onesrow[0:size, half, :])
                    last = nc.tensor.matmul(
                        bank[4 + chunk][32 * j:32 * j + 32, kind * S:(kind + 1) * S], lhs,
                        probs[0:size, g % 2, j, kt * S:(kt + 1) * S],
                        start=(kind == 0 and half == 0 and kt == 0),
                        stop=(half == 1 and kt == tiles - 1),
                        skip_group_check=True)
            if kind == 1:
                last.then_inc(A["av"], 1)


        def ahead(A, r, following):
            if not r.at(0):
                return None
            if r.at(1):
                return A, r.at(1)
            return following and (following, Round(0))

        def pe_round(pe, A, r, scored, values_ready, early, late, following=None, leading=None):
            coming = ahead(A, r, following)
            for g in range(GROUPS):
                first = g * GROUP
                scores = list(scored[g]) if coming else []
                values = (A, r.at(0), g - 1) if g else (A, r.at(-1), GROUPS - 1)
                if leading and g == 0 and r.first:
                    values = (leading, Round(NB - 1), GROUPS - 1)
                if r.at(0):
                    pe_exponents(pe, A, r, (first, first + 1))
                for slot in scores[0:2]:
                    pe_score(pe, *coming, slot)
                early(r, g)
                if values[1]:
                    if values[2] == 0:
                        values_ready(values[1])
                    pe_values(pe, *values, 0)
                if r.at(0):
                    pe_exponents(pe, A, r, (first + 2, first + 3))
                for slot in scores[2:]:
                    pe_score(pe, *coming, slot)
                if values[1]:
                    pe_values(pe, *values, 1)
                late(r, g, (lambda: pe_max_rows(pe, *coming)) if coming and g == last_scored(scored) else None)

        def act_round(act, A, r, scored, late, following=None):
            coming = ahead(A, r, following)
            for g in range(GROUPS):
                if r.at(0):
                    act_exp(act, A, r, range(g * GROUP, (g + 1) * GROUP))
                    if g == last_scored(scored) and coming:
                        act_max_rows(act, *coming)
                late(r, g)

        def dve_round(dve, A, r, scored, next_done, late, following=None, leading=None):
            coming = ahead(A, r, following)
            for g in range(GROUPS):
                if coming:
                    for slot in scored[g]:
                        dve_max(dve, *coming, slot)
                    if g == last_scored(scored):
                        dve_split_max(dve, *coming)
                if g == GROUPS - 1 and r.at(0):
                    dve_attn(dve, A, r, 0, next_done)
                late(r, g)
                if g == 0 and r.at(-1):
                    dve_attn(dve, A, r.at(-1), 1, next_done)
                if g == 0 and leading and r.first:
                    dve_attn(dve, leading, Round(NB - 1), 1, next_done)

        def dve_attn(dve, A, r, chunk, next_done):
            dve.wait_ge(A["av"], r.count(GROUPS, 2 * chunk + 2))
            if chunk == 0:
                wait(dve, next_done, r.count(1))
            nc.vector.reciprocal(recip[:, chunk, :], bank[4 + chunk][:, S:])
            dve.drain()
            nc.vector.tensor_tensor(attnT[:, chunk, :], bank[4 + chunk][:, 0:S], recip[:, chunk, :], ALU.mult
                                    ).then_inc(A["attn"], 1)

        def pad_regions(eng, experts, done):
            eng.wait_ge(m_filled, 1)
            for e in experts:
                at = eng.value_load(filled_i[0:1, e:e + 1], min_val=e * REGION, max_val=e * REGION + TOKENS)
                eng.dma_start(routed[bass.ds(at, P), :], padding[:]).then_inc(done, 16)

        @block.sync
        def _(sp):
            for name, tile in context:
                sp.dma_start(tile, t[name]).then_inc(loaded_ctx, 16)
            sp.dma_start(x_all[:, 0:2 * TT, :], t["x"][:, 0:2 * TT, :]).then_inc(x_first, 16)
            for name, tile in weights:
                sp.dma_start(tile, t[name]).then_inc(loaded, 16)
            sp.dma_start(x_all[:, 2 * TT:, :], t["x"][:, 2 * TT:, :]).then_inc(x_rest, 16)

            for b in range(NB):
                sp.wait_ge(s_v2, b + 1)
                sp.dma_start(v2_dram[b], v2_stage[b % len(v2_stage)][0:M].rearrange("p h d -> p (h d)")
                             ).then_inc(s_v2st[b % 2], 16)
            sp.wait_ge(s_k2t, 1)
            for a in range(TERMS):
                for c in range(KC):
                    for group, part, n in K_STORES:
                        if part <= a < part + n:
                            sp.dma_start(
                                k2_terms[:, group + a - part, c * P:(c + 1) * P, :].rearrange("b p m -> p b m"),
                                k2parts[:, a, c, :, :]).then_inc(s_k2st, 16)

            for name, tile in later:
                sp.dma_start(tile, t[name]).then_inc(loaded2, 16)

            def load(r, half):
                load_half(sp, A, r, half, qk_terms[r.count(1)][0], qk_terms[r.count(1)][1], kst)

            def project(r):
                if r.pair is None and r.own == NB - 2:
                    sp.wait_ge(s_k2st, 16 * STORED * KC)
                    sp.wait_ge(p_store[0], STORES)
                    load(Round(0), 0)
                    load(Round(0), 1)
                    sp.wait_ge(p_store[1], STORES)
                    load(Round(1), 0)
                if r.last:
                    sp_max_rows(sp, A, Round(0))
                sp.wait_ge(p_qT, r.count(2 * TT, 2 * TT))
                for qk, stores in enumerate((Q_STORES, K_STORES)):
                    store_parts(sp, qk_terms[r.count(1)][qk], qkT[r.side][:, qk], stores, p_store[r.side])
            rounds(sp, project)

            def residual(r):
                wait(sp, a_x1, r.count(1, -1))
                sp.dma_start(resid[r.side][:], t["x"][:, bass.ds(r.count(TT), TT), :]
                             ).then_inc(a_res[r.side], 16)

            def load_expert(e):
                sp.dma_start(moe[:, bass.ds(e, 1), :], t["moe"][:, bass.ds(e, 1), :]).then_inc(c_moe, 16)

            def store_residual(r):
                sp.wait_ge(a_x1, r.count(1, 1))
                sp.dma_start(x1_dram[r.count(1)], x_new[r.side][:]).then_inc(a_x1st[r.side], 16)

            def store_queries(r):
                sp.wait_ge(a_q2t, r.count(1, 1))
                store_parts(sp, q2_terms[r.count(1)], q2T[r.side], Q_STORES, a_q2st[r.side])

            for i in range(2):
                sp.wait_ge(p_store[i], STORES * NB // 2)
            sp.wait_ge(p_vsb, NB)

            def load_cross(r, half):
                load_half(sp, C, r, half, q2_terms[r.count(1)], k2_terms[r.count(1)], k2st)

            def self_round(r):
                if r.at(1):
                    load(r.at(1), 1)
                else:
                    for i in range(2):
                        sp.wait_ge(a_q2st[i], 2 * 16 * len(Q_STORES))
                    sp.wait_ge(A["st"], H * (NB - 1))
                    load_cross(Round(0), 0)
                    load_cross(Round(0), 1)
                residual(r)
                if r.pair is not None:
                    load_expert(r.count(1, -2))
                if r.at(-1):
                    store_residual(r.at(-1))
                if r.at(2):
                    load(r.at(2), 0)
                elif r.last:
                    sp.wait_ge(A["st"], H * (NB - 1) + HALF)
                    load_cross(Round(1), 0)
                sp_max_rows(sp, *((A, r.at(1)) if r.at(1) else (C, Round(0))))
                if r.at(-2):
                    store_queries(r.at(-2))
            rounds(sp, self_round)

            for i in range(2):
                sp.wait_ge(s_v2st[i], 16 * NB // 2)
                sp.wait_ge(a_x1st[i], 16)
            sp.wait_ge(A["st"], H * NB)

            def load_values2(r):
                wait(sp, C["av"], r.count(GROUPS, -GROUPS))
                sp.dma_start(v2pad[r.side][0:M, 0, :, :].rearrange("p h d -> p (h d)"), v2_dram[r.count(1)]
                             ).then_inc(c_v2[r.side], 16)
                if r.opening:
                    sp.wait_ge(a_x1, NB - 1 + r.own)
                wait(sp, c_x2, r.count(1, -1))
                sp.dma_start(resid[r.side][:], x1_dram[r.count(1)]).then_inc(c_res[r.side], 16)

            def store_out(r):
                sp.wait_ge(c_x2, r.count(1, 1))
                sp.dma_start(out[bass.ds(r.count(S), S), :].rearrange("(t p) c -> p t c", p=P),
                             x_new[r.side][:]).then_inc(c_out[r.side], 16)

            def cross_round(r):
                if r.at(0) and r.at(1):
                    load_cross(r.at(1), 1)
                if r.at(0):
                    load_values2(r)
                if r.pair is not None:
                    load_expert(r.count(1, NB - 6))
                if r.first:
                    store_residual(Round(NB - 1))
                if r.at(-2):
                    store_out(r.at(-2))
                if r.at(0) and r.at(2):
                    load_cross(r.at(2), 0)
                if r.at(0) and r.at(1):
                    sp_max_rows(sp, C, r.at(1))
                if r.opening:
                    store_queries(Round(NB - 2 + r.own))
                if r.opening and r.own == 1:
                    for i in range(2):
                        sp.wait_ge(a_x1st[i], 16 * NB // 2)
                        sp.wait_ge(a_q2st[i], 16 * len(Q_STORES) * NB // 2)
                    sp.wait_ge(A["av"], GROUPS * NB)
            rounds(sp, cross_round, after=2)

            sp.dma_start(routed[SPARE:SPARE + P, :], padding[:]).then_inc(m_pad[0], 16)
            pad_regions(sp, range(0, E // 2), m_pad[0])
            sp.wait_ge(m_pad[0], 16 * (E // 2 + 1))
            sp.wait_ge(m_pad[1], 16 * (E // 2))
            for i in range(2):
                sp.wait_ge(c_scatter[i], 16 * 2 * TT * NB // 2)
            sp.wait_ge(m_table, 1)

            def block_rows(r):
                at = sp.value_load(block_i[0:1, 0, bass.ds(r.count(1), 1)], min_val=0, max_val=SPARE)
                wait(sp, m_gate, r.count(1, -1))
                wait(sp, m_xTps, r.count(1, -1))
                sp.dma_start(xs[r.side], routed[bass.ds(at, P), :]).then_inc(m_xs[r.side], 16)
            blocks(sp, block_rows)

        @block.gpsimd
        def _(pool):
            for tile in (v2pad[0][:], v2pad[1][:], vpad[0], vpad[1]):
                last = nc.gpsimd.memset(tile, 0.0)
            last.then_inc(s_zero, 1)
            for tile in (onesrow[:], mterms[:]):
                nc.gpsimd.memset(tile, 0.0)
            for half in range(2):
                pool.drain()
                nc.gpsimd.memset(onesrow[:, half, half * HD:(half + 1) * HD], 1.0)
            for stk in kst + k2st:
                pool.drain()
                last = nc.gpsimd.memset(stk[ROWS:AUG, :, :], 1.0)
            last.then_inc(s_ones, 1)

            pool.drain()
            pool.wait_ge(s_k2f, 4)
            flat = k2parts.rearrange("p a c b m -> p a (c b m)")
            for a in range(TERMS):
                last = nc.gpsimd.tensor_copy(flat[:, a, :], k2f)
                if a < TERMS - 1:
                    pool.drain()
                    nc.gpsimd.tensor_tensor(k2f, k2f, flat[:, a, :], ALU.subtract)
                    pool.drain()
            last.then_inc(s_k2t, 1)

            def rotate(r):
                wait(pool, p_terms, r.count(1))
                for tt in range(TT):
                    pool.wait_ge(p_n, r.count(TT, tt + 1))
                    src = normed[:, tt, :].rearrange("p (q d h) -> p q d h", q=2, h=H)
                    dst = rotated[:, tt, :].rearrange("p (q d h) -> p q d h", q=2, h=H)
                    for lo, hi in ((0, HD // 2), (HD // 2, 0)):
                        turn = tables[:, 1, tt, :, lo:lo + HD // 2].unsqueeze(3).broadcast_to([P, 2, HD // 2, H])
                        nc.gpsimd.tensor_tensor(dst[:, :, lo:lo + HD // 2, :], src[:, :, hi:hi + HD // 2, :],
                                                turn, ALU.mult)
                    pool.drain()
                    shift = tables[:, 2, tt, :, :].unsqueeze(3).broadcast_to([P, 2, HD, H])
                    nc.gpsimd.tensor_tensor(dst, dst, shift, ALU.add).then_inc(p_rot, 1)
            pool.wait_ge(s_tab, 2)
            rounds(pool, rotate)

            def spread_values(r):
                pool.wait_ge(p_vsb, r.count(1, 1))
                wait(pool, A["av"], r.count(GROUPS, -GROUPS))
                src = values[:, bass.ds(r.count(TT), TT), :].rearrange("p t (h two d) -> p t h two d", two=2, d=HD)
                dst = vpad[r.side].rearrange("p t (h two) d -> p t h two d", two=2)
                for half in range(2):
                    last = nc.gpsimd.tensor_copy(dst[:, :, :, half, half * HD:(half + 1) * HD],
                                                 src[:, :, :, half, :])
                last.then_inc(A["vpad"], 1)

            def self_round(r):
                if r.at(0) and r.at(1):
                    spread_values(r.at(1))
                if r.at(0):
                    pool.wait_ge(a_res[r.side], r.turns(16, 16))
                    nc.gpsimd.tensor_tensor(resid[r.side][:], resid[r.side][:],
                                            bias_p[:, :].unsqueeze(1).broadcast_to([P, TT, D]),
                                            ALU.add).then_inc(a_resb, 1)
                if r.at(-1):
                    pool.wait_ge(a_var, r.at(-1).count(1, 1))
                    rsqrt_on_pool(pool).then_inc(a_rstd, 1)
            pool.wait_ge(loaded2, 16 * len(later))
            for i in range(2):
                pool.wait_ge(s_v2st[i], 16 * NB // 2)
            spread_values(Round(0))
            rounds(pool, self_round, after=1)

            pool.wait_ge(loaded2, 16 * len(later))

            def send(r):
                pool.wait_ge(c_pos, r.count(1, 1))
                pool.wait_ge(c_xn, r.count(1, 1))
                nc.gpsimd.tensor_tensor(rows3[r.side][:, :, D + 1:], pick[0][:], pick[1][:],
                                        ALU.add).then_inc(c_gates, 1)
                pool.drain()
                for tt in range(TT):
                    for i in range(2):
                        at = tt * 2 + i
                        nc.gpsimd.indirect_dma_start(
                            out=routed, in_=rows3[r.side][:, tt, :], in_offset=None,
                            out_offset=bass.IndirectOffsetOnAxis(ap=pos[r.side][:, at:at + 1], axis=0),
                        ).then_inc(c_scatter[r.side], 16)

            def cross_round(r):
                if r.at(0):
                    pool.wait_ge(c_res[r.side], r.turns(16, 16))
                    nc.gpsimd.tensor_tensor(resid[r.side][:], resid[r.side][:],
                                            bias_2[:, :].unsqueeze(1).broadcast_to([P, TT, D]),
                                            ALU.add).then_inc(c_resb, 1)
                if r.at(-1):
                    pool.wait_ge(c_var, r.at(-1).count(1, 1))
                    rsqrt_on_pool(pool).then_inc(c_rstd, 1)
                if r.at(-2):
                    send(r.at(-2))
            rounds(pool, cross_round, after=2)

            for i in range(2):
                pool.wait_ge(c_out[i], 16 * NB // 2)

            def add_rows(r):
                wait(pool, m_added, r.count(16))
                pool.wait_ge(m_res, r.count(1, 1))
                nc.gpsimd.tensor_tensor(tokens[:], tokens_of[:, bass.ds(r.count(1), 1)],
                                        onesrow[:, 0, HD:HD + 1].bitcast(I32), ALU.add)
                pool.drain()
                nc.gpsimd.indirect_dma_start(
                    out=out, in_=result[r.side], in_offset=None,
                    out_offset=bass.IndirectOffsetOnAxis(ap=tokens[:], axis=0),
                    bounds_check=TOKENS - 1, oob_is_err=False, compute_op=ALU.add).then_inc(m_added, 16)
            blocks(pool, add_rows)
            pool.wait_ge(m_added, 16 * BLOCKS)

        @block.scalar
        def _(act):
            for i in range(4):
                act.wait_ge(s_k2ps, i + 1)
                nc.scalar.copy(k2f[:, i * (NB * M // 2):(i + 1) * (NB * M // 2)],
                               bank[2 + i % 2][:, 0:NB * M // 2]).then_inc(s_k2f, 1)
            def evacuate_xT(r):
                act.wait_ge(p_xTps, r.count(1, 1))
                wait(act, p_v, r.count(1, -1))
                nc.scalar.copy(xnT[r.side], bank[6][:, :].rearrange("p (k s) -> p k s", k=KC)).then_inc(p_xT, 1)

            def squares(r):
                wait(act, p_sum, r.count(1))
                for tt in range(TT):
                    act.wait_ge(p_qk, r.count(TT, tt + 1))
                    nc.scalar.activation(square[:, tt, :], bank[QK_BANKS[r.side][tt]][:, :], ACT.Square
                                         ).then_inc(p_sq, 1)
                act.wait_ge(p_v, r.count(1, 1))
                nc.scalar.copy(values[:, bass.ds(r.count(TT), TT), :],
                               bank[4][:, :].rearrange("p (t c) -> p t c", t=TT)).then_inc(p_vsb, 1)

            def row_roots(i):
                act.wait_ge(p_rows, i + 1)
                tiles = ROW_GROUPS[i]
                nc.scalar.activation(row_rstd[:, tiles], row_rstd[:, tiles], ACT.Sqrt).then_inc(p_root, 1)

            row_roots(0)
            evacuate_xT(Round(0))
            row_roots(1)
            squares(Round(0))
            evacuate_xT(Round(1))
            act.wait_ge(s_zero, 1)
            for b in range(NB):
                act.wait_ge(s_v2ps, b + 1)
                if b >= len(v2_stage):
                    act.wait_ge(s_v2st[b % 2], 16 * (b // 2))
                src = bank[2 + b % 2][0:M, 0:D].rearrange("p (h two d) -> p h two d", two=2, d=HD)
                dst = v2_stage[b % len(v2_stage)][0:M].rearrange("p (h two) d -> p h two d", two=2)
                for half in range(2):
                    last = nc.scalar.copy(dst[:, :, half, half * HD:(half + 1) * HD], src[:, :, half, :])
                last.then_inc(s_v2, 1)


            def project(r):
                if r.at(0):
                    act.wait_ge(p_sum, r.count(1, 1))
                    nc.scalar.activation(spread, spread, ACT.Sqrt).then_inc(p_root, 1)
                if r.at(0) and r.at(1):
                    squares(r.at(1))
                if r.at(0) and r.at(2):
                    evacuate_xT(r.at(2))
                if r.at(-1):
                    r = r.at(-1)
                    wait(act, p_store[r.side], r.turns(STORES))
                    for i in range(2 * TT):
                        tt, qk = i // 2, i % 2
                        act.wait_ge(p_qTps, r.count(2 * TT, i + 1))
                        nc.scalar.copy(
                            qkT[r.side][:, qk, :, :, tt * P:(tt + 1) * P],
                            bank16[2 + i % 2][:, 0:TERMS * KC * P].rearrange("p (a c s) -> p a c s", a=TERMS, s=P)
                        ).then_inc(p_qT, 1)
            rounds(act, project)
            act_max_rows(act, A, Round(0))
            project(Round(NB))

            def late(r, g):
                if g == 0 and r.at(-2):
                    r = r.at(-2)
                    act.wait_ge(a_q2ps, r.count(1, 1))
                    wait(act, a_q2t, r.count(1))
                    for c in range(KC):
                        last = nc.scalar.activation(q2f[:, c, :], bank[6][:, c * S:(c + 1) * S], ACT.Identity,
                                                    bias=bias_q[:, c:c + 1], scale=HD ** -0.5)
                    last.then_inc(a_q2f, 1)
                if g == 3 and r.at(-1):
                    r = r.at(-1)
                    act.wait_ge(a_xTps, r.count(1, 1))
                    wait(act, a_q2ps, r.count(1))
                    nc.scalar.copy(xn2T[:], bank[7][:, :].rearrange("p (k s) -> p k s", k=KC)).then_inc(a_xT, 1)

            rounds(act, lambda r: act_round(act, A, r, SELF_SCORED, late, following=C))
            self_late = late

            def late(r, g):
                if r.opening:
                    self_late(Round(NB + r.own), g)
                if r.first and g == 0:
                    act.wait_ge(A["av"], GROUPS * NB)
                if g == 0 and r.at(-2):
                    r = r.at(-2)
                    act.wait_ge(c_xTps, r.count(1, 1))
                    wait(act, c_logit, r.count(1))
                    nc.scalar.copy(xn2T[:], bank[7][:, :].rearrange("p (k s) -> p k s", k=KC)).then_inc(c_xT, 1)
                if g == 1 and r.at(-1):
                    r = r.at(-1)
                    if r.first:
                        act.wait_ge(a_q2t, NB)
                    act.wait_ge(c_h, r.count(1, 1))
                    wait(act, c_y, r.count(1))
                    for c in range(HID // P):
                        last = nc.scalar.activation(hidT[:, c, :], bank[6 + c // 2][:, (c % 2) * S:(c % 2 + 1) * S],
                                                    ACT.Relu, bias=bias_1[:, c:c + 1])
                    last.then_inc(c_hT, 1)
                if g == 2 and r.at(-2):
                    act.wait_ge(c_gap, r.at(-2).count(1, 1))
                    nc.scalar.activation(share[1][:], gap[:], ACT.Exp).then_inc(c_ed, 1)

            act.wait_ge(loaded2, 16 * len(later))
            act.wait_ge(A["av"], GROUPS * NB - 1)
            rounds(act, lambda r: act_round(act, C, r, CROSS_SCORED, late), after=2)

            pad_regions(act, range(E // 2, E), m_pad[1])

            def rows_in(r):
                act.wait_ge(m_xTps, r.count(1, 1))
                wait(act, m_h, r.count(2, -2))
                nc.scalar.copy(xsT[r.side], bank[0][:, 0:D].rearrange("p (k c) -> p k c", k=KC)).then_inc(m_xT, 1)

            def silu(r):
                act.wait_ge(m_h, r.count(2, 1))
                wait(act, m_hid, r.count(1, -1))
                nc.scalar.activation(act1[r.side], bank[2 + 2 * r.side][:, :], ACT.Silu).then_inc(m_silu, 1)

            def hidden(r):
                act.wait_ge(m_hTps, r.count(1, 1))
                wait(act, m_y, r.count(1, -1))
                nc.scalar.copy(hidT2[r.side], bank[1][:, :].rearrange("p (k c) -> p k c", k=HID // P)
                               ).then_inc(m_hT, 1)

            rows_in(Round(0))
            rows_in(Round(1))
            silu(Round(0))

            def expert_block(r):
                if not r.final:
                    silu(r.next())
                hidden(r)
                if not r.last_two:
                    rows_in(r.next().next())
            blocks(act, expert_block, last=True)

        @block.vector
        def _(dve):
            def row_variance(tiles):
                for first in range(tiles.start, tiles.stop, 4 * TT):
                    group = range(first, min(first + 4 * TT, tiles.stop))
                    for i, tile in enumerate(group):
                        nc.vector.bn_stats(row_moments[:, i, :], x_all[:, tile, :])
                    dve.drain()
                    for i, tile in enumerate(group):
                        nc.vector.bn_aggr(row_stats[:, tile, :], row_moments[:, i, :])
                    dve.drain()
                return nc.vector.tensor_scalar(row_rstd[:, tiles], row_stats[:, tiles, 1], 1e-5, None, ALU.add)

            def norm_rows(r):
                rows = x_all[:, bass.ds(r.count(TT), TT), :]
                wait(dve, p_xTps, r.count(1, -1))
                for tt in range(TT):
                    last = nc.vector.tensor_scalar(xn[r.side][:, tt, :], rows[:, tt, :],
                                                   row_stats[:, bass.ds(r.count(TT, tt), 1), 0],
                                                   row_rstd[:, bass.ds(r.count(TT, tt), 1)], ALU.subtract, ALU.mult)
                last.then_inc(p_xn, 1)

            dve.wait_ge(x_first, 16)
            row_variance(ROW_GROUPS[0]).then_inc(p_rows, 1)
            dve.wait_ge(loaded, 16 * len(weights))
            for k in range(KC):
                nc.vector.tensor_reduce(wmean[:, k, :].rearrange("p (q h) -> p q h", q=2),
                                        wqkv[:, k, 0:2 * D].rearrange("p (q d h) -> p q h d", q=2, h=H),
                                        axis=X, op=ALU.add)
            dve.drain()
            nc.vector.tensor_scalar(wmean, wmean, 1.0 / HD, None, ALU.mult)
            dve.drain()
            for k in range(KC):
                w = wqkv[:, k, 0:2 * D].rearrange("p (q d h) -> p q d h", q=2, h=H)
                mean = wmean[:, k, :].rearrange("p (q h) -> p q h", q=2).unsqueeze(2).broadcast_to([P, 2, HD, H])
                last = nc.vector.tensor_tensor(w, w, mean, ALU.subtract)
            last.then_inc(s_tab, 1)
            dve.drain()
            for tt in range(TT):
                cos = angles[:, 0, tt, :].unsqueeze(1).broadcast_to([P, 2, HD])
                sin = angles[:, 1, tt, :].unsqueeze(1).broadcast_to([P, 2, HD])
                nc.vector.tensor_tensor(tables[:, 0, tt, :, :], affine[:, 0, :, :], cos, ALU.mult)
                nc.vector.tensor_tensor(tables[:, 1, tt, :, :], affine[:, 1, :, :], sin, ALU.mult)
                nc.vector.tensor_tensor(tables[:, 2, tt, :, :], affine[:, 2, :, :], cos, ALU.mult)
                nc.vector.tensor_tensor(wmean[:, tt, :].rearrange("p (q d) -> p q d", q=2), affine[:, 3, :, :],
                                        sin, ALU.mult)
            dve.drain()
            for tt in range(TT):
                nc.vector.tensor_tensor(tables[:, 2, tt, :, :], tables[:, 2, tt, :, :],
                                        wmean[:, tt, :].rearrange("p (q d) -> p q d", q=2), ALU.add)
            dve.drain()
            for a in range(3):
                last = nc.vector.tensor_scalar(tables[:, a, :, 0, :], tables[:, a, :, 0, :], HD ** -0.5, None,
                                               ALU.mult)
            last.then_inc(s_tab, 1)

            dve.wait_ge(p_root, 1)
            nc.vector.reciprocal(row_rstd[:, ROW_GROUPS[0]], row_rstd[:, ROW_GROUPS[0]])
            dve.drain()
            norm_rows(Round(0))
            norm_rows(Round(1))
            dve.wait_ge(x_rest, 16)
            row_variance(ROW_GROUPS[1]).then_inc(p_rows, 1)
            dve.wait_ge(p_root, 2)
            nc.vector.reciprocal(row_rstd[:, ROW_GROUPS[1]], row_rstd[:, ROW_GROUPS[1]])
            dve.drain()

            def project(r):
                here, before = r.at(0), r.at(-1)
                if here:
                    for tt in range(TT):
                        dve.wait_ge(p_sq, r.count(TT, tt + 1))
                        nc.vector.tensor_reduce(spread[:, tt * 2 * H:(tt + 1) * 2 * H].rearrange("p (q h) -> p q h", q=2),
                                                square[:, tt, :].rearrange("p (q d h) -> p q h d", q=2, h=H),
                                                axis=X, op=ALU.add)
                    dve.drain()
                    nc.vector.tensor_scalar(spread, spread, 1.0 / HD, 1e-6, ALU.mult, ALU.add).then_inc(p_sum, 1)
                if here and r.at(2):
                    norm_rows(r.at(2))
                if before:
                    parts = terms[before.side]
                    dve.drain()
                    dve.wait_ge(p_rot, before.count(TT, TT))
                    nc.vector.tensor_tensor(direct, direct, rotated, ALU.add)
                    dve.drain()
                    wait(dve, p_qTps, before.count(2 * TT, -2 * TT))
                    nc.vector.tensor_copy(parts[:, :, 0, :], direct)
                if here:
                    dve.wait_ge(p_root, r.count(1, 3))
                    nc.vector.reciprocal(spread, spread)
                if before:
                    dve.drain()
                    nc.vector.tensor_tensor(direct, direct, parts[:, :, 0, :], ALU.subtract)
                    dve.drain()
                    nc.vector.tensor_copy(parts[:, :, 1, :], direct)
                    dve.drain()
                    nc.vector.tensor_tensor(parts[:, :, 2, :], direct, parts[:, :, 1, :], ALU.subtract
                                            ).then_inc(p_terms, 1)
                if here:
                    dve.drain()
                    for tt in range(TT):
                        inverse = spread[:, tt * 2 * H:(tt + 1) * 2 * H].rearrange("p (q h) -> p q h", q=2)
                        nc.vector.tensor_tensor(normed[:, tt, :].rearrange("p (q d h) -> p q d h", q=2, h=H),
                                                bank[QK_BANKS[r.side][tt]][:, :].rearrange("p (q d h) -> p q d h",
                                                                                           q=2, h=H),
                                                inverse.unsqueeze(2).broadcast_to([P, 2, HD, H]), ALU.mult
                                                ).then_inc(p_n, 1)
                    dve.drain()
                    for tt in range(TT):
                        nc.vector.tensor_tensor(
                            direct[:, tt, :].rearrange("p (q d h) -> p q d h", q=2, h=H),
                            normed[:, tt, :].rearrange("p (q d h) -> p q d h", q=2, h=H),
                            tables[:, 0, tt, :, :].unsqueeze(3).broadcast_to([P, 2, HD, H]), ALU.mult)
            rounds(dve, project)
            dve.wait_ge(s_ones, 1)
            for slot in range(H):
                dve_max(dve, A, Round(0), slot)
            dve_split_max(dve, A, Round(0))
            project(Round(NB))

            def split_queries(r):
                dve.wait_ge(a_q2f, r.count(1, 1))
                wait(dve, a_q2st[r.side], r.turns(16 * len(Q_STORES)))
                parts = q2T[r.side]
                nc.vector.tensor_copy(parts[:, 0, :, :], q2f)
                dve.drain()
                nc.vector.tensor_tensor(q2rest, q2f, parts[:, 0, :, :], ALU.subtract)
                dve.drain()
                nc.vector.tensor_copy(parts[:, 1, :, :], q2rest)
                dve.drain()
                nc.vector.tensor_tensor(parts[:, 2, :, :], q2rest, parts[:, 1, :, :],
                                        ALU.subtract).then_inc(a_q2t, 1)

            dve.wait_ge(loaded2, 16 * len(later))
            nc.vector.tensor_scalar(bias_q[:], bias_q[:], HD ** -0.5, None, ALU.mult)

            def late(r, g):
                if g == 1 and r.at(-1):
                    r = r.at(-1)
                    dve.wait_ge(a_proj, r.count(1, 1))
                    dve.wait_ge(a_resb, r.count(1, 1))
                    wait(dve, a_x1st[r.side], r.turns(16))
                    nc.vector.tensor_tensor(x_new[r.side][:], bank[6][:, :].rearrange("p (t c) -> p t c", t=TT),
                                            resid[r.side][:], ALU.add).then_inc(a_x1, 1)
                    dve.drain()
                    moments_of(dve, x_new[r.side], 1e-5).then_inc(a_var, 1)
                elif g == 2:
                    if r.at(-1):
                        dve.wait_ge(a_rstd, r.at(-1).count(1, 1))
                        wait(dve, a_xTps, r.at(-1).count(1))
                        norm_into(xn2, x_new[r.at(-1).side]).then_inc(a_xn, 1)
                    if r.at(-2):
                        split_queries(r.at(-2))
            rounds(dve, lambda r: dve_round(dve, A, r, SELF_SCORED, a_proj, late, following=C))
            self_late = late

            def choose(r):
                wait(dve, c_gates, r.count(1))
                dve.wait_ge(c_logit, r.count(1, 1))
                nc.vector.tensor_copy(logits[:], bank[6][:, 0:TT * E].rearrange("p (t e) -> p t e", t=TT)
                                      ).then_inc(c_lg, 1)
                for i in range(2):
                    dve.drain()
                    nc.vector.tensor_reduce(best[i][:], logits[:], axis=X, op=ALU.max)
                    dve.drain()
                    nc.vector.tensor_tensor(key[:], logits[:], best[i][:, :].unsqueeze(2).broadcast_to([P, TT, E]),
                                            ALU.is_ge)
                    dve.drain()
                    nc.vector.tensor_tensor(key[:], key[:], first_of[:, :].unsqueeze(1).broadcast_to([P, TT, E]),
                                            ALU.mult)
                    dve.drain()
                    nc.vector.tensor_reduce(top[:], key[:], axis=X, op=ALU.max)
                    dve.drain()
                    nc.vector.tensor_tensor(pick[i][:], key[:], top[:, :].unsqueeze(2).broadcast_to([P, TT, E]),
                                            ALU.is_equal)
                    dve.drain()
                    if i == 0:
                        nc.vector.scalar_tensor_tensor(logits[:], pick[0][:], LOW, logits[:], ALU.mult, ALU.add)
                nc.vector.tensor_tensor(gap[:], best[1][:], best[0][:], ALU.subtract).then_inc(c_gap, 1)
                nc.vector.tensor_tensor(chosen[:], pick[0][:], pick[1][:], ALU.add).then_inc(c_mask, 1)

            def place(r):
                dve.wait_ge(c_ed, r.count(1, 1))
                nc.vector.tensor_scalar(share[0][:], share[1][:], 1.0, None, ALU.add)
                dve.drain()
                nc.vector.reciprocal(share[0][:], share[0][:])
                dve.drain()
                nc.vector.tensor_tensor(share[1][:], share[1][:], share[0][:], ALU.mult)
                dve.wait_ge(c_rank, r.count(1, 1))
                counted = bank[7][:, 0:(TT + 1) * E].rearrange("p (t e) -> p t e", e=E)
                nc.vector.tensor_tensor(ranks[:], counted[:, 0:TT, :],
                                        filled[:, :].unsqueeze(1).broadcast_to([P, TT, E]), ALU.add)
                dve.drain()
                nc.vector.tensor_tensor(filled[:], filled[:], counted[:, TT, :], ALU.add).then_inc(c_rk, 1)
                rows = rows3[r.side]
                nc.vector.tensor_copy(rows[:, :, D:D + 1].bitcast(I32),
                                      token_ids[:, bass.ds(r.count(TT), TT)].unsqueeze(2))
                for i in range(2):
                    nc.vector.tensor_tensor(taken[i][:], pick[i][:], ranks[:], ALU.mult)
                dve.drain()
                for i in range(2):
                    nc.vector.tensor_reduce(posf[:, :, i], taken[i][:], axis=X, op=ALU.add)
                    nc.vector.tensor_tensor(pick[i][:], pick[i][:],
                                            share[i][:, :].unsqueeze(2).broadcast_to([P, TT, E]), ALU.mult)
                dve.drain()
                nc.vector.tensor_copy(pos[r.side][:, :].rearrange("p (t i) -> p t i", t=TT), posf[:]
                                      ).then_inc(c_pos, 1)

            dve.wait_ge(loaded2, 16 * len(later))
            nc.vector.tensor_copy(filled[:], region_at[:])
            def late(r, g):
                if r.first:
                    self_late(Round(NB), g)
                if r.opening and r.own == 1 and g == 1:
                    split_queries(Round(NB - 1))
                if r.first and g == 2:
                    dve.wait_ge(a_proj, NB)
                if g == 0 and r.at(-2):
                    r = r.at(-2)
                    dve.wait_ge(c_rstd, r.count(1, 1))
                    wait(dve, c_scatter[r.side], r.turns(16 * 2 * TT))
                    norm_into(rows3[r.side], x_new[r.side]).then_inc(c_xn, 1)
                if g == 1 and r.at(-2):
                    choose(r.at(-2))
                if g == 3:
                    if r.at(-1):
                        last = r.at(-1)
                        if last.opening:
                            dve.wait_ge(a_x1st[last.side], 16 * NB // 2)
                        dve.wait_ge(c_y, last.count(1, 1))
                        dve.wait_ge(c_resb, last.count(1, 1))
                        wait(dve, c_out[last.side], last.turns(16))
                        nc.vector.tensor_tensor(x_new[last.side][:],
                                                bank[6][:, :].rearrange("p (t c) -> p t c", t=TT),
                                                resid[last.side][:], ALU.add).then_inc(c_x2, 1)
                        dve.drain()
                        moments_of(dve, x_new[last.side], 1e-5).then_inc(c_var, 1)
                    if r.at(-2):
                        place(r.at(-2))
            rounds(dve, lambda r: dve_round(dve, C, r, CROSS_SCORED, c_h, late, leading=A), after=2)

            dve.drain()
            nc.vector.tensor_copy(filled_i[:], filled[:]).then_inc(m_filled, 1)
            nc.vector.tensor_tensor(step_f[:], filled[:], region_at[:], ALU.subtract)
            dve.drain()
            nc.vector.tensor_scalar(count_i[:], step_f[:], float(P - 1), None, ALU.add)
            dve.drain()
            nc.vector.tensor_scalar(count_i[:], count_i[:], 7, None, ALU.arith_shift_right)
            dve.drain()
            nc.vector.tensor_copy(ends_f[:], count_i[:])
            for e in range(1, E):
                dve.drain()
                nc.vector.tensor_tensor(ends_f[:, e:e + 1], ends_f[:, e:e + 1], ends_f[:, e - 1:e], ALU.add)
            dve.drain()
            nc.vector.memset(past[:, :, 0:1], 1.0)
            nc.vector.tensor_tensor(past[:, :, 1:], block_at[:, :].unsqueeze(2).broadcast_to([P, BLOCKS, E]),
                                    ends_f[:, :].unsqueeze(1).broadcast_to([P, BLOCKS, E]), ALU.is_ge)
            nc.vector.tensor_copy(step_f[:], region_at[:])
            dve.drain()
            nc.vector.scalar_tensor_tensor(step_f[:, 1:], ends_f[:, 0:E - 1], -float(P), step_f[:, 1:],
                                           ALU.mult, ALU.add)
            nc.vector.tensor_tensor(of_block, past[:, :, 0:E], past[:, :, 1:], ALU.subtract)
            dve.drain()
            nc.vector.tensor_tensor(scaled, of_block, step_f[:, :].unsqueeze(1).broadcast_to([P, BLOCKS, E]),
                                    ALU.mult)
            nc.vector.tensor_reduce(block_f[:, 1, :], past[:, :, 1:], axis=X, op=ALU.add)
            dve.drain()
            nc.vector.tensor_reduce(block_f[:, 0, :], scaled, axis=X, op=ALU.add)
            nc.vector.tensor_scalar(block_f[:, 1, :], block_f[:, 1, :], float(E - 1), None, ALU.min)
            dve.drain()
            nc.vector.scalar_tensor_tensor(block_f[:, 0, :], block_at[:], float(P), block_f[:, 0, :],
                                           ALU.mult, ALU.add)
            dve.drain()
            nc.vector.tensor_scalar(scaled[:, :, 0], block_f[:, 0, :], -1.0, float(SPARE), ALU.mult, ALU.add)
            dve.drain()
            nc.vector.tensor_tensor(scaled[:, :, 0], scaled[:, :, 0], past[:, :, E], ALU.mult)
            dve.drain()
            nc.vector.tensor_tensor(block_f[:, 0, :], block_f[:, 0, :], scaled[:, :, 0], ALU.add)
            dve.drain()
            nc.vector.tensor_copy(block_i, block_f[:]).then_inc(m_table, 1)

            def read_columns(r):
                dve.wait_ge(m_xs[r.side], r.turns(16, 16))
                nc.vector.tensor_tensor(gates[r.side], xs[r.side][:, D + 1:],
                                        of_block[:, bass.ds(r.count(1), 1), :].rearrange("p o e -> p (o e)"),
                                        ALU.mult)
                dve.drain()
                nc.vector.tensor_copy(tokens_of[:, bass.ds(r.count(1), 1)], xs[r.side][:, D:D + 1].bitcast(I32))
                nc.vector.tensor_reduce(gate[r.side], gates[r.side], axis=X, op=ALU.add).then_inc(m_gate, 1)

            def multiply(r):
                dve.wait_ge(m_silu, r.count(1, 1))
                dve.wait_ge(m_h, r.count(2, 2))
                wait(dve, m_hTps, r.count(1, -1))
                nc.vector.scalar_tensor_tensor(hid[r.side], act1[r.side], gate[r.side], bank[3 + 2 * r.side][:, :],
                                               ALU.mult, ALU.mult).then_inc(m_hid, 1)

            def take_result(r):
                dve.wait_ge(m_y, r.count(1, 1))
                wait(dve, m_added, r.count(16, -16))
                nc.vector.tensor_copy(result[r.side], bank[6 + r.side][:, 0:D]).then_inc(m_res, 1)

            read_columns(Round(0))
            read_columns(Round(1))
            dve.drain()
            multiply(Round(0))

            def expert_block(r):
                if not r.final:
                    multiply(r.next())
                if not r.last_two:
                    read_columns(r.next().next())
                if not r.first:
                    take_result(r.previous())
                dve.drain()
            blocks(dve, expert_block, last=True)
            take_result(Round(BLOCKS - 1))

        @block.tensor
        def _(pe):
            pe.wait_ge(loaded_ctx, 16 * len(context))
            for i in range(4):
                c, half = i // 2, i % 2
                if i >= 2:
                    pe.wait_ge(s_k2f, i - 1)
                for k in range(KC):
                    last = nc.tensor.matmul(bank[2 + i % 2][:, 0:NB * M // 2], wk[:, k, c * P:(c + 1) * P],
                                            ctxT[:, k, half * (NB * M // 2):(half + 1) * (NB * M // 2)],
                                            start=(k == 0), stop=(k == KC - 1))
                last.then_inc(s_k2ps, 1)
            def turn_rows(r):
                pe.wait_ge(p_xn, r.count(1, 1))
                wait(pe, p_xT, r.count(1))
                for tt in range(TT):
                    for k in range(KC):
                        last = nc.tensor.transpose(bank[6][:, k * S + tt * P:k * S + (tt + 1) * P],
                                                   xn[r.side][:, tt, k * P:(k + 1) * P], identf[:])
                last.then_inc(p_xTps, 1)

            def multiply(r):
                pe.wait_ge(p_xT, r.count(1, 1))
                wait(pe, p_n, r.count(TT, -TT))
                for tt in range(TT):
                    for k in range(KC):
                        last = nc.tensor.matmul(bank[QK_BANKS[r.side][tt]][:, :], xnT[r.side][:, k, tt * P:(tt + 1) * P],
                                                wqkv[:, k, 0:2 * D], start=(k == 0), stop=(k == KC - 1))
                    last.then_inc(p_qk, 1)
                wait(pe, p_vsb, r.count(1))
                for tt in range(TT):
                    for k in range(KC):
                        last = nc.tensor.matmul(bank[4][:, tt * D:(tt + 1) * D], xnT[r.side][:, k, tt * P:(tt + 1) * P],
                                                wqkv[:, k, 2 * D:3 * D], start=(k == 0), stop=(k == KC - 1))
                last.then_inc(p_v, 1)

            pe.wait_ge(s_tab, 1)
            turn_rows(Round(0))
            multiply(Round(0))
            turn_rows(Round(1))
            pe.wait_ge(s_k2f, 4)
            for b in range(NB):
                if b >= 2:
                    pe.wait_ge(s_v2, b - 1)
                for k in range(KC):
                    last = nc.tensor.matmul(bank[2 + b % 2][0:M, 0:D], ctxT[:, k, b * M:(b + 1) * M],
                                            wv[:, k, :], start=(k == 0), stop=(k == KC - 1))
                last.then_inc(s_v2ps, 1)
            pe.wait_ge(s_v2, NB)

            def project(r):
                if r.at(0) and r.at(1):
                    multiply(r.at(1))
                if r.at(0) and r.at(2):
                    turn_rows(r.at(2))
                if r.at(-1):
                    r = r.at(-1)
                    pe.wait_ge(p_terms, r.count(1, 1))
                    for i in range(2 * TT):
                        tt, qk = i // 2, i % 2
                        wait(pe, p_qT, r.count(2 * TT, i - 1))
                        for a in range(TERMS):
                            for c in range(KC):
                                n = a * KC + c
                                last = nc.tensor.transpose(
                                    bank16[2 + i % 2][:, n * P:(n + 1) * P],
                                    terms[r.side][:, tt, a, qk * D + c * P:qk * D + (c + 1) * P], ident[:])
                        last.then_inc(p_qTps, 1)
            rounds(pe, project)
            pe.wait_ge(p_n, TT * NB)
            pe.wait_ge(s_ones, 1)
            for slot in range(H):
                pe_score(pe, A, Round(0), slot)
            pe_max_rows(pe, A, Round(0))
            project(Round(NB))

            pe.wait_ge(p_qT, 2 * TT * NB)
            pe.wait_ge(p_vsb, NB)
            pe.wait_ge(loaded2, 16 * len(later))

            def early(r, g):
                pass

            def late(r, g, max_rows):
                if max_rows:
                    max_rows()
                if g == 0 and r.at(-2):
                    r = r.at(-2)
                    pe.wait_ge(a_xT, r.count(1, 1))
                    pe.wait_ge(a_x1, r.count(1, 1))
                    for c in range(KC):
                        for k in range(KC):
                            last = nc.tensor.matmul(bank[6][:, c * S:(c + 1) * S], wq[:, k, c * P:(c + 1) * P],
                                                    xn2T[:, k, :], start=(k == 0), stop=(k == KC - 1))
                    last.then_inc(a_q2ps, 1)
                if g == 1 and r.at(-1):
                    r = r.at(-1)
                    pe.wait_ge(A["attn"], r.count(2, 2))
                    wait(pe, a_q2f, r.count(1))
                    for tt in range(TT):
                        for c in range(KC):
                            last = nc.tensor.matmul(bank[6][:, tt * D:(tt + 1) * D], attnT[:, c, tt * P:(tt + 1) * P],
                                                    wp[:, c, :], start=(c == 0), stop=(c == KC - 1))
                    last.then_inc(a_proj, 1)
                if g == 3 and r.at(-1):
                    r = r.at(-1)
                    pe.wait_ge(a_xn, r.count(1, 1))
                    wait(pe, a_xT, r.count(1))
                    for tt in range(TT):
                        for k in range(KC):
                            last = nc.tensor.transpose(bank[7][:, k * S + tt * P:k * S + (tt + 1) * P],
                                                       xn2[:, tt, k * P:(k + 1) * P], identf[:])
                    last.then_inc(a_xTps, 1)

            def values_ready(r):
                pe.wait_ge(A["vpad"], r.count(1, 1))


            rounds(pe, lambda r: pe_round(pe, A, r, SELF_SCORED, values_ready, early, late, following=C))
            self_late = late

            pe.wait_ge(A["exp"], H * NB)

            def early(r, g):
                if g == 1 and r.at(-2):
                    route(r.at(-2))
                if g == 3 and r.at(-2):
                    rank(r.at(-2))

            def late(r, g, max_rows):
                if r.opening:
                    self_late(Round(NB + r.own), g, None)
                if g == 0 and r.at(-2):
                    r = r.at(-2)
                    pe.wait_ge(c_xn, r.count(1, 1))
                    for tt in range(TT):
                        for k in range(KC):
                            last = nc.tensor.transpose(bank[7][:, k * S + tt * P:k * S + (tt + 1) * P],
                                                       rows3[r.side][:, tt, k * P:(k + 1) * P], identf[:])
                    last.then_inc(c_xTps, 1)
                if g == 1 and r.at(-1):
                    r = r.at(-1)
                    if r.first:
                        pe.wait_ge(a_q2f, NB)
                        pe.wait_ge(a_xT, NB)
                    pe.wait_ge(C["attn"], r.count(2, 2))
                    wait(pe, c_lg, r.count(1))
                    wait(pe, c_xT, r.count(1))
                    for c in range(HID // P):
                        for k in range(KC):
                            last = nc.tensor.matmul(bank[6 + c // 2][:, (c % 2) * S:(c % 2 + 1) * S],
                                                    w1[:, k, c * P:(c + 1) * P], attnT[:, k, :],
                                                    start=(k == 0), stop=(k == KC - 1))
                    last.then_inc(c_h, 1)
                if max_rows and not r.at(-1):
                    max_rows()
                if g == 2 and r.at(-1):
                    pe.wait_ge(c_hT, r.at(-1).count(1, 1))
                    for tt in range(TT):
                        if tt == 1 and max_rows:
                            max_rows()
                        for k in range(HID // P):
                            last = nc.tensor.matmul(bank[6][:, tt * D:(tt + 1) * D], hidT[:, k, tt * P:(tt + 1) * P],
                                                    w2[:, k, :], start=(k == 0), stop=(k == HID // P - 1))
                    last.then_inc(c_y, 1)

            def values_ready(r):
                if r.first:
                    pe.wait_ge(A["attn"], 2 * NB)
                pe.wait_ge(c_v2[r.side], r.turns(16, 16))

            def route(r):
                pe.wait_ge(c_xT, r.count(1, 1))
                pe.wait_ge(c_x2, r.count(1, 1))
                for tt in range(TT):
                    for k in range(KC):
                        last = nc.tensor.matmul(bank[6][:, tt * E:(tt + 1) * E], xn2T[:, k, tt * P:(tt + 1) * P],
                                                wg[:, k, :], start=(k == 0), stop=(k == KC - 1))
                last.then_inc(c_logit, 1)

            def rank(r):
                pe.wait_ge(c_mask, r.count(1, 1))
                pe.wait_ge(c_hT, r.count(1, 1 if r.last else 2))
                nc.tensor.matmul(bank[7][:, 0:E], below[:], chosen[:, 0, :], start=True, stop=True)
                nc.tensor.matmul(bank[7][:, E:2 * E], below[:], chosen[:, 1, :], start=True, stop=False)
                nc.tensor.matmul(bank[7][:, E:2 * E], ones[:], chosen[:, 0, :], start=False, stop=True)
                nc.tensor.matmul(bank[7][:, 2 * E:3 * E], ones[:], chosen[:, 0, :], start=True, stop=False)
                nc.tensor.matmul(bank[7][:, 2 * E:3 * E], ones[:], chosen[:, 1, :], start=False,
                                 stop=True).then_inc(c_rank, 1)

            rounds(pe, lambda r: pe_round(pe, C, r, CROSS_SCORED, values_ready, early, late, leading=A), after=2)

            pe.wait_ge(c_moe, 16 * E)
            pe.wait_ge(C["max"], H * NB)
            pe.wait_ge(C["exp"], H * NB)
            pe.wait_ge(C["attn"], 2 * NB)
            pe.wait_ge(c_lg, NB)
            pe.wait_ge(c_rk, NB)
            pe.wait_ge(m_table, 1)

            def rows_in(r):
                pe.wait_ge(m_xs[r.side], r.turns(16, 16))
                wait(pe, m_xT, r.count(1))
                for k in range(KC):
                    last = nc.tensor.transpose(bank[0][:, k * P:(k + 1) * P], xs[r.side][:, k * P:(k + 1) * P],
                                               identf[:])
                last.then_inc(m_xTps, 1)

            def first_layer(r):
                expert = pe.value_load(block_i[0:1, 1, bass.ds(r.count(1), 1)], min_val=0, max_val=E - 1)
                pe.wait_ge(m_xT, r.count(1, 1))
                wait(pe, m_hid, r.count(1, -1))
                for i in range(2):
                    for k in range(KC):
                        at = (i * KC + k) * HID
                        last = nc.tensor.matmul(bank[2 + 2 * r.side + i][:, :], xsT[r.side][:, k, :],
                                                moe[:, bass.ds(expert, 1), at:at + HID].rearrange("p o n -> p (o n)"),
                                                start=(k == 0), stop=(k == KC - 1))
                    last.then_inc(m_h, 1)

            def turn_hidden(r):
                pe.wait_ge(m_hid, r.count(1, 1))
                wait(pe, m_hT, r.count(1))
                for k in range(HID // P):
                    last = nc.tensor.transpose(bank[1][:, k * P:(k + 1) * P], hid[r.side][:, k * P:(k + 1) * P],
                                               identf[:])
                last.then_inc(m_hTps, 1)

            def second_layer(r):
                expert = pe.value_load(block_i[0:1, 1, bass.ds(r.count(1), 1)], min_val=0, max_val=E - 1)
                pe.wait_ge(m_hT, r.count(1, 1))
                wait(pe, m_res, r.count(1, -1))
                for k in range(HID // P):
                    at = 2 * KC * HID + k * D
                    last = nc.tensor.matmul(bank[6 + r.side][:, 0:D], hidT2[r.side][:, k, :],
                                            moe[:, bass.ds(expert, 1), at:at + D].rearrange("p o n -> p (o n)"),
                                            start=(k == 0), stop=(k == HID // P - 1))
                last.then_inc(m_y, 1)

            rows_in(Round(0))
            rows_in(Round(1))
            first_layer(Round(0))

            def expert_block(r):
                if not r.final:
                    first_layer(r.next())
                turn_hidden(r)
                if not r.last_two:
                    rows_in(r.next().next())
                if not r.first:
                    second_layer(r.previous())
            blocks(pe, expert_block, last=True)
            second_layer(Round(BLOCKS - 1))


def layouts(x, ctx, w):
    def rows(a, pieces):
        return np.ascontiguousarray(a.reshape(pieces, P, -1).transpose(1, 0, 2))

    def spread(a):
        return np.ascontiguousarray(np.broadcast_to(a, (P,) + a.shape))

    swap = np.r_[HD // 2:HD, 0:HD // 2]
    freq = 1.0 / np.float32(10000.0) ** (np.arange(HD // 2, dtype=np.float32) / np.float32(HD // 2))
    emb = np.outer(np.arange(S, dtype=np.float32), freq.astype(np.float32)).astype(np.float32)
    emb = np.concatenate([emb, emb], -1)
    sign = np.where(np.arange(HD) < HD // 2, -1.0, 1.0)
    cos = np.cos(emb).astype(np.float32).reshape(TT, P, HD).transpose(1, 0, 2)
    sin = (np.sin(emb) * sign).astype(np.float32).reshape(TT, P, HD).transpose(1, 0, 2)
    by_channel = np.arange(D).reshape(H, HD).T.reshape(-1)
    by_channel3 = np.concatenate([by_channel, D + by_channel, np.arange(2 * D, 3 * D)])
    gamma = np.stack([w["attn_q_gamma"], w["attn_k_gamma"]])
    beta = np.stack([w["attn_q_beta"], w["attn_k_beta"]])
    pad = KC * P - TEXT - 1

    def padded(weight, bias):
        return rows(np.concatenate([weight, bias[None], np.zeros((pad, D), np.float32)]), KC)

    columns = ctx.reshape(NB * M, TEXT).T
    bf16 = mybir.dt.np(BF16)
    token = np.arange(P)
    padding = np.zeros((P, ROW), np.int32)
    padding[:, D] = TOKENS + token
    up = [w["ffn_" + n].transpose(0, 2, 1).reshape(E, KC, P, HID) for n in ("w1", "w3")]
    down = w["ffn_w2"].transpose(0, 2, 1).reshape(E, HID // P, P, D)
    experts = [a.transpose(2, 0, 1, 3).reshape(P, E, -1) for a in (*up, down)]
    return {
        "moe": np.ascontiguousarray(np.concatenate(experts, -1)),
        "w1": rows(w["xattn_W1"], KC),
        "w2": rows(w["xattn_W2"], HID // P),
        "wg": rows(w["ffn_wg"].T, KC),
        "bias_1": np.ascontiguousarray(w["xattn_b1"].reshape(HID // P, P).T),
        "bias_2": spread(w["xattn_b2"]),
        "below": np.triu(np.ones((P, P)), 1).astype(bf16),
        "ones": np.ones((P, P), bf16),
        "token_ids": (np.arange(NB * TT)[None, :] * P + token[:, None]).astype(np.int32),
        "first_of": spread(np.arange(E, 0, -1).astype(np.float32)),
        "region_at": spread((np.arange(E) * REGION).astype(np.float32)),
        "block_at": spread(np.arange(BLOCKS).astype(np.float32)),
        "padding": padding.view(np.float32),
        "x": rows(x.reshape(TOKENS, D), NB * TT),
        "wqkv": rows(w["attn_w_qkv"][by_channel3].T, KC),
        "angles": np.ascontiguousarray(np.stack([cos, sin], 1)),
        "affine": spread(np.stack([gamma, gamma[:, swap], beta, beta[:, swap]])),
        "identf": np.eye(P, dtype=np.float32),
        "ident": np.eye(P).astype(bf16),
        "ctxT": rows(np.concatenate([columns, np.ones((1, NB * M), np.float32),
                                     np.zeros((pad, NB * M), np.float32)]), KC),
        "wk": padded(w["xattn_Wk"][:, by_channel], w["xattn_bk"][by_channel]),
        "wv": padded(w["xattn_Wv"], w["xattn_bv"]),
        "wp": rows(w["attn_w_proj"].T, KC),
        "wq": rows(w["xattn_Wq"][:, by_channel], KC),
        "bias_q": np.ascontiguousarray(w["xattn_bq"][by_channel].reshape(KC, P).T),
        "bias_p": spread(w["attn_b_proj"]),
    }


def kernel(**inputs):
    import concourse.bacc as bacc
    from concourse.bass_utils import run_bass_kernel_spmd

    given = {k: np.asarray(v) for k, v in inputs.items()}
    arrays = layouts(given["x"], given["ctx_768"],
                     {k[3:]: v for k, v in given.items() if k.startswith("L0_")})
    nc = bacc.Bacc("TRN2", target_bir_lowering=False, num_devices=1)
    tiles = {k: nc.dram_tensor("in_" + k, a.shape, mybir.dt.from_np(a.dtype), kind="ExternalInput").ap()
             for k, a in arrays.items()}
    out = nc.dram_tensor("out", (TOKENS, D), F32, kind="ExternalOutput").ap()
    decoder_layer(nc, tiles, out)
    result = run_bass_kernel_spmd(nc, [{"in_" + k: a for k, a in arrays.items()}], core_ids=[0])
    return result.results[0]["out"].reshape(NB, S, D)
```
